# Optimizing a Trainium2 kernel written in Bass

```python
import numpy as np
import jax
import jax.numpy as jnp

def _softmax(x, axis=-1):
    return jax.nn.softmax(x, axis=axis)

def _gelu(x):
    return jax.nn.gelu(x, approximate=True)

def _silu(x):
    return jax.nn.silu(x)

def _sigmoid(x):
    return jax.nn.sigmoid(x)

def _layernorm(x, axis=-1, eps=1e-05):
    m = jnp.mean(x, axis=axis, keepdims=True)
    v = jnp.var(x, axis=axis, keepdims=True)
    return (x - m) / jnp.sqrt(v + eps)

def _scatter_add(tgt, idx, src, axis=0):
    return tgt.at[idx].add(src)

def _segment_sum(src, seg, n):
    return jax.ops.segment_sum(src, seg, n)
kernel_name = 'mk_gnn_preln_d4_gnn_r64_2df694'

def setup_inputs(seed: int=0):
    np.random.seed(seed)
    _w = jnp.asarray

    def _rec_inputs():
        import jax
        import jax.numpy as jnp
        _gk = jax.random.key(seed)
        x = -0.000202 + 1 * jax.random.normal(jax.random.fold_in(_gk, 1), (50000, 128), jnp.float32)
        src = jax.random.randint(jax.random.fold_in(_gk, 2), (12500,), 0, 50000, jnp.int32)
        dst = jnp.minimum((50000 * jax.random.uniform(jax.random.fold_in(_gk, 3), (12500,)) ** 2.0).astype(jnp.int32), 49999)
        _o = jnp.argsort(dst, stable=True)
        src = src[_o]
        dst = dst[_o]
        edge_attr_128 = 5.93493e-05 + 1.00006 * jax.random.normal(jax.random.fold_in(_gk, 12), (12500, 128), jnp.float32)
        return (x, src, dst, edge_attr_128)
    x, src, dst, edge_attr_128 = _rec_inputs()

    def _L0_gnn_setup():
        import jax, jax.numpy as jnp
        import numpy as np
        N_NODES = 50000
        N_EDGES = 25000
        IN_DIM = 128
        HEADS = 4
        OUT_DIM = 32
        LEAKY_SLOPE = 0.2
        BETA = 0.5
        C = 1.2
        key = jax.random.key(seed)
        k1, k2, k3, k4, k5, k6 = jax.random.split(key, 6)
        x = jax.random.normal(k1, (N_NODES, IN_DIM), dtype=jnp.float32)
        edge_index = jax.random.randint(k2, (2, N_EDGES), 0, N_NODES, dtype=jnp.int64)
        glorot = 1.0 / np.sqrt(IN_DIM)
        W = jax.random.uniform(k3, (IN_DIM, HEADS * OUT_DIM), jnp.float32, -glorot, glorot)
        att_src = jax.random.uniform(k4, (HEADS, OUT_DIM), jnp.float32, -glorot, glorot)
        att_dst = jax.random.uniform(k5, (HEADS, OUT_DIM), jnp.float32, -glorot, glorot)
        bias = jnp.zeros((HEADS * OUT_DIM,), jnp.float32)
        return {'x': x, 'edge_index': edge_index, 'W': W, 'att_src': att_src, 'att_dst': att_dst, 'bias': bias}
    _L0_gnn_all = _L0_gnn_setup()
    _L0_gnn_in = {k: v for k, v in _L0_gnn_all.items() if k in ('W', 'att_src', 'att_dst', 'bias')}
    del _L0_gnn_all

    def _L1_gnn_setup():
        import jax, jax.numpy as jnp
        import numpy as np
        N_NODES = 50000
        N_EDGES = 9375
        HIDDEN = 128
        N_GRAPHS = 32
        key = jax.random.key(seed)
        ks = jax.random.split(key, 8)
        x = jax.random.normal(ks[0], (N_NODES, HIDDEN), dtype=jnp.float32)
        edge_index = jax.random.randint(ks[1], (2, N_EDGES), 0, N_NODES, dtype=jnp.int64)
        edge_attr = jax.random.normal(ks[2], (N_EDGES, HIDDEN), dtype=jnp.float32)
        u = jax.random.normal(ks[3], (N_GRAPHS, HIDDEN), dtype=jnp.float32)
        batch = jax.random.randint(ks[4], (N_NODES,), 0, N_GRAPHS, dtype=jnp.int64)
        s1 = 1.0 / np.sqrt(2 * HIDDEN)
        s2 = 1.0 / np.sqrt(HIDDEN)
        W1 = jax.random.uniform(ks[5], (2 * HIDDEN, HIDDEN), jnp.float32, -s1, s1)
        b1 = jnp.zeros((HIDDEN,), jnp.float32)
        W2 = jax.random.uniform(ks[6], (HIDDEN, HIDDEN), jnp.float32, -s2, s2)
        b2 = jnp.zeros((HIDDEN,), jnp.float32)
        return {'x': x, 'edge_index': edge_index, 'edge_attr': edge_attr, 'u': u, 'batch': batch, 'W1': W1, 'b1': b1, 'W2': W2, 'b2': b2}
    _L1_gnn_all = _L1_gnn_setup()
    _L1_gnn_in = {k: v for k, v in _L1_gnn_all.items() if k in ('u', 'W1', 'b1', 'W2', 'b2')}
    del _L1_gnn_all

    def _L2_gnn_setup():
        import jax, jax.numpy as jnp
        import numpy as np
        N_NODES = 100000
        N_EDGES = 25000
        IN_CH = 128
        OUT_CH = 128
        key = jax.random.key(seed)
        k1, k2, k3, k4 = jax.random.split(key, 4)
        x = jax.random.normal(k1, (N_NODES, IN_CH), dtype=jnp.float32)
        edge_index = jax.random.randint(k2, (2, N_EDGES), 0, N_NODES, dtype=jnp.int64)
        bound = 1.0 / np.sqrt(IN_CH)
        W = jax.random.uniform(k3, (OUT_CH, IN_CH), minval=-bound, maxval=bound, dtype=jnp.float32)
        b = jax.random.uniform(k4, (OUT_CH,), minval=-bound, maxval=bound, dtype=jnp.float32)
        return {'x': x, 'edge_index': edge_index, 'W': W, 'b': b}
    _L2_gnn_all = _L2_gnn_setup()
    _L2_gnn_in = {k: v for k, v in _L2_gnn_all.items() if k in ('W', 'b')}
    del _L2_gnn_all

    def _L3_gnn_setup():
        import jax, jax.numpy as jnp
        import numpy as np
        N = 50000
        E = 12500
        IN_DIM = 128
        HID = 64
        HEADS = 4
        OUT_DIM = 128

        def _gat_conv(x, src, dst, W, a_src, a_dst, bias, heads, out_ch):
            n = x.shape[0]
            h = (x @ W).reshape(n, heads, out_ch)
            alpha_s = jnp.einsum('nhc,hc->nh', h, a_src)
            alpha_d = jnp.einsum('nhc,hc->nh', h, a_dst)
            e = jax.nn.leaky_relu(alpha_s[src] + alpha_d[dst], 0.2)
            m = jax.ops.segment_max(e, dst, num_segments=n)
            m = jnp.where(jnp.isfinite(m), m, 0.0)
            ex = jnp.exp(e - m[dst])
            denom = jax.ops.segment_sum(ex, dst, num_segments=n)
            alpha = ex / denom[dst]
            out = jax.ops.segment_sum(alpha[:, :, None] * h[src], dst, num_segments=n)
            return out.reshape(n, heads * out_ch) + bias
        key = jax.random.key(seed)
        ks = jax.random.split(key, 12)
        s = lambda fan: 1.0 / np.sqrt(fan)
        return {'features': jax.random.normal(ks[0], (N, IN_DIM), jnp.float32), 'edge_index': jax.random.randint(ks[1], (2, E), 0, N, jnp.int64), 'W1': jax.random.normal(ks[2], (IN_DIM, HEADS * HID), jnp.float32) * s(IN_DIM), 'att_src1': jax.random.normal(ks[3], (HEADS, HID), jnp.float32) * s(HID), 'att_dst1': jax.random.normal(ks[4], (HEADS, HID), jnp.float32) * s(HID), 'bias1': jnp.zeros((HEADS * HID,), jnp.float32), 'W2': jax.random.normal(ks[5], (HEADS * HID, OUT_DIM), jnp.float32) * s(HEADS * HID), 'att_src2': jax.random.normal(ks[6], (1, OUT_DIM), jnp.float32) * s(OUT_DIM), 'att_dst2': jax.random.normal(ks[7], (1, OUT_DIM), jnp.float32) * s(OUT_DIM), 'bias2': jnp.zeros((OUT_DIM,), jnp.float32)}
    _L3_gnn_all = _L3_gnn_setup()
    _L3_gnn_in = {k: v for k, v in _L3_gnn_all.items() if k in ('W1', 'att_src1', 'att_dst1', 'bias1', 'W2', 'att_src2', 'att_dst2', 'bias2')}
    del _L3_gnn_all
    return {'x': x, 'src': src, 'dst': dst, 'edge_attr_128': edge_attr_128, 'L0_gnn_W': _L0_gnn_in['W'], 'L0_gnn_att_src': _L0_gnn_in['att_src'], 'L0_gnn_att_dst': _L0_gnn_in['att_dst'], 'L0_gnn_bias': _L0_gnn_in['bias'], 'L1_gnn_u': _L1_gnn_in['u'], 'L1_gnn_W1': _L1_gnn_in['W1'], 'L1_gnn_b1': _L1_gnn_in['b1'], 'L1_gnn_W2': _L1_gnn_in['W2'], 'L1_gnn_b2': _L1_gnn_in['b2'], 'L2_gnn_W': _L2_gnn_in['W'], 'L2_gnn_b': _L2_gnn_in['b'], 'L3_gnn_W1': _L3_gnn_in['W1'], 'L3_gnn_att_src1': _L3_gnn_in['att_src1'], 'L3_gnn_att_dst1': _L3_gnn_in['att_dst1'], 'L3_gnn_bias1': _L3_gnn_in['bias1'], 'L3_gnn_W2': _L3_gnn_in['W2'], 'L3_gnn_att_src2': _L3_gnn_in['att_src2'], 'L3_gnn_att_dst2': _L3_gnn_in['att_dst2'], 'L3_gnn_bias2': _L3_gnn_in['bias2']}

def reference(x, src, dst, edge_attr_128, L0_gnn_W, L0_gnn_att_src, L0_gnn_att_dst, L0_gnn_bias, L1_gnn_u, L1_gnn_W1, L1_gnn_b1, L1_gnn_W2, L1_gnn_b2, L2_gnn_W, L2_gnn_b, L3_gnn_W1, L3_gnn_att_src1, L3_gnn_att_dst1, L3_gnn_bias1, L3_gnn_W2, L3_gnn_att_src2, L3_gnn_att_dst2, L3_gnn_bias2):
    import jax
    import jax.numpy as jnp

    def _L0_gnn_ref(x, edge_index, W, att_src, att_dst, bias):
        import jax, jax.numpy as jnp
        import numpy as np
        N_NODES = 50000
        N_EDGES = 25000
        IN_DIM = 128
        HEADS = 4
        OUT_DIM = 32
        LEAKY_SLOPE = 0.2
        BETA = 0.5
        C = 1.2
        N = x.shape[0]
        H, D = att_src.shape
        loop = jnp.arange(N, dtype=edge_index.dtype)
        src = jnp.concatenate([edge_index[0], loop])
        dst = jnp.concatenate([edge_index[1], loop])
        xp = (x @ W).reshape(N, H, D)
        a_src = jnp.einsum('nhd,hd->nh', xp, att_src)
        a_dst = jnp.einsum('nhd,hd->nh', xp, att_dst)
        alpha = jax.nn.leaky_relu(a_src[src] + a_dst[dst], LEAKY_SLOPE)
        amax = jax.ops.segment_max(alpha, dst, num_segments=N)
        e = jnp.exp(alpha - amax[dst])
        denom = jax.ops.segment_sum(e, dst, num_segments=N)
        w = e / (denom[dst] + 1e-16)
        msg = xp[src] * w[:, :, None]
        out = jax.ops.segment_sum(msg, dst, num_segments=N).reshape(N, H * D)
        z = out + bias
        return BETA * z + (C - BETA) * (z * jax.nn.sigmoid(z))

    def _L1_gnn_ref(x, edge_index, edge_attr, u, batch, W1, b1, W2, b2):
        import jax, jax.numpy as jnp
        import numpy as np
        N_NODES = 50000
        N_EDGES = 9375
        HIDDEN = 128
        N_GRAPHS = 32
        col = edge_index[1]
        agg = jax.ops.segment_sum(edge_attr, col, num_segments=x.shape[0])
        combined = jnp.concatenate([x, agg], axis=1)
        h = jax.nn.relu(combined @ W1 + b1)
        return h @ W2 + b2

    def _L2_gnn_ref(x, edge_index, W, b):
        import jax, jax.numpy as jnp
        import numpy as np
        N_NODES = 100000
        N_EDGES = 25000
        IN_CH = 128
        OUT_CH = 128
        n = x.shape[0]
        src, dst = (edge_index[0], edge_index[1])
        agg = jax.ops.segment_sum(x[src], dst, num_segments=n)
        ones_e = jnp.ones((edge_index.shape[1],), dtype=x.dtype)
        neighbor_count = jax.ops.segment_sum(ones_e, dst, num_segments=n)
        neighbor_count = jnp.maximum(neighbor_count, 1.0)[:, None]
        agg = (x + agg) / (1.0 + neighbor_count)
        out = agg @ W.T + b
        return jax.nn.leaky_relu(out, negative_slope=0.2)

    def _L3_gnn_ref(features, edge_index, W1, att_src1, att_dst1, bias1, W2, att_src2, att_dst2, bias2):
        import jax, jax.numpy as jnp
        import numpy as np
        N = 50000
        E = 12500
        IN_DIM = 128
        HID = 64
        HEADS = 4
        OUT_DIM = 128

        def _gat_conv(x, src, dst, W, a_src, a_dst, bias, heads, out_ch):
            n = x.shape[0]
            h = (x @ W).reshape(n, heads, out_ch)
            alpha_s = jnp.einsum('nhc,hc->nh', h, a_src)
            alpha_d = jnp.einsum('nhc,hc->nh', h, a_dst)
            e = jax.nn.leaky_relu(alpha_s[src] + alpha_d[dst], 0.2)
            m = jax.ops.segment_max(e, dst, num_segments=n)
            m = jnp.where(jnp.isfinite(m), m, 0.0)
            ex = jnp.exp(e - m[dst])
            denom = jax.ops.segment_sum(ex, dst, num_segments=n)
            alpha = ex / denom[dst]
            out = jax.ops.segment_sum(alpha[:, :, None] * h[src], dst, num_segments=n)
            return out.reshape(n, heads * out_ch) + bias
        n = features.shape[0]
        loops = jnp.arange(n, dtype=edge_index.dtype)
        src = jnp.concatenate([edge_index[0], loops])
        dst = jnp.concatenate([edge_index[1], loops])
        act = lambda v: jax.nn.leaky_relu(v, 0.2)
        x = _gat_conv(features, src, dst, W1, att_src1, att_dst1, bias1, HEADS, HID)
        x = act(x)
        x = _gat_conv(x, src, dst, W2, att_src2, att_dst2, bias2, 1, OUT_DIM)
        x = act(x)
        return x + features
    edge_index = jnp.stack([src, dst])
    batch0 = jnp.zeros((50000,), jnp.int32)
    h = jnp.maximum(_layernorm(x, axis=-1), 0.0)
    x = x + _L0_gnn_ref(h, edge_index, L0_gnn_W, L0_gnn_att_src, L0_gnn_att_dst, L0_gnn_bias)
    h = jnp.maximum(_layernorm(x, axis=-1), 0.0)
    x = x + _L1_gnn_ref(h, edge_index, edge_attr_128, L1_gnn_u, batch0, L1_gnn_W1, L1_gnn_b1, L1_gnn_W2, L1_gnn_b2)
    h = jnp.maximum(_layernorm(x, axis=-1), 0.0)
    x = x + _L2_gnn_ref(h, edge_index, L2_gnn_W, L2_gnn_b)
    h = jnp.maximum(_layernorm(x, axis=-1), 0.0)
    x = x + _L3_gnn_ref(h, edge_index, L3_gnn_W1, L3_gnn_att_src1, L3_gnn_att_dst1, L3_gnn_bias1, L3_gnn_W2, L3_gnn_att_src2, L3_gnn_att_dst2, L3_gnn_bias2)
    return x

_drawn_inputs = setup_inputs


def setup_inputs(seed=0):
    import zlib

    import numpy as np

    out = dict(_drawn_inputs(seed))
    spreads = {'L0_gnn_bias': (0.0, 0.1),
     'L1_gnn_b1': (0.0, 0.1),
     'L1_gnn_b2': (0.0, 0.1),
     'L3_gnn_bias1': (0.0, 0.281),
     'L3_gnn_bias2': (0.0, 0.1)}
    factors = {'L0_gnn_att_src': 8.0,
     'L0_gnn_att_dst': 57.467,
     'L3_gnn_att_src1': 22.556,
     'L3_gnn_att_dst1': 64.0,
     'L3_gnn_att_src2': 25.527,
     'L3_gnn_att_dst2': 64.0}
    for name, (base, spread) in spreads.items():
        noise = np.random.default_rng([zlib.crc32(name.encode()), seed]).standard_normal(out[name].shape)
        drawn = base * np.exp(spread * noise) if base else spread * noise
        out[name] = jnp.asarray(drawn.astype(out[name].dtype))
    for name, factor in factors.items():
        out[name] = (out[name] * factor).astype(out[name].dtype)
    return out
```

```python
from contextlib import ExitStack

import concourse.bass as bass
from concourse import mybir

F32 = mybir.dt.float32
I32 = mybir.dt.int32
ALU = mybir.AluOpType
ACT = mybir.ActivationFunctionType
AX = mybir.AxisListType.X

P = 128
D = 128
TG = 4
NS = 4
GROUP = P * TG
EPS = 1e-5
SLOPE = 0.2
BIG = 1e30


def past(eng, sem, value):
    if isinstance(value, int) and value <= 0:
        return
    eng.wait_ge(sem, value)


class Chain:

    def __init__(self, eng, sem):
        self.eng, self.sem, self.base, self.n, self.before, self.per_body, self.i = eng, sem, 0, 0, 0, None, None

    def body(self, i):
        if isinstance(i, int) and i == 0:
            self.before = self.base = self.n
        elif isinstance(i, int) and self.i == i - 1:
            self.base = self.base + self.n
        else:
            self.per_body = self.per_body or self.n
            self.base = self.before + i * self.per_body
        self.n, self.i = 0, i if isinstance(i, int) else None

    def add(self, ins):
        ins.then_inc(self.sem, 1)
        self.n += 1
        return self.n

    def upto(self, n):
        self.eng.wait_ge(self.sem, self.base + n)


def alone(eng):
    eng.nop(nofuse=True)


def run_slots(eng, chain, units, order):
    lags = [lag for _, lag in order]
    chain = chain or Chain(eng, None)

    def slot(i, c):
        for stage, lag in order:
            u, r = NS * i + (c - lag), i + (c - lag) // NS
            if not (isinstance(u, int) and not 0 <= u < units):
                stage(u, (c - lag) % NS, r)

    peeled = 1 - (-max(lags) // NS) if max(lags) > 0 else 1
    assert units // NS > peeled and min(lags) >= -(units % NS)
    for n in range(min(lags), NS * peeled):
        before = chain.n
        slot(n // NS, n % NS)
    per_body = NS * (chain.n - before)
    ahead = chain.n
    with eng.Fori(peeled, units // NS) as i:
        chain.base, chain.n = ahead + (i - peeled) * per_body, 0
        for c in range(NS):
            slot(i, c)
        assert chain.n == per_body
    chain.base, chain.n = ahead + (units // NS - peeled) * per_body, 0
    for n in range(units // NS * NS, units + max(lags)):
        slot(n // NS, n % NS)


def layer_stats(chain, x, stats, mv, tiles):
    for j in range(tiles):
        last = chain.add(chain.eng.bn_stats(stats[:, j, :], x[:, j, :]))
    chain.upto(last)
    alone(chain.eng)
    for j in range(tiles):
        last = chain.eng.bn_aggr(mv[:, j, :], stats[:, j, :])
    return last


def layer_rstd(chain, mv, ve, rs, half):
    alone(chain.eng)
    n = chain.add(chain.eng.tensor_scalar(ve, mv[:, :, 1], EPS, None, ALU.add))
    chain.upto(n)
    return chain.eng.tensor_tensor(rs, ve, half, ALU.pow)


def layer_norm(chain, x, mv, rs, h, tiles):
    for j in range(tiles):
        last = chain.eng.tensor_scalar(h[:, j, :], x[:, j, :], mv[:, j, 0:1], rs[:, j:j + 1],
                                       ALU.subtract, ALU.mult)
    return last


class Net:
    pass


def load_weights(nc, ctx, a):
    w = Net()

    def sb(name, shape, dt=F32):
        return ctx.enter_context(nc.sbuf_tensor(name, shape, dt))

    H0 = a["L0_gnn_att_src"].shape[0]
    H3 = a["L3_gnn_att_src1"].shape[0]
    C3 = a["L3_gnn_W1"].shape[1] // P
    w.H0, w.H3, w.C3 = H0, H3, C3
    w.w0 = sb("w0", [P, D + 2 * H0])
    w.w1x = sb("w1x", [P, D])
    w.w1e = sb("w1e", [P, D])
    w.w1b = sb("w1b", [P, D])
    w.w2 = sb("w2", [P, D])
    w.w2raw = sb("w2raw", [P, D])
    w.w3 = sb("w3", [P, C3 * P + 2 * H3])
    w.w4 = sb("w4", [P, C3, D + 2])
    w.b0 = sb("b0", [P, D])
    w.b1 = sb("b1", [P, 1])
    w.b1b = sb("b1b", [P, D])
    w.b2 = sb("b2", [P, D])
    w.b3 = sb("b3", [P, C3])
    w.b3row = sb("b3row", [P, C3 * P])
    w.b4 = sb("b4", [P, D])
    w.ident = sb("ident", [P, P])
    w.half = sb("half", [P, TG])
    with ExitStack() as tmp:
        att = [tmp.enter_context(nc.sbuf_tensor(f"att{k}", [P, n], F32))
               for k, n in enumerate((D, D, C3 * P, C3 * P, D, D))]
        prod = tmp.enter_context(nc.sbuf_tensor("prod", [P, 8, C3 * P], F32))
        w2t = tmp.enter_context(nc.psum_tensor("w2t", [P, D], F32))
        loaded = tmp.enter_context(nc.semaphore("weights_loaded"))
        ident_step = tmp.enter_context(nc.semaphore("ident_step"))
        prod_ready = tmp.enter_context(nc.semaphore("prod_ready"))
        w2_turned = tmp.enter_context(nc.semaphore("w2_turned"))
        block = tmp.enter_context(nc.Block())

        def rows(ap):
            return ap.rearrange("(a n) -> a n", a=1).to_broadcast([P, ap.shape[0]])

        loads = [
            (w.w0[:, 0:D], a["L0_gnn_W"]), (w.w1x[:, :], a["L1_gnn_W1"][0:D, :]),
            (w.w1e[:, :], a["L1_gnn_W1"][D:2 * D, :]), (w.w1b[:, :], a["L1_gnn_W2"]),
            (w.w2raw[:, :], a["L2_gnn_W"]), (w.w3[:, 0:C3 * P], a["L3_gnn_W1"]),
            (w.w4[:, :, 0:D], a["L3_gnn_W2"].rearrange("(c p) n -> p c n", p=P)),
            (w.b0[:, :], rows(a["L0_gnn_bias"])), (w.b1[:, :], a["L1_gnn_b1"].rearrange("(p a) -> p a", a=1)),
            (w.b1b[:, :], rows(a["L1_gnn_b2"])), (w.b2[:, :], rows(a["L2_gnn_b"])),
            (w.b3row[:, :], rows(a["L3_gnn_bias1"])), (w.b4[:, :], rows(a["L3_gnn_bias2"])),
        ] + [(w.b3[:, c:c + 1], a["L3_gnn_bias1"][c * P:(c + 1) * P].rearrange("(p a) -> p a", a=1))
             for c in range(C3)] + [
            (t[:, :], rows(a[n].rearrange("h d -> (h d)"))) for t, n in zip(att, (
                "L0_gnn_att_src", "L0_gnn_att_dst", "L3_gnn_att_src1", "L3_gnn_att_dst1",
                "L3_gnn_att_src2", "L3_gnn_att_dst2"))]

        @block.sync
        def _(sp):
            for dst, src in loads:
                sp.dma_start(dst, src).then_inc(loaded, 16)

        @block.gpsimd
        def _(pool):
            pool.memset(w.half[:, :], -0.5)
            pool.memset(w.ident[:, :], 0.0).then_inc(ident_step, 1)
            pool.wait_ge(ident_step, 1)
            pool.affine_select(out=w.ident[:, :], in_=w.ident[:, :], compare_op=ALU.not_equal, fill=1.0,
                               base=0, pattern=[[-1, P]], channel_multiplier=1).then_inc(ident_step, 1)
        @block.tensor
        def _(pe):
            pe.wait_ge(ident_step, 2)
            pe.wait_ge(loaded, 16 * len(loads))
            pe.transpose(w2t[:, :], w.w2raw[:, :], w.ident[:, :]).then_inc(w2_turned, 1)

        @block.vector
        def _(dve):
            dve.wait_ge(loaded, 16 * len(loads))
            folds = [(w.w0[:, 0:D], att[0][:, :], H0, w.w0[:, D:D + H0]),
                     (w.w0[:, 0:D], att[1][:, :], H0, w.w0[:, D + H0:D + 2 * H0]),
                     (w.w3[:, 0:C3 * P], att[2][:, :], H3, w.w3[:, C3 * P:C3 * P + H3]),
                     (w.w3[:, 0:C3 * P], att[3][:, :], H3, w.w3[:, C3 * P + H3:C3 * P + 2 * H3])]
            for c in range(C3):
                folds.append((w.w4[:, c, 0:D], att[4][:, :], 1, w.w4[:, c, D:D + 1]))
                folds.append((w.w4[:, c, 0:D], att[5][:, :], 1, w.w4[:, c, D + 1:D + 2]))
            for n, (weight, row, heads, out) in enumerate(folds):
                width = weight.shape[1]
                dve.tensor_tensor(prod[:, n, 0:width], weight, row, ALU.mult).then_inc(prod_ready, 1)
            for n, (weight, row, heads, out) in enumerate(folds):
                width = weight.shape[1]
                dve.wait_ge(prod_ready, n + 1)
                dve.tensor_reduce(out, prod[:, n, 0:width].rearrange("p (h d) -> p h d", h=heads), AX, ALU.add)
            dve.wait_ge(w2_turned, 1)
            dve.tensor_copy(w.w2[:, :], w2t[:, :])
    return w


def dense_pass(nc, w, x_dram, tables, out_dram):
    t2_dram, t3_dram, t4_dram = tables
    N = x_dram.shape[0]
    groups = -(-N // GROUP)
    C3 = w.C3
    short = groups * GROUP - N
    assert 0 <= short < GROUP and short % TG == 0
    skip = short // TG

    with ExitStack() as ctx:
        def sb(name, shape, dt=F32):
            return [ctx.enter_context(nc.sbuf_tensor(f"d_{name}{s}", shape, dt)) for s in range(NS)]

        def pb(name, shape):
            return [ctx.enter_context(nc.psum_tensor(f"d_{name}{s}", shape, F32)) for s in range(NS)]

        def sem(name):
            return ctx.enter_context(nc.semaphore("d_" + name))

        def banks(pa):
            return pa[:, :, :].rearrange("p t n -> p (t n)").rearrange("p (b t n) -> p b t n", b=2, t=TG)

        X = sb("x", [P, TG, D])
        X1 = sb("x1", [P, TG, D])
        X1B = sb("x1b", [P, TG, D])
        X2 = sb("x2", [P, TG, D])
        X3 = sb("x3", [P, TG, D])
        XH = sb("xh", [P, TG, D])
        OUT = sb("out", [P, TG, D])
        H = sb("h", [P, TG, D])
        HT = sb("ht", [P, TG, P])
        Z0 = sb("z0", [P, TG, D])
        Y0 = sb("y0", [P, TG, D])
        S0 = sb("s0", [P, TG, D])
        Z1T = sb("z1t", [P, TG, P])
        Z2 = sb("z2", [P, TG, D])
        L2 = sb("l2", [P, TG, D])
        C1Z = sb("c1z", [P, C3, TG * P])
        C1T = sb("c1t", [P, C3, TG, P])
        G = sb("g", [P, TG, D + 2])
        Z4 = sb("z4", [P, TG, D])
        L4 = sb("l4", [P, TG, D])
        ST = [sb(f"st{k}", [P, TG, 6]) for k in range(4)]
        MV = [sb(f"mv{k}", [P, TG, 2]) for k in range(4)]
        VE = [sb(f"ve{k}", [P, TG]) for k in range(4)]
        RS = [sb(f"rs{k}", [P, TG]) for k in range(4)]
        NM = [sb(f"nm{k}", [P, TG]) for k in range(4)]
        PA = pb("pa", [P, TG, 2 * D])
        PT = [banks(pa)[:, 0] for pa in PA]
        PB = [banks(pa)[:, 1] for pa in PA]

        x_loaded = [sem(f"x_loaded{s}") for s in range(NS)]
        x2_stored = [sem(f"x2_stored{s}") for s in range(NS)]
        x3_stored = [sem(f"x3_stored{s}") for s in range(NS)]
        g_stored = [sem(f"g_stored{s}") for s in range(NS)]
        out_stored = [sem(f"out_stored{s}") for s in range(NS)]
        dve_step, pool_step = sem("dve_step"), sem("pool_step")
        stats_ready = [sem(f"stats_ready{k}") for k in range(4)]
        rstd_ready = [sem(f"rstd_ready{k}") for k in range(4)]
        shift_ready = [sem(f"shift_ready{k}") for k in range(4)]
        h_ready = [sem(f"h_ready{k}") for k in range(4)]
        turned = [sem(f"turned{k}") for k in range(4)]
        ht_ready = [sem(f"ht_ready{k}") for k in range(4)]
        mm0_done, y0_ready, z0_ready, s0_ready, x1_ready, x1b_ready = (
            sem(n) for n in ("mm0_done", "y0_ready", "z0_ready", "s0_ready", "x1_ready", "x1b_ready"))
        mm1_done, z1_ready, mm1b_done, x2_ready = (
            sem(n) for n in ("mm1_done", "z1_ready", "mm1b_done", "x2_ready"))
        mm2_done, z2_ready, l2_ready, x3_ready, xh_ready = (
            sem(n) for n in ("mm2_done", "z2_ready", "l2_ready", "x3_ready", "xh_ready"))
        mm3_done, c1z_ready, c1_ready, mm4_done, g_ready, z4_ready, l4_ready, out_ready = (
            sem(n) for n in ("mm3_done", "c1z_ready", "c1_ready", "mm4_done", "g_ready", "z4_ready", "l4_ready", "out_ready"))
        layer_in = [X, X1, X2, X3]
        layer_in_ready = [None, x1_ready, x2_ready, x3_ready]

        block = ctx.enter_context(nc.Block())

        def rows(dram, u):
            start = N - GROUP if last_group(u) else u * GROUP
            return dram[bass.ds(start, GROUP), :].rearrange("(p t) n -> p t n", t=TG)

        def last_group(u):
            return isinstance(u, int) and u == groups - 1

        @block.sync
        def _(sp):
            def load(u, s, r):
                past(sp, x1_ready, u + 1 - NS)
                sp.dma_start(X[s][:, :, :], rows(x_dram, u)).then_inc(x_loaded[s], 16)

            def store(dram, tile, ready, stored):
                def stage(u, s, r):
                    sp.wait_ge(ready, u + 1)
                    lo = skip if last_group(u) else 0
                    sp.dma_start(rows(dram, u)[lo:P], tile[s][lo:P, :, :]).then_inc(stored[s], 16)
                return stage

            run_slots(sp, None, groups, [
                (load, -1), (store(t2_dram, X2, x2_ready, x2_stored), 2), (store(t3_dram, X3, x3_ready, x3_stored), 3),
                (store(t4_dram, G, g_ready, g_stored), 4), (store(out_dram, OUT, out_ready, out_stored), 4)])
            for stored in (x2_stored, x3_stored, g_stored, out_stored):
                for s in range(NS):
                    sp.wait_ge(stored[s], 16 * len(range(s, groups, NS)))

        @block.gpsimd
        def _(pool):
            chain = Chain(pool, pool_step)

            def rstd(k):
                def stage(u, s, r):
                    pool.wait_ge(stats_ready[k], u + 1)
                    layer_rstd(chain, MV[k][s], VE[k][s][:, :], RS[k][s][:, :], w.half[:, :])\
                        .then_inc(rstd_ready[k], 1)
                return stage

            def add_b1(u, s, r):
                pool.wait_ge(x1_ready, u + 1)
                pool.tensor_tensor(X1B[s][:, :, :], X1[s][:, :, :],
                                   w.b1b[:, None, :].to_broadcast([P, TG, D]), ALU.add).then_inc(x1b_ready, 1)

            def x3(u, s, r):
                pool.wait_ge(l2_ready, u + 1)
                past(pool, x3_stored[s], 16 * r)
                pool.tensor_tensor(X3[s][:, :, :], X2[s][:, :, :], L2[s][:, :, :], ALU.add).then_inc(x3_ready, 1)

            def z4(u, s, r):
                pool.wait_ge(g_ready, u + 1)
                pool.tensor_tensor(Z4[s][:, :, :], G[s][:, :, 0:D],
                                   w.b4[:, None, :].to_broadcast([P, TG, D]), ALU.add).then_inc(z4_ready, 1)

            def final(u, s, r):
                pool.wait_ge(l4_ready, u + 1)
                past(pool, out_stored[s], 16 * r)
                pool.wait_ge(xh_ready, u + 1)
                pool.tensor_tensor(OUT[s][:, :, :], XH[s][:, :, :], L4[s][:, :, :], ALU.add).then_inc(out_ready, 1)

            run_slots(pool, chain, groups, [
                (x3, 2), (rstd(0), 0), (rstd(3), 2), (rstd(2), 1), (z4, 3), (add_b1, 0), (rstd(1), 0),
                (final, 3)])

        @block.scalar
        def _(act):
            chain = Chain(act, None)

            def turn(k):
                def stage(u, s, r):
                    act.wait_ge(turned[k], u + 1)
                    act.activation(HT[s][:, :, :], PT[s][:, :, :], ACT.Copy).then_inc(ht_ready[k], 1)
                return stage

            def norm(k):
                def stage(u, s, r):
                    act.wait_ge(shift_ready[k], u + 1)
                    if k == 0:
                        past(act, xh_ready, u + 1 - NS)
                    for j in range(TG):
                        last = act.activation(H[s][:, j, :], layer_in[k][s][:, j, :], ACT.Relu,
                                              bias=NM[k][s][:, j:j + 1], scale=RS[k][s][:, j:j + 1])
                    last.then_inc(h_ready[k], 1)
                return stage

            def s0(u, s, r):
                act.wait_ge(z0_ready, u + 1)
                act.activation(S0[s][:, :, :], Z0[s][:, :, :], ACT.Silu).then_inc(s0_ready, 1)

            def z1(u, s, r):
                act.wait_ge(mm1_done, u + 1)
                act.activation(Z1T[s][:, :, :], PB[s][:, :, :], ACT.Relu, bias=w.b1[:, 0:1]).then_inc(z1_ready, 1)

            def c1(u, s, r):
                act.wait_ge(mm3_done, u + 1)
                pa = PA[s][:, :, :].rearrange("p t n -> p (t n)").rearrange("p (c n) -> p c n", c=C3)
                for c in range(C3):
                    last = act.activation(C1Z[s][:, c, :], pa[:, c, :], ACT.Identity, bias=w.b3[:, c:c + 1])
                last.then_inc(c1z_ready, 1)

            def g(u, s, r):
                act.wait_ge(mm4_done, u + 1)
                past(act, g_stored[s], 16 * r)
                past(act, z4_ready, u + 1 - NS)
                act.activation(G[s][:, :, :], PA[s][:, :, 0:D + 2], ACT.Copy).then_inc(g_ready, 1)

            run_slots(act, chain, groups, [
                (turn(1), 1), (c1, 3), (z1, 1), (norm(0), 0), (turn(0), 0), (norm(3), 2), (g, 3), (s0, 0),
                (norm(2), 1), (turn(3), 2), (turn(2), 1), (norm(1), 0)])

        @block.tensor
        def _(pe):
            chain = Chain(pe, None)

            def turn(k):
                def stage(u, s, r):
                    pe.wait_ge(h_ready[k], u + 1)
                    if k == 0:
                        past(pe, g_ready, u + 1 - NS)
                    for j in range(TG):
                        last = pe.transpose(PT[s][:, j, :], H[s][:, j, :], w.ident[:, :])
                    last.then_inc(turned[k], 1)
                return stage

            def mm(k, weight, acc, done):
                def stage(u, s, r):
                    pe.wait_ge(ht_ready[k], u + 1)
                    for j in range(TG):
                        last = pe.matmul(acc[s][:, j, :], HT[s][:, j, :], weight, start=True, stop=True)
                    last.then_inc(done, 1)
                return stage

            def mm1(u, s, r):
                pe.wait_ge(ht_ready[1], u + 1)
                pe.matmul(PB[s][:, :, :], w.w1x[:, :], HT[s][:, :, :], start=True, stop=True).then_inc(mm1_done, 1)

            def mm1b(u, s, r):
                pe.wait_ge(z1_ready, u + 1)
                for j in range(TG):
                    last = pe.matmul(PT[s][:, j, :], Z1T[s][:, j, :], w.w1b[:, :], start=True, stop=True)
                last.then_inc(mm1b_done, 1)

            def mm3(u, s, r):
                pe.wait_ge(ht_ready[3], u + 1)
                pa = PA[s][:, :, :].rearrange("p t n -> p (t n)").rearrange("p (c n) -> p c n", c=C3)
                for c in range(C3):
                    last = pe.matmul(pa[:, c, :], w.w3[:, c * P:(c + 1) * P],
                                     HT[s][:, :, :].rearrange("p t n -> p (t n)"), start=True, stop=True)
                last.then_inc(mm3_done, 1)

            def mm4(u, s, r):
                pe.wait_ge(c1_ready, u + 1)
                for j in range(TG):
                    for c in range(C3):
                        last = pe.matmul(PA[s][:, j, 0:D + 2], C1T[s][:, c, j, :], w.w4[:, c, :],
                                         start=(c == 0), stop=(c == C3 - 1))
                last.then_inc(mm4_done, 1)

            run_slots(pe, chain, groups, [
                (turn(1), 1), (mm1, 1), (mm1b, 1), (turn(0), 0), (mm4, 3),
                (mm(0, w.w0[:, 0:D], PB, mm0_done), 0), (turn(3), 2), (turn(2), 1),
                (mm(2, w.w2[:, :], PB, mm2_done), 1), (mm3, 2)])

        @block.vector
        def _(dve):
            chain = Chain(dve, dve_step)

            def leaky(out, z):
                return dve.scalar_tensor_tensor(out=out, in0=z, scalar=SLOPE, in1=z, op0=ALU.mult, op1=ALU.max)

            def row(bias):
                return bias[:, None, :].to_broadcast([P, TG, D])

            def stats(k):
                def stage(u, s, r):
                    if k == 0:
                        dve.wait_ge(x_loaded[s], 16 * (r + 1))
                    else:
                        dve.wait_ge(layer_in_ready[k], u + 1)
                    layer_stats(chain, layer_in[k][s], ST[k][s], MV[k][s], TG).then_inc(stats_ready[k], 1)
                return stage

            def shift(k):
                def stage(u, s, r):
                    dve.wait_ge(rstd_ready[k], u + 1)
                    dve.scalar_tensor_tensor(out=NM[k][s][:, :], in0=MV[k][s][:, :, 0], scalar=-1.0,
                                             in1=RS[k][s][:, :], op0=ALU.mult, op1=ALU.mult)\
                        .then_inc(shift_ready[k], 1)
                return stage

            def z0(u, s, r):
                dve.wait_ge(mm0_done, u + 1)
                dve.tensor_tensor(Z0[s][:, :, :], PB[s][:, :, :], row(w.b0), ALU.add).then_inc(z0_ready, 1)

            def y0(u, s, r):
                dve.wait_ge(z0_ready, u + 1)
                dve.scalar_tensor_tensor(out=Y0[s][:, :, :], in0=Z0[s][:, :, :], scalar=0.5, in1=X[s][:, :, :],
                                         op0=ALU.mult, op1=ALU.add).then_inc(y0_ready, 1)

            def x1(u, s, r):
                dve.wait_ge(s0_ready, u + 1)
                past(dve, x1b_ready, u + 1 - NS)
                dve.wait_ge(y0_ready, u + 1)
                dve.scalar_tensor_tensor(out=X1[s][:, :, :], in0=S0[s][:, :, :], scalar=1.2 - 0.5,
                                         in1=Y0[s][:, :, :], op0=ALU.mult, op1=ALU.add).then_inc(x1_ready, 1)

            def x2(u, s, r):
                dve.wait_ge(mm1b_done, u + 1)
                dve.wait_ge(x1b_ready, u + 1)
                past(dve, x2_stored[s], 16 * r)
                past(dve, x3_ready, u + 1 - NS)
                dve.tensor_tensor(X2[s][:, :, :], PT[s][:, :, :], X1B[s][:, :, :], ALU.add).then_inc(x2_ready, 1)

            def z2(u, s, r):
                dve.wait_ge(mm2_done, u + 1)
                dve.scalar_tensor_tensor(out=Z2[s][:, :, :], in0=PB[s][:, :, :], scalar=0.5, in1=row(w.b2),
                                         op0=ALU.mult, op1=ALU.add).then_inc(z2_ready, 1)

            def l2(u, s, r):
                dve.wait_ge(z2_ready, u + 1)
                leaky(L2[s][:, :, :], Z2[s][:, :, :]).then_inc(l2_ready, 1)

            def c1(u, s, r):
                dve.wait_ge(c1z_ready, u + 1)
                leaky(C1T[s][:, :, :, :].rearrange("p c t n -> p (c t n)"),
                      C1Z[s][:, :, :].rearrange("p c n -> p (c n)")).then_inc(c1_ready, 1)

            def xh(u, s, r):
                dve.wait_ge(h_ready[3], u + 1)
                past(dve, out_ready, u + 1 - NS)
                dve.tensor_tensor(XH[s][:, :, :], H[s][:, :, :], X3[s][:, :, :], ALU.add).then_inc(xh_ready, 1)

            def l4(u, s, r):
                dve.wait_ge(z4_ready, u + 1)
                leaky(L4[s][:, :, :], Z4[s][:, :, :]).then_inc(l4_ready, 1)

            run_slots(dve, chain, groups, [
                (l2, 2), (stats(0), 0), (stats(3), 2), (shift(0), 0), (c1, 3), (shift(3), 2), (x2, 1),
                (stats(2), 1), (z0, 0), (y0, 0), (shift(2), 1), (x1, 0), (stats(1), 0), (xh, 2), (l4, 3),
                (shift(1), 0), (z2, 1)])


class Phase:

    def __init__(self, nc, name):
        self.nc, self.name, self.ctx, self.sems = nc, name, ExitStack(), []

    def sb(self, name, shape, dt=F32):
        return self.ctx.enter_context(self.nc.sbuf_tensor(f"{self.name}_{name}", shape, dt))

    def sb2(self, name, shape, dt=F32):
        return [self.sb(f"{name}{s}", shape, dt) for s in range(2)]

    def pb2(self, name, shape):
        return [self.ctx.enter_context(self.nc.psum_tensor(f"{self.name}_{name}{s}", shape, F32)) for s in range(2)]

    def sem(self, name):
        self.sems.append(self.nc.alloc_semaphore(f"{self.name}_{name}"))
        return self.sems[-1]

    def sem2(self, name):
        return [self.sem(f"{name}{s}") for s in range(2)]

    def end(self):
        self.ctx.close()
        self.nc.clear_and_free_semaphores(self.sems)
        self.nc.all_engine_barrier(sem_only=True)


class Edges:
    pass


def run_units(eng, chain, units, body):
    def go(i, streams=(0, 1)):
        if chain:
            chain.body(i)
        body(i, streams)

    pairs = units // 2
    go(0)
    with eng.Fori(1, pairs - 1) as i:
        go(i)
    go(pairs - 1)
    if units % 2:
        go(pairs, (0,))


def load_edges(nc, ctx, w, a):
    e = Edges()
    E = a["dst"].shape[0]
    R = max(r for r in range(1, P + 1) if E % r == 0 and (E // r) % TG == 0)
    T = E // R
    assert (T // TG) >= 4
    e.R, e.T, e.units = R, T, T // TG

    def sb(name, shape, dt=F32):
        return ctx.enter_context(nc.sbuf_tensor("e_" + name, shape, dt))

    e.src = sb("src", [R, T], I32)
    e.dst = sb("dst", [R, T], I32)
    e.row = sb("row", [R, T], I32)
    e.cont = sb("cont", [R, T])
    e.pen = sb("pen", [R, T])
    e.shifts = [1 << k for k in range((T - 1).bit_length())]
    e.penr = sb("penr", [R, len(e.shifts), T])
    e.lastpen = sb("lastpen", [R, T])
    e.lead = sb("lead", [R, T])
    e.leadpen = sb("leadpen", [R, T])
    e.trailpen = sb("trailpen", [R, T])
    e.carry = sb("carry", [R, R])
    e.penf = sb("penf", [R, R])
    e.penb = sb("penb", [R, R])
    e.rcount = sb("rcount", [R, T])

    ph = Phase(nc, "mask")
    DX = ph.sb("dx", [R, T + 2], I32)
    DF = ph.sb("df", [R, T + 2])
    CONTN = ph.sb("contn", [R, T])
    TRAIL = ph.sb("trail", [R, T])
    ROWF = ph.sb("rowf", [R, T])
    SAME = ph.sb("same", [R, len(e.shifts), T])
    ONES = ph.sb("ones", [R, T])
    CNT = ph.sb("cnt", [R, T])
    HEADS = ph.sb("heads", [R, R])
    TAILS = ph.sb("tails", [R, R])
    EF = ph.sb("ef", [R, R])
    HB, TB = ph.pb2("pm", [R, R])
    CC = ph.ctx.enter_context(nc.psum_tensor("mask_cc", [R, 1], F32))
    edges_set, loaded, step = ph.sem("edges_set"), ph.sem("loaded"), ph.sem("dve_step")
    mats_ready, turned, eq_ready, tri_ready = (ph.sem(n) for n in ("mats_ready", "turned", "eq_ready", "tri_ready"))
    cnt_ready, cnt_carried = ph.sem("cnt_ready"), ph.sem("cnt_carried")
    dst = a["dst"].rearrange("(p t) -> p t", t=T)
    with nc.Block() as block, nc.allow_non_contiguous_dma("one index per partition"):
        @block.sync
        def _(sp):
            sp.dma_start(e.src[:, :], a["src"].rearrange("(p t) -> p t", t=T)).then_inc(loaded, 16)
            sp.dma_start(e.dst[:, :], dst).then_inc(loaded, 16)
            sp.dma_start(DX[:, 1:T + 1], dst).then_inc(loaded, 16)
            sp.wait_ge(edges_set, 1)
            sp.dma_start(DX[1:R, 0:1], dst[0:R - 1, T - 1:T]).then_inc(loaded, 16)
            sp.dma_start(DX[0:R - 1, T + 1:T + 2], dst[1:R, 0:1]).then_inc(loaded, 16)

        @block.gpsimd
        def _(pool):
            pool.memset(DX[:, 0:1], -1)
            pool.memset(DX[:, T + 1:T + 2], -1).then_inc(edges_set, 1)
            pool.wait_ge(eq_ready, 2)
            pool.affine_select(out=e.carry[:, :], in_=e.carry[:, :], compare_op=ALU.is_gt, fill=0.0,
                               base=0, pattern=[[1, R]], channel_multiplier=-1).then_inc(tri_ready, 1)
            pool.affine_select(out=EF[:, :], in_=EF[:, :], compare_op=ALU.is_gt, fill=0.0,
                               base=0, pattern=[[-1, R]], channel_multiplier=1).then_inc(tri_ready, 1)

        @block.tensor
        def _(pe):
            pe.wait_ge(mats_ready, 2)
            pe.transpose(HB[:, :], HEADS[:, :], w.ident[0:R, 0:R]).then_inc(turned, 1)
            pe.transpose(TB[:, :], TAILS[:, :], w.ident[0:R, 0:R]).then_inc(turned, 1)
            pe.wait_ge(tri_ready, 2)
            pe.wait_ge(cnt_ready, 1)
            pe.matmul(CC[:, :], e.carry[:, :], CNT[:, T - 1:T], start=True, stop=True).then_inc(cnt_carried, 1)

        @block.vector
        def _(dve):
            count = [0]

            def link(ins):
                count[0] += 1
                ins.then_inc(step, 1)
                dve.wait_ge(step, count[0])

            dve.memset(ONES[:, :], 1.0)
            dve.wait_ge(loaded, 80)
            link(dve.tensor_copy(DF[:, :], DX[:, :]))
            mid = DF[:, 1:T + 1]
            dve.tensor_copy(HEADS[:, :], DF[:, 1:2].to_broadcast([R, R])).then_inc(mats_ready, 1)
            dve.tensor_copy(TAILS[:, :], DF[:, T:T + 1].to_broadcast([R, R])).then_inc(mats_ready, 1)
            dve.tensor_tensor(e.cont[:, :], mid, DF[:, 0:T], ALU.is_equal)
            link(dve.tensor_tensor(CONTN[:, :], mid, DF[:, 2:T + 2], ALU.is_equal))
            dve.tensor_scalar(e.lastpen[:, :], CONTN[:, :], -BIG, None, ALU.mult)
            dve.tensor_scalar(e.pen[:, :], e.cont[:, :], -1.0, BIG, ALU.add, ALU.mult)
            for k, shift in enumerate(e.shifts):
                last = dve.tensor_tensor(SAME[:, k, 0:T - shift], DF[:, 1:T + 1 - shift], DF[:, 1 + shift:T + 1],
                                         ALU.is_equal)
            link(last)
            for k, shift in enumerate(e.shifts):
                dve.tensor_scalar(e.penr[:, k, 0:T - shift], SAME[:, k, 0:T - shift], -1.0, BIG, ALU.add, ALU.mult)
            dve.tensor_tensor_scan(e.lead[:, :], e.cont[:, :], e.cont[:, :], 1.0, ALU.mult, ALU.mult)
            dve.tensor_scalar(TRAIL[:, :], mid, DF[:, T:T + 1], None, ALU.is_equal)
            dve.tensor_tensor_scan(CNT[:, :], e.cont[:, :], ONES[:, :], 0.0, ALU.mult, ALU.add).then_inc(cnt_ready, 1)
            link(dve.scalar_tensor_tensor(out=ROWF[:, :], in0=CONTN[:, :], scalar=65536.0, in1=mid,
                                          op0=ALU.mult, op1=ALU.add))
            dve.tensor_copy(e.row[:, :], ROWF[:, :])
            dve.tensor_scalar(e.leadpen[:, :], e.lead[:, :], -1.0, BIG, ALU.add, ALU.mult)
            dve.tensor_scalar(e.trailpen[:, :], TRAIL[:, :], -1.0, BIG, ALU.add, ALU.mult)
            dve.wait_ge(turned, 2)
            dve.tensor_scalar(e.carry[:, :], HB[:, :], DF[:, T:T + 1], None, ALU.is_equal).then_inc(eq_ready, 1)
            dve.tensor_scalar(EF[:, :], TB[:, :], DF[:, 1:2], None, ALU.is_equal).then_inc(eq_ready, 1)
            dve.wait_ge(tri_ready, 2)
            dve.tensor_scalar(e.penf[:, :], EF[:, :], -1.0, BIG, ALU.add, ALU.mult)
            dve.tensor_scalar(e.penb[:, :], e.carry[:, :], -1.0, BIG, ALU.add, ALU.mult)
            dve.wait_ge(cnt_carried, 1)
            link(dve.scalar_tensor_tensor(out=CNT[:, :], in0=e.lead[:, :], scalar=CC[:, 0:1], in1=CNT[:, :],
                                          op0=ALU.mult, op1=ALU.add))
            link(dve.tensor_scalar(CNT[:, :], CNT[:, :], 1.0, 1.0, ALU.max, ALU.add))
            dve.reciprocal(e.rcount[:, :], CNT[:, :])
    ph.end()
    return e


def edge_softmax(nc, w, e, name, H, as_src, as_self, ad_self, eps, out, spread):
    R, T = e.R, e.T
    ph = Phase(nc, name)
    A = ph.sb("a", [R, H, T])
    AS = ph.sb("as", [R, H, T])
    L = ph.sb("l", [R, H, T])
    LS = ph.sb("ls", [R, H, T])
    F = ph.sb("f", [R, H, T])
    B = ph.sb("b", [R, H, T])
    FAR = ph.sb("far", [R, 2 * H, T])
    OWN = ph.sb("own", [R, 2 * H, T])
    ENDS = ph.sb("ends", [R, 2, H, R])
    PICK = ph.sb("pick", [R, 2, H, R])
    CM = ph.sb("cm", [R, 2, H])
    DEN = ph.sb("den", [R, H, T])
    DT = ph.sb("dt", [R, H])
    PE_ENDS = [ph.ctx.enter_context(nc.psum_tensor(f"{name}_pe{d}", [R, H, P], F32)) for d in range(2)]
    PE_OWN = [ph.ctx.enter_context(nc.psum_tensor(f"{name}_po{d}", [R, H, P], F32)) for d in range(2)]
    PD = ph.ctx.enter_context(nc.psum_tensor(f"{name}_pd", [R, H], F32))
    step, ends_ready, ends_turned = ph.sem("dve_step"), ph.sem("ends_ready"), ph.sem("ends_turned")
    arg_ready, exp_ready, tails_ready, tails_carried, own_ready, own_turned = (
        ph.sem(n) for n in ("arg_ready", "exp_ready", "tails_ready", "tails_carried", "own_ready", "own_turned"))

    def turned(ap):
        return ap.rearrange("p t h -> p h t")

    with nc.Block() as block:
        @block.tensor
        def _(pe):
            if spread:
                pe.wait_ge(own_ready, 2 * H)
                for d in range(2):
                    for h in range(H):
                        last = pe.transpose(PE_OWN[d][:, h, 0:R], ENDS[:, d, h, :], w.ident[0:R, 0:R])
                last.then_inc(own_turned, 1)
            pe.wait_ge(ends_ready, 2 * H)
            for d in range(2):
                for h in range(H):
                    last = pe.transpose(PE_ENDS[d][:, h, 0:R], ENDS[:, d, h, :], w.ident[0:R, 0:R])
            last.then_inc(ends_turned, 1)
            pe.wait_ge(tails_ready, 1)
            pe.matmul(PD[:, :], e.carry[:, :], DT[:, :], start=True, stop=True).then_inc(tails_carried, 1)

        @block.scalar
        def _(act):
            act.wait_ge(arg_ready, 2)
            act.activation(out.w[:, :, :], F[:, :, :], ACT.Exp).then_inc(exp_ready, 1)
            act.activation(AS[:, :, :], LS[:, :, :], ACT.Exp).then_inc(exp_ready, 1)

        @block.vector
        def _(dve):
            count = [0]

            def link(ins):
                count[0] += 1
                ins.then_inc(step, 1)
                dve.wait_ge(step, count[0])

            def from_slot_on(m, heads_):
                for k, shift in enumerate(e.shifts):
                    n = T - shift
                    link(dve.tensor_tensor(FAR[:, 0:heads_, 0:n], m[:, :, shift:T],
                                           e.penr[:, k, None, 0:n].to_broadcast([R, heads_, n]), ALU.add))
                    link(dve.tensor_tensor(m[:, :, 0:n], m[:, :, 0:n], FAR[:, 0:heads_, 0:n], ALU.max))

            link(dve.tensor_tensor(AS[:, :, :], turned(as_self), turned(ad_self), ALU.add))
            link(dve.scalar_tensor_tensor(out=LS[:, :, :], in0=AS[:, :, :], scalar=SLOPE, in1=AS[:, :, :],
                                          op0=ALU.mult, op1=ALU.max))
            ad = turned(ad_self)
            if spread:
                lastpen = e.lastpen[:, None, :].to_broadcast([R, H, T])
                dve.tensor_tensor(OWN[:, 0:H, :], ad, lastpen, ALU.add)
                link(dve.tensor_tensor(OWN[:, H:2 * H, :], LS[:, :, :], lastpen, ALU.add))
                from_slot_on(OWN, 2 * H)
                for h in range(2 * H):
                    dve.tensor_copy(ENDS[:, h // H, h % H, :], OWN[:, h, 0:1].to_broadcast([R, R]))\
                        .then_inc(own_ready, 1)
                dve.wait_ge(own_turned, 1)
                for d in range(2):
                    last = dve.tensor_tensor(PICK[:, d, :, :], PE_OWN[d][:, :, 0:R],
                                             e.penb[:, None, :].to_broadcast([R, H, R]), ALU.add)
                link(last)
                link(dve.tensor_reduce(CM[:, :, :].rearrange("p d h -> p (d h)"),
                                       PICK[:, :, :, :].rearrange("p d h q -> p (d h) q"), AX, ALU.max))
                for h in range(2 * H):
                    last = dve.scalar_tensor_tensor(out=OWN[:, h, :], in0=e.trailpen[:, :],
                                                    scalar=CM[:, h // H, h % H:h % H + 1], in1=OWN[:, h, :],
                                                    op0=ALU.add, op1=ALU.max)
                link(last)
                link(dve.tensor_copy(LS[:, :, :], OWN[:, H:2 * H, :]))
                ad = OWN[:, 0:H, :]
            link(dve.tensor_tensor(A[:, :, :], turned(as_src), ad, ALU.add))
            link(dve.scalar_tensor_tensor(out=L[:, :, :], in0=A[:, :, :], scalar=SLOPE, in1=A[:, :, :],
                                          op0=ALU.mult, op1=ALU.max))
            for h in range(H):
                dve.tensor_tensor_scan(F[:, h, :], e.pen[:, :], L[:, h, :], -BIG, ALU.add, ALU.max)
            link(dve.tensor_copy(B[:, :, :], L[:, :, :]))
            from_slot_on(B, H)
            for d, (m, t) in enumerate(((F, T - 1), (B, 0))):
                for h in range(H):
                    dve.tensor_copy(ENDS[:, d, h, :], m[:, h, t:t + 1].to_broadcast([R, R])).then_inc(ends_ready, 1)
            dve.wait_ge(ends_turned, 1)
            for d, pen in enumerate((e.penf, e.penb)):
                last = dve.tensor_tensor(PICK[:, d, :, :], PE_ENDS[d][:, :, 0:R],
                                         pen[:, None, :].to_broadcast([R, H, R]), ALU.add)
            link(last)
            link(dve.tensor_reduce(CM[:, :, :].rearrange("p d h -> p (d h)"),
                                   PICK[:, :, :, :].rearrange("p d h q -> p (d h) q"), AX, ALU.max))
            for h in range(H):
                dve.scalar_tensor_tensor(out=F[:, h, :], in0=e.leadpen[:, :], scalar=CM[:, 0, h:h + 1],
                                         in1=F[:, h, :], op0=ALU.add, op1=ALU.max)
                last = dve.scalar_tensor_tensor(out=B[:, h, :], in0=e.trailpen[:, :], scalar=CM[:, 1, h:h + 1],
                                                in1=B[:, h, :], op0=ALU.add, op1=ALU.max)
            link(last)
            link(dve.tensor_tensor(B[:, :, :], F[:, :, :], B[:, :, :], ALU.max))
            link(dve.tensor_tensor(B[:, :, :], B[:, :, :], LS[:, :, :], ALU.max))
            dve.tensor_tensor(F[:, :, :], L[:, :, :], B[:, :, :], ALU.subtract).then_inc(arg_ready, 1)
            dve.tensor_tensor(LS[:, :, :], LS[:, :, :], B[:, :, :], ALU.subtract).then_inc(arg_ready, 1)
            dve.wait_ge(exp_ready, 2)
            for h in range(H):
                last = dve.tensor_tensor_scan(DEN[:, h, :], e.cont[:, :], out.w[:, h, :], 0.0, ALU.mult, ALU.add)
            link(last)
            dve.tensor_copy(DT[:, :], DEN[:, :, T - 1]).then_inc(tails_ready, 1)
            dve.wait_ge(tails_carried, 1)
            for h in range(H):
                last = dve.scalar_tensor_tensor(out=DEN[:, h, :], in0=e.lead[:, :], scalar=PD[:, h:h + 1],
                                                in1=DEN[:, h, :], op0=ALU.mult, op1=ALU.add)
            link(last)
            link(dve.scalar_tensor_tensor(out=DEN[:, :, :], in0=DEN[:, :, :], scalar=eps, in1=AS[:, :, :],
                                          op0=ALU.add, op1=ALU.add))
            link(dve.reciprocal(out.rd[:, :, :], DEN[:, :, :]))
            dve.tensor_tensor(out.ws[:, :, :], AS[:, :, :], out.rd[:, :, :], ALU.mult)
            dve.tensor_tensor(out.lrd[:, :, :], out.rd[:, :, :],
                              e.lead[:, None, :].to_broadcast([R, H, T]), ALU.mult)
    ph.end()


def gather_rows(pool, chain, table, index, stage, tile, done, u):
    alone(pool)
    n = chain.add(pool.tensor_copy(stage[:, :], index[:, bass.ds(u * TG, TG)]))
    chain.upto(n)
    alone(pool)
    for j in range(TG):
        pool.indirect_dma_start(out=tile[:, j, :], out_offset=None, in_=table,
                                in_offset=bass.IndirectOffsetOnAxis(ap=stage[:, j:j + 1], axis=0)).then_inc(done, 16)


def scatter_rows(pool, chain, table, index, stage, tile, done, u):
    alone(pool)
    n = chain.add(pool.tensor_copy(stage[:, :], index[:, bass.ds(u * TG, TG)]))
    chain.upto(n)
    alone(pool)
    for j in range(TG):
        pool.indirect_dma_start(out=table, out_offset=bass.IndirectOffsetOnAxis(ap=stage[:, j:j + 1], axis=0),
                                in_=tile[:, j, :], in_offset=None, bounds_check=table.shape[0] - 1,
                                oob_is_err=False).then_inc(done, 16)


def project_ends(nc, w, e, name, source_table, keep_dst, weight, widths, outs):
    R, units = e.R, e.units
    ph = Phase(nc, name)
    XG = ph.sb2("xg", [R, TG, D])
    IDX = ph.sb2("idx", [R, TG], I32)
    H = ph.sb2("h", [R, TG, D])
    HT = ph.sb2("ht", [P, TG, P])
    ST = ph.sb2("st", [R, TG, 6])
    MV = ph.sb2("mv", [R, TG, 2])
    VE = ph.sb2("ve", [R, TG])
    RS = ph.sb2("rs", [R, TG])
    PT = ph.pb2("pt", [P, TG, P])
    wide = [512 if x > 256 else 256 if x > 128 else 128 for x in widths]
    PW = [ph.ctx.enter_context(nc.psum_tensor(f"{name}_pw{s}", [R, TG, wide[s]], F32)) for s in range(2)]
    gathered = ph.sem2("gathered")
    kept = ph.sem("kept")
    pool_step, dve_step = ph.sem("pool_step"), ph.sem("dve_step")
    stats_ready, rstd_ready, h_ready, turned, ht_ready, mm_done, saved = (
        ph.sem(n) for n in ("stats_ready", "rstd_ready", "h_ready", "turned", "ht_ready", "mm_done", "saved"))
    index = [e.src, e.dst]
    gathers = (0, 1) if keep_dst else (0,)

    with nc.Block() as block:
        @block.sync
        def _(sp):
            def body(i, streams):
                if keep_dst:
                    sp.wait_ge(gathered[1], 16 * TG * (i + 1))
                    sp.dma_start(tiles(e.x, i), XG[1][:, :, :]).then_inc(kept, 16)
                else:
                    past(sp, h_ready, 2 * i)
                    sp.dma_start(XG[1][:, :, :], tiles(e.x, i)).then_inc(gathered[1], 16)

            run_units(sp, None, 2 * units, body)
            if keep_dst:
                sp.wait_ge(kept, 16 * units)

        @block.gpsimd
        def _(pool):
            chain = Chain(pool, pool_step)

            def gather(i, s):
                gather_rows(pool, chain, source_table, index[s], IDX[s], XG[s], gathered[s], i)

            for s in gathers:
                gather(0, s)

            def body(i, streams):
                for s in streams:
                    u = 2 * i + s
                    pool.wait_ge(stats_ready, u + 1)
                    layer_rstd(chain, MV[s], VE[s][:, :], RS[s][:, :], w.half[0:R, :]).then_inc(rstd_ready, 1)
                    if s in gathers and not (isinstance(i, int) and i == units - 1):
                        pool.wait_ge(h_ready, u + 1)
                        if s == 1:
                            pool.wait_ge(kept, 16 * (i + 1))
                        gather(i + 1, s)

            run_units(pool, chain, 2 * units, body)

        @block.scalar
        def _(act):
            def body(i, streams):
                for s in streams:
                    act.wait_ge(turned, 2 * i + s + 1)
                    act.activation(HT[s][:, :, 0:R], PT[s][:, :, 0:R], ACT.Relu).then_inc(ht_ready, 1)
                for s in streams:
                    act.wait_ge(mm_done, 2 * i + s + 1)
                    alone(act)
                    act.activation(outs[s][:, bass.ds(i * TG, TG), :], PW[s][:, :, 0:widths[s]], ACT.Copy)\
                        .then_inc(saved, 1)

            run_units(act, None, 2 * units, body)

        @block.tensor
        def _(pe):
            def body(i, streams):
                for s in streams:
                    pe.wait_ge(h_ready, 2 * i + s + 1)
                    for j in range(TG):
                        last = pe.transpose(PT[s][:, j, 0:R], H[s][:, j, :], w.ident[0:R, 0:R])
                    last.then_inc(turned, 1)
                for s in streams:
                    u = 2 * i + s
                    pe.wait_ge(ht_ready, u + 1)
                    past(pe, saved, u - 1)
                    for j in range(TG):
                        last = pe.matmul(PW[s][:, j, 0:widths[s]], HT[s][:, j, 0:R], weight[s], start=True, stop=True)
                    last.then_inc(mm_done, 1)

            run_units(pe, None, 2 * units, body)

        @block.vector
        def _(dve):
            chain = Chain(dve, dve_step)

            def body(i, streams):
                for s in streams:
                    u = 2 * i + s
                    dve.wait_ge(gathered[s], (16 * TG if s in gathers else 16) * (i + 1))
                    layer_stats(chain, XG[s], ST[s], MV[s], TG).then_inc(stats_ready, 1)
                for s in streams:
                    u = 2 * i + s
                    dve.wait_ge(rstd_ready, u + 1)
                    past(dve, turned, u - 1)
                    layer_norm(chain, XG[s], MV[s], RS[s], H[s], TG).then_inc(h_ready, 1)

            run_units(dve, chain, 2 * units, body)
    ph.end()


def per_head(ap, u, d):
    v = ap[:, :, bass.ds(u * TG, TG)].rearrange("p h t -> p t h")
    return v[:, :, :, None].to_broadcast([v.shape[0], TG, ap.shape[1], d])


def heads(ap, h):
    return ap.rearrange("p t (h d) -> p t h d", h=h)


def tiles(ap, u):
    return ap[:, bass.ds(u * TG, TG)]


def move_rows(sp, units, dram, tile_in, used, loaded, tile_out=None, ready=None, kept=None):
    def load(i, s):
        past(sp, used, 2 * i + s - 1)
        sp.dma_start(tile_in[s][:, :, :], tiles(dram, 2 * i + s)).then_inc(loaded[s], 16)

    def body(i, streams):
        for s in streams:
            if not (isinstance(i, int) and 2 * (i + 1) + s >= units):
                load(i + 1, s)
            if ready is not None:
                sp.wait_ge(ready, 2 * i + s + 1)
                sp.dma_start(tiles(dram, 2 * i + s), tile_out[s][:, :, :]).then_inc(kept[s], 16)

    load(0, 0)
    load(0, 1)
    run_units(sp, None, units, body)
    if ready is not None:
        sp.wait_ge(kept[0], 16 * (units - units // 2))
        sp.wait_ge(kept[1], 16 * (units // 2))


def sum_runs(nc, w, e, name, msg, H, sm, carried):
    R, units = e.R, e.units
    width = carried.shape[1]
    ph = Phase(nc, name)
    M = ph.sb2("m", [R, TG, width])
    RUN = ph.sb2("run", [R, TG, width])
    CS = ph.sb2("cs", [R, TG])
    PC = ph.ctx.enter_context(nc.psum_tensor(f"{name}_pc", [R, width], F32))
    step, run_ready, stored, tail_done = (ph.sem(n) for n in ("dve_step", "run_ready", "stored", "tail_done"))
    last_run = RUN[(units - 1) % 2][:, TG - 1, :]
    with nc.Block() as block:
        @block.vector
        def _(dve):
            chain = Chain(dve, step)
            chain.add(dve.memset(RUN[1][:, TG - 1, :], 0.0))

            def body(i, streams):
                for s in streams:
                    u = 2 * i + s
                    alone(dve)
                    chain.add(dve.tensor_copy(CS[s][:, :], tiles(e.cont, u)))
                    alone(dve)
                    n = chain.add(dve.tensor_tensor(heads(M[s][:, :, :], H), heads(tiles(msg, u), H),
                                                    per_head(sm.w, u, width // H), ALU.mult))
                    past(dve, stored, u - 1)
                    for j in range(TG):
                        chain.upto(n)
                        before = RUN[s][:, j - 1, :] if j else RUN[1 - s][:, TG - 1, :]
                        ins = dve.scalar_tensor_tensor(out=RUN[s][:, j, :], in0=before, scalar=CS[s][:, j:j + 1],
                                                       in1=M[s][:, j, :], op0=ALU.mult, op1=ALU.add)
                        if j < TG - 1:
                            n = chain.add(ins)
                    ins.then_inc(run_ready, 1)
                    dve.wait_ge(run_ready, u + 1)

            run_units(dve, chain, units, body)

        @block.scalar
        def _(act):
            def body(i, streams):
                for s in streams:
                    act.wait_ge(run_ready, 2 * i + s + 1)
                    alone(act)
                    act.activation(tiles(msg, 2 * i + s), RUN[s][:, :, :], ACT.Copy).then_inc(stored, 1)

            run_units(act, None, units, body)
            act.wait_ge(tail_done, 1)
            act.activation(carried[:, :], PC[:, :], ACT.Copy)

        @block.tensor
        def _(pe):
            pe.wait_ge(run_ready, units)
            pe.matmul(PC[:, :], e.carry[:, :], last_run, start=True, stop=True).then_inc(tail_done, 1)
    ph.end()


def sum_layer0(nc, w, e, name, xps, xpd, edge_attr, sm, carried0, carried1):
    R, units, H = e.R, e.units, w.H0
    ph = Phase(nc, name)
    M = ph.sb2("m", [R, TG, D])
    RUN = ph.sb2("run", [R, TG, D])
    EA = ph.sb2("ea", [R, TG, D])
    ER = ph.sb2("er", [R, TG, D])
    CS = ph.sb2("cs", [R, TG])
    A = ph.sb2("a", [R, TG, D])
    B = ph.sb2("b", [R, TG, D])
    PC = ph.pb2("pc", [R, D])
    ea_loaded = ph.sem2("ea_loaded")
    step, run_ready, er_ready, er_stored, a_ready, b_ready, sum_ready, tail_done = (
        ph.sem(n) for n in ("dve_step", "run_ready", "er_ready", "er_stored", "a_ready", "b_ready", "sum_ready",
                            "tail_done"))
    ea = edge_attr.rearrange("(p t) d -> p t d", p=R)
    odd = (units - 1) % 2
    with nc.Block() as block:
        @block.sync
        def _(sp):
            def body(i, streams):
                for s in streams:
                    u = 2 * i + s
                    past(sp, er_ready, u - 1)
                    sp.dma_start(EA[s][:, :, :], ea[:, bass.ds(u * TG, TG), :]).then_inc(ea_loaded[s], 16)

            run_units(sp, None, units, body)

        @block.gpsimd
        def _(pool):
            def body(i, streams):
                for s in streams:
                    u = 2 * i + s
                    past(pool, sum_ready, u - 1)
                    alone(pool)
                    pool.tensor_tensor(heads(B[s][:, :, :], H), heads(tiles(xpd, u), H),
                                       per_head(sm.ws, u, D // H), ALU.mult).then_inc(b_ready, 1)
                    pool.wait_ge(run_ready, u + 1)
                    alone(pool)
                    pool.tensor_tensor(heads(A[s][:, :, :], H), heads(RUN[s][:, :, :], H),
                                       per_head(sm.rd, u, D // H), ALU.mult).then_inc(a_ready, 1)

            run_units(pool, None, units, body)

        @block.scalar
        def _(act):
            def body(i, streams):
                for s in streams:
                    u = 2 * i + s
                    act.wait_ge(er_ready, u + 1)
                    act.wait_ge(b_ready, u + 1)
                    alone(act)
                    act.activation(tiles(xpd, u), ER[s][:, :, :], ACT.Copy).then_inc(er_stored, 1)

            run_units(act, None, units, body)
            act.wait_ge(tail_done, 1)
            act.activation(carried0[:, :], PC[0][:, :], ACT.Copy)
            act.activation(carried1[:, :], PC[1][:, :], ACT.Copy)

        @block.tensor
        def _(pe):
            pe.wait_ge(run_ready, units)
            pe.wait_ge(er_ready, units)
            pe.matmul(PC[0][:, :], e.carry[:, :], RUN[odd][:, TG - 1, :], start=True, stop=True)
            pe.matmul(PC[1][:, :], e.carry[:, :], ER[odd][:, TG - 1, :], start=True, stop=True).then_inc(tail_done, 1)

        @block.vector
        def _(dve):
            chain = Chain(dve, step)
            chain.add(dve.memset(RUN[1][:, TG - 1, :], 0.0))
            chain.add(dve.memset(ER[1][:, TG - 1, :], 0.0))

            def body(i, streams):
                for s in streams:
                    u = 2 * i + s
                    alone(dve)
                    chain.add(dve.tensor_copy(CS[s][:, :], tiles(e.cont, u)))
                    alone(dve)
                    n = chain.add(dve.tensor_tensor(heads(M[s][:, :, :], H), heads(tiles(xps, u), H),
                                                    per_head(sm.w, u, D // H), ALU.mult))
                    past(dve, a_ready, u - 1)
                    past(dve, er_stored, u - 1)
                    dve.wait_ge(ea_loaded[s], 16 * (i + 1))
                    for j in range(TG):
                        chain.upto(n)
                        for run, new in ((RUN, M), (ER, EA)):
                            before = run[s][:, j - 1, :] if j else run[1 - s][:, TG - 1, :]
                            ins = dve.scalar_tensor_tensor(out=run[s][:, j, :], in0=before, scalar=CS[s][:, j:j + 1],
                                                           in1=new[s][:, j, :], op0=ALU.mult, op1=ALU.add)
                            if j < TG - 1:
                                n = chain.add(ins)
                            else:
                                ins.then_inc(run_ready if run is RUN else er_ready, 1)
                    dve.wait_ge(run_ready, u + 1)
                    dve.wait_ge(er_ready, u + 1)
                for s in streams:
                    u = 2 * i + s
                    dve.wait_ge(a_ready, u + 1)
                    dve.wait_ge(b_ready, u + 1)
                    alone(dve)
                    dve.tensor_tensor(tiles(xps, u), A[s][:, :, :], B[s][:, :, :], ALU.add).then_inc(sum_ready, 1)

            run_units(dve, chain, units, body)
    ph.end()


def layers01(nc, w, e, name, out0, agg1, sm, carried0, carried1, table):
    R, units, H = e.R, e.units, w.H0
    ph = Phase(nc, name)
    X = ph.sb2("x", [R, TG, D])
    C0, C1, Z0A, Z0, Y0, S0, AG, X1, X1B, X2, HN = (
        ph.sb2(n, [R, TG, D]) for n in ("c0", "c1", "z0a", "z0", "y0", "s0", "ag", "x1", "x1b", "x2", "h"))
    HT, AT, Z1T = (ph.sb2(n, [P, TG, P]) for n in ("ht", "at", "z1t"))
    IDX = ph.sb2("idx", [R, TG], I32)
    ST, MV, VE, RS = ph.sb2("st", [R, TG, 6]), ph.sb2("mv", [R, TG, 2]), ph.sb2("ve", [R, TG]), ph.sb2("rs", [R, TG])
    PH, PG, P1, P2 = (ph.pb2(n, [P, TG, P]) for n in ("ph", "pg", "p1", "p2"))
    scattered, loaded, kept = ph.sem2("scattered"), ph.sem2("loaded"), ph.sem2("kept")
    pool_step, dve_step = ph.sem("pool_step"), ph.sem("dve_step")
    (c_ready, z0a_ready, z0_ready, ag_ready, s0_ready, x1_ready, x1b_ready, stats_ready, rstd_ready, h_ready, turned,
     ht_ready, mm1_done, z1_ready, mm1b_done, x2_ready) = (ph.sem(n) for n in (
         "c_ready", "z0a_ready", "z0_ready", "ag_ready", "s0_ready", "x1_ready", "x1b_ready", "stats_ready",
         "rstd_ready", "h_ready", "turned", "ht_ready", "mm1_done", "z1_ready", "mm1b_done", "x2_ready"))

    def row(bias):
        return bias[0:R, None, :].to_broadcast([R, TG, D])

    with nc.Block() as block:
        @block.sync
        def _(sp):
            move_rows(sp, units, e.x, X, x1_ready, loaded, X2, x2_ready, kept)

        @block.gpsimd
        def _(pool):
            chain = Chain(pool, pool_step)

            def carry(i, s):
                u = 2 * i + s
                past(pool, ag_ready, u - 1)
                past(pool, z0a_ready, u - 1)
                alone(pool)
                pool.tensor_tensor(heads(C0[s][:, :, :], H), heads(carried0[:, None, :].to_broadcast([R, TG, D]), H),
                                   per_head(sm.lrd, u, D // H), ALU.mult)
                alone(pool)
                pool.tensor_tensor(C1[s][:, :, :], carried1[:, None, :].to_broadcast([R, TG, D]),
                                   tiles(e.lead, u)[:, :, None].to_broadcast([R, TG, D]), ALU.mult)\
                    .then_inc(c_ready, 1)

            def x1b(i, s):
                pool.wait_ge(x1_ready, 2 * i + s + 1)
                pool.tensor_tensor(X1B[s][:, :, :], X1[s][:, :, :], row(w.b1b), ALU.add).then_inc(x1b_ready, 1)

            def rstd(i, s):
                pool.wait_ge(stats_ready, 2 * i + s + 1)
                layer_rstd(chain, MV[s], VE[s][:, :], RS[s][:, :], w.half[0:R, :]).then_inc(rstd_ready, 1)

            def scatter(i, s):
                pool.wait_ge(x2_ready, 2 * i + s + 1)
                past(pool, scattered[s], 16 * TG * i)
                scatter_rows(pool, chain, table, e.row, IDX[s], X2[s], scattered[s], 2 * i + s)

            def body(i, streams):
                for stage in (carry, x1b, rstd, scatter):
                    for s in streams:
                        stage(i, s)

            run_units(pool, chain, units, body)
            pool.wait_ge(scattered[0], 16 * TG * (units - units // 2))
            pool.wait_ge(scattered[1], 16 * TG * (units // 2))

        @block.scalar
        def _(act):
            def s0(i, s):
                act.wait_ge(z0_ready, 2 * i + s + 1)
                act.activation(S0[s][:, :, :], Z0[s][:, :, :], ACT.Silu).then_inc(s0_ready, 1)

            def turn(i, s):
                act.wait_ge(turned, 2 * i + s + 1)
                act.activation(HT[s][:, :, 0:R], PH[s][:, :, 0:R], ACT.Relu)
                act.activation(AT[s][:, :, 0:R], PG[s][:, :, 0:R], ACT.Copy).then_inc(ht_ready, 1)

            def z1(i, s):
                act.wait_ge(mm1_done, 2 * i + s + 1)
                act.activation(Z1T[s][:, :, 0:R], P1[s][:, :, 0:R], ACT.Relu, bias=w.b1[:, 0:1]).then_inc(z1_ready, 1)

            def body(i, streams):
                for stage in (s0, turn, z1):
                    for s in streams:
                        stage(i, s)

            run_units(act, None, units, body)

        @block.tensor
        def _(pe):
            def turn(i, s):
                pe.wait_ge(h_ready, 2 * i + s + 1)
                pe.wait_ge(ag_ready, 2 * i + s + 1)
                for j in range(TG):
                    pe.transpose(PH[s][:, j, 0:R], HN[s][:, j, :], w.ident[0:R, 0:R])
                for j in range(TG):
                    last = pe.transpose(PG[s][:, j, 0:R], AG[s][:, j, :], w.ident[0:R, 0:R])
                last.then_inc(turned, 1)

            def mm1(i, s):
                pe.wait_ge(ht_ready, 2 * i + s + 1)
                pe.matmul(P1[s][:, :, 0:R], w.w1x[:, :], HT[s][:, :, 0:R], start=True, stop=False)
                pe.matmul(P1[s][:, :, 0:R], w.w1e[:, :], AT[s][:, :, 0:R], start=False, stop=True)\
                    .then_inc(mm1_done, 1)

            def mm1b(i, s):
                pe.wait_ge(z1_ready, 2 * i + s + 1)
                past(pe, x2_ready, 2 * i + s - 1)
                for j in range(TG):
                    last = pe.matmul(P2[s][0:R, j, 0:D], Z1T[s][:, j, 0:R], w.w1b[:, :], start=True, stop=True)
                last.then_inc(mm1b_done, 1)

            def body(i, streams):
                for stage in (turn, mm1, mm1b):
                    for s in streams:
                        stage(i, s)

            run_units(pe, None, units, body)

        @block.vector
        def _(dve):
            chain = Chain(dve, dve_step)
            y0_at = [0, 0]

            def z0(i, s):
                u = 2 * i + s
                dve.wait_ge(c_ready, u + 1)
                alone(dve)
                dve.tensor_tensor(Z0A[s][:, :, :], tiles(out0, u), C0[s][:, :, :], ALU.add).then_inc(z0a_ready, 1)
                alone(dve)
                past(dve, turned, u - 1)
                alone(dve)
                dve.tensor_tensor(AG[s][:, :, :], tiles(agg1, u), C1[s][:, :, :], ALU.add).then_inc(ag_ready, 1)
                dve.wait_ge(z0a_ready, u + 1)
                dve.tensor_tensor(Z0[s][:, :, :], Z0A[s][:, :, :], row(w.b0), ALU.add).then_inc(z0_ready, 1)
                dve.wait_ge(z0_ready, u + 1)
                dve.wait_ge(loaded[s], 16 * (i + 1))
                y0_at[s] = chain.add(dve.scalar_tensor_tensor(out=Y0[s][:, :, :], in0=Z0[s][:, :, :], scalar=0.5,
                                                              in1=X[s][:, :, :], op0=ALU.mult, op1=ALU.add))

            def x1(i, s):
                u = 2 * i + s
                dve.wait_ge(s0_ready, u + 1)
                chain.upto(y0_at[s])
                dve.scalar_tensor_tensor(out=X1[s][:, :, :], in0=S0[s][:, :, :], scalar=1.2 - 0.5,
                                         in1=Y0[s][:, :, :], op0=ALU.mult, op1=ALU.add).then_inc(x1_ready, 1)
                dve.wait_ge(x1_ready, u + 1)
                layer_stats(chain, X1[s], ST[s], MV[s], TG).then_inc(stats_ready, 1)

            def norm(i, s):
                dve.wait_ge(rstd_ready, 2 * i + s + 1)
                layer_norm(chain, X1[s], MV[s], RS[s], HN[s], TG).then_inc(h_ready, 1)

            def x2(i, s):
                u = 2 * i + s
                dve.wait_ge(mm1b_done, u + 1)
                dve.wait_ge(x1b_ready, u + 1)
                past(dve, scattered[s], 16 * TG * i)
                past(dve, kept[s], 16 * i)
                dve.tensor_tensor(X2[s][:, :, :], P2[s][0:R, :, 0:D], X1B[s][:, :, :], ALU.add).then_inc(x2_ready, 1)

            def body(i, streams):
                for stage in (z0, x1, norm, x2):
                    for s in streams:
                        stage(i, s)

            run_units(dve, chain, units, body)
    ph.end()


def gather_norm(nc, w, e, name, table, out, carried):
    R, units = e.R, e.units
    ph = Phase(nc, name)
    XG, HN, HR, RUN = (ph.sb2(n, [R, TG, D]) for n in ("xg", "h", "hr", "run"))
    IDX = ph.sb2("idx", [R, TG], I32)
    CS = ph.sb2("cs", [R, TG])
    ST, MV, VE, RS = ph.sb2("st", [R, TG, 6]), ph.sb2("mv", [R, TG, 2]), ph.sb2("ve", [R, TG]), ph.sb2("rs", [R, TG])
    PC = ph.ctx.enter_context(nc.psum_tensor(f"{name}_pc", [R, D], F32))
    gathered = ph.sem2("gathered")
    pool_step, dve_step, stats_ready, rstd_ready, h_ready, hr_ready, run_ready, stored, tail_done = (
        ph.sem(n) for n in ("pool_step", "dve_step", "stats_ready", "rstd_ready", "h_ready", "hr_ready", "run_ready",
                            "stored", "tail_done"))
    with nc.Block() as block:
        @block.gpsimd
        def _(pool):
            chain = Chain(pool, pool_step)

            def gather(i, s):
                gather_rows(pool, chain, table, e.src, IDX[s], XG[s], gathered[s], 2 * i + s)

            gather(0, 0)
            gather(0, 1)

            def body(i, streams):
                for s in streams:
                    pool.wait_ge(stats_ready, 2 * i + s + 1)
                    layer_rstd(chain, MV[s], VE[s][:, :], RS[s][:, :], w.half[0:R, :]).then_inc(rstd_ready, 1)
                for s in streams:
                    if not (isinstance(i, int) and 2 * (i + 1) + s >= units):
                        pool.wait_ge(h_ready, 2 * i + s + 1)
                        gather(i + 1, s)

            run_units(pool, chain, units, body)

        @block.scalar
        def _(act):
            def body(i, streams):
                for s in streams:
                    act.wait_ge(h_ready, 2 * i + s + 1)
                    past(act, run_ready, 2 * i + s - 1)
                    act.activation(HR[s][:, :, :], HN[s][:, :, :], ACT.Relu).then_inc(hr_ready, 1)
                for s in streams:
                    act.wait_ge(run_ready, 2 * i + s + 1)
                    alone(act)
                    act.activation(tiles(out, 2 * i + s), RUN[s][:, :, :], ACT.Copy).then_inc(stored, 1)

            run_units(act, None, units, body)
            act.wait_ge(tail_done, 1)
            act.activation(carried[:, :], PC[:, :], ACT.Copy)

        @block.tensor
        def _(pe):
            pe.wait_ge(run_ready, units)
            pe.matmul(PC[:, :], e.carry[:, :], RUN[(units - 1) % 2][:, TG - 1, :], start=True, stop=True)\
                .then_inc(tail_done, 1)

        @block.vector
        def _(dve):
            chain = Chain(dve, dve_step)
            chain.add(dve.memset(RUN[1][:, TG - 1, :], 0.0))

            def body(i, streams):
                for s in streams:
                    dve.wait_ge(gathered[s], 16 * TG * (i + 1))
                    alone(dve)
                    layer_stats(chain, XG[s], ST[s], MV[s], TG).then_inc(stats_ready, 1)
                for s in streams:
                    u = 2 * i + s
                    dve.wait_ge(rstd_ready, u + 1)
                    past(dve, hr_ready, u - 1)
                    layer_norm(chain, XG[s], MV[s], RS[s], HN[s], TG).then_inc(h_ready, 1)
                for s in streams:
                    u = 2 * i + s
                    alone(dve)
                    n = chain.add(dve.tensor_copy(CS[s][:, :], tiles(e.cont, u)))
                    dve.wait_ge(hr_ready, u + 1)
                    past(dve, stored, u - 1)
                    for j in range(TG):
                        chain.upto(n)
                        before = RUN[s][:, j - 1, :] if j else RUN[1 - s][:, TG - 1, :]
                        ins = dve.scalar_tensor_tensor(out=RUN[s][:, j, :], in0=before, scalar=CS[s][:, j:j + 1],
                                                       in1=HR[s][:, j, :], op0=ALU.mult, op1=ALU.add)
                        if j < TG - 1:
                            n = chain.add(ins)
                    ins.then_inc(run_ready, 1)
                    dve.wait_ge(run_ready, u + 1)

            run_units(dve, chain, units, body)
    ph.end()


def layer2(nc, w, e, name, run, carried, table):
    R, units = e.R, e.units
    ph = Phase(nc, name)
    X = ph.sb2("x", [R, TG, D])
    C, T1, T2, T3, Z, L, X3, HN = (ph.sb2(n, [R, TG, D]) for n in ("c", "t1", "t2", "t3", "z", "l", "x3", "h"))
    HT = ph.sb2("ht", [P, TG, P])
    IDX = ph.sb2("idx", [R, TG], I32)
    ST, MV, VE, RS = ph.sb2("st", [R, TG, 6]), ph.sb2("mv", [R, TG, 2]), ph.sb2("ve", [R, TG]), ph.sb2("rs", [R, TG])
    PT, PB = ph.pb2("pt", [P, TG, P]), ph.pb2("pb", [P, TG, P])
    scattered, loaded, kept = ph.sem2("scattered"), ph.sem2("loaded"), ph.sem2("kept")
    (pool_step, dve_step, c_ready, t1_ready, t2_ready, t3_ready, z_ready, l_ready, x3_ready, stats_ready,
     rstd_ready, h_ready, turned, ht_ready, mm_done) = (ph.sem(n) for n in (
         "pool_step", "dve_step", "c_ready", "t1_ready", "t2_ready", "t3_ready", "z_ready", "l_ready", "x3_ready",
         "stats_ready", "rstd_ready", "h_ready", "turned", "ht_ready", "mm_done"))
    with nc.Block() as block:
        @block.sync
        def _(sp):
            move_rows(sp, units, e.x, X, x3_ready, loaded, X3, x3_ready, kept)

        @block.gpsimd
        def _(pool):
            chain = Chain(pool, pool_step)

            def carry(i, s):
                u = 2 * i + s
                past(pool, t1_ready, u - 1)
                alone(pool)
                pool.tensor_tensor(C[s][:, :, :], carried[:, None, :].to_broadcast([R, TG, D]),
                                   tiles(e.lead, u)[:, :, None].to_broadcast([R, TG, D]), ALU.mult)\
                    .then_inc(c_ready, 1)

            def rstd(i, s):
                pool.wait_ge(stats_ready, 2 * i + s + 1)
                layer_rstd(chain, MV[s], VE[s][:, :], RS[s][:, :], w.half[0:R, :]).then_inc(rstd_ready, 1)

            def scatter(i, s):
                pool.wait_ge(x3_ready, 2 * i + s + 1)
                past(pool, scattered[s], 16 * TG * i)
                scatter_rows(pool, chain, table, e.row, IDX[s], X3[s], scattered[s], 2 * i + s)

            def body(i, streams):
                for stage in (carry, rstd, scatter):
                    for s in streams:
                        stage(i, s)

            run_units(pool, chain, units, body)
            pool.wait_ge(scattered[0], 16 * TG * (units - units // 2))
            pool.wait_ge(scattered[1], 16 * TG * (units // 2))

        @block.scalar
        def _(act):
            def body(i, streams):
                for s in streams:
                    act.wait_ge(turned, 2 * i + s + 1)
                    act.activation(HT[s][:, :, 0:R], PT[s][:, :, 0:R], ACT.Copy).then_inc(ht_ready, 1)

            run_units(act, None, units, body)

        @block.tensor
        def _(pe):
            def body(i, streams):
                for s in streams:
                    pe.wait_ge(t3_ready, 2 * i + s + 1)
                    for j in range(TG):
                        last = pe.transpose(PT[s][:, j, 0:R], T3[s][:, j, :], w.ident[0:R, 0:R])
                    last.then_inc(turned, 1)
                for s in streams:
                    pe.wait_ge(ht_ready, 2 * i + s + 1)
                    past(pe, z_ready, 2 * i + s - 1)
                    for j in range(TG):
                        last = pe.matmul(PB[s][0:R, j, 0:D], HT[s][:, j, 0:R], w.w2[:, :], start=True, stop=True)
                    last.then_inc(mm_done, 1)

            run_units(pe, None, units, body)

        @block.vector
        def _(dve):
            chain = Chain(dve, dve_step)

            def stats(i, s):
                u = 2 * i + s
                dve.wait_ge(loaded[s], 16 * (i + 1))
                layer_stats(chain, X[s], ST[s], MV[s], TG).then_inc(stats_ready, 1)
                dve.wait_ge(c_ready, u + 1)
                alone(dve)
                dve.tensor_tensor(T1[s][:, :, :], tiles(run, u), C[s][:, :, :], ALU.add).then_inc(t1_ready, 1)

            def norm(i, s):
                u = 2 * i + s
                dve.wait_ge(rstd_ready, u + 1)
                layer_norm(chain, X[s], MV[s], RS[s], HN[s], TG).then_inc(h_ready, 1)
                dve.wait_ge(h_ready, u + 1)
                dve.wait_ge(t1_ready, u + 1)
                dve.scalar_tensor_tensor(out=T2[s][:, :, :], in0=HN[s][:, :, :], scalar=0.0, in1=T1[s][:, :, :],
                                         op0=ALU.max, op1=ALU.add).then_inc(t2_ready, 1)
                dve.wait_ge(t2_ready, u + 1)
                past(dve, turned, u - 1)
                alone(dve)
                dve.tensor_tensor(T3[s][:, :, :], T2[s][:, :, :],
                                  tiles(e.rcount, u)[:, :, None].to_broadcast([R, TG, D]), ALU.mult)\
                    .then_inc(t3_ready, 1)

            def x3(i, s):
                u = 2 * i + s
                dve.wait_ge(mm_done, u + 1)
                dve.tensor_tensor(Z[s][:, :, :], PB[s][0:R, :, 0:D], w.b2[0:R, None, :].to_broadcast([R, TG, D]),
                                  ALU.add).then_inc(z_ready, 1)
                dve.wait_ge(z_ready, u + 1)
                dve.scalar_tensor_tensor(out=L[s][:, :, :], in0=Z[s][:, :, :], scalar=SLOPE, in1=Z[s][:, :, :],
                                         op0=ALU.mult, op1=ALU.max).then_inc(l_ready, 1)
                dve.wait_ge(l_ready, u + 1)
                past(dve, scattered[s], 16 * TG * i)
                past(dve, kept[s], 16 * i)
                dve.tensor_tensor(X3[s][:, :, :], X[s][:, :, :], L[s][:, :, :], ALU.add).then_inc(x3_ready, 1)

            def body(i, streams):
                for stage in (stats, norm, x3):
                    for s in streams:
                        stage(i, s)

            run_units(dve, chain, units, body)
    ph.end()


def layer3_first(nc, w, e, name, run, own, sm, carried, table):
    R, units, H, C3 = e.R, e.units, w.H3, w.C3
    W3 = C3 * P
    ph = Phase(nc, name)
    X, HN, XH = (ph.sb2(n, [R, TG, D]) for n in ("x", "h", "xh"))
    CR, V, SELF = (ph.sb2(n, [R, TG, W3]) for n in ("cr", "v", "self"))
    G = ph.sb2("g", [R, TG, D + 2])
    HT = ph.sb2("ht", [P, TG, P])
    VT = ph.sb2("vt", [P, C3, TG, P])
    IDX = ph.sb2("idx", [R, TG], I32)
    ST, MV, VE, RS = ph.sb2("st", [R, TG, 6]), ph.sb2("mv", [R, TG, 2]), ph.sb2("ve", [R, TG]), ph.sb2("rs", [R, TG])
    PT, PA = ph.pb2("pt", [P, TG, P]), ph.pb2("pa", [P, TG, W3])
    scattered, loaded, kept = ph.sem2("scattered"), ph.sem2("loaded"), ph.sem2("kept")
    (pool_step, dve_step, c_ready, xh_ready, stats_ready, rstd_ready, h_ready, turned, ht_ready, mm_done, self_ready,
     v_ready, v_turned, vt_ready, mm4_done, g_ready, g_kept) = (ph.sem(n) for n in (
         "pool_step", "dve_step", "c_ready", "xh_ready", "stats_ready", "rstd_ready", "h_ready", "turned",
         "ht_ready", "mm_done", "self_ready", "v_ready", "v_turned", "vt_ready", "mm4_done", "g_ready", "g_kept"))

    def halves(pa):
        return pa[:, :, :].rearrange("p t n -> p (t n)").rearrange("p (c t n) -> p c t n", c=C3, t=TG)

    with nc.Block() as block:
        @block.sync
        def _(sp):
            move_rows(sp, units, e.x, X, xh_ready, loaded, XH, xh_ready, kept)

        @block.gpsimd
        def _(pool):
            chain = Chain(pool, pool_step)

            def carry(i, s):
                u = 2 * i + s
                past(pool, v_ready, u - 1)
                alone(pool)
                pool.tensor_tensor(heads(CR[s][:, :, :], H), heads(carried[:, None, :].to_broadcast([R, TG, W3]), H),
                                   per_head(sm.lrd, u, W3 // H), ALU.mult).then_inc(c_ready, 1)

            def rstd(i, s):
                pool.wait_ge(stats_ready, 2 * i + s + 1)
                layer_rstd(chain, MV[s], VE[s][:, :], RS[s][:, :], w.half[0:R, :]).then_inc(rstd_ready, 1)

            def scatter(i, s):
                pool.wait_ge(g_ready, 2 * i + s + 1)
                past(pool, scattered[s], 16 * TG * i)
                scatter_rows(pool, chain, table, e.row, IDX[s], G[s], scattered[s], 2 * i + s)

            def body(i, streams):
                for stage in (rstd, carry, scatter):
                    for s in streams:
                        stage(i, s)

            run_units(pool, chain, units, body)
            pool.wait_ge(scattered[0], 16 * TG * (units - units // 2))
            pool.wait_ge(scattered[1], 16 * TG * (units // 2))

        @block.scalar
        def _(act):
            def turn(i, s):
                act.wait_ge(turned, 2 * i + s + 1)
                act.activation(HT[s][:, :, 0:R], PT[s][:, :, 0:R], ACT.Relu).then_inc(ht_ready, 1)

            def turn_v(i, s):
                act.wait_ge(v_turned, 2 * i + s + 1)
                for c in range(C3):
                    last = act.activation(VT[s][:, c, :, 0:R], halves(PA[s])[:, c, :, 0:R], ACT.Copy)
                last.then_inc(vt_ready, 1)

            def g(i, s):
                u = 2 * i + s
                act.wait_ge(mm4_done, u + 1)
                past(act, scattered[s], 16 * TG * i)
                act.activation(G[s][:, :, :], PA[s][0:R, :, 0:D + 2], ACT.Copy).then_inc(g_ready, 1)
                act.wait_ge(g_ready, u + 1)
                alone(act)
                act.activation(tiles(own, u), G[s][:, :, :], ACT.Copy).then_inc(g_kept, 1)

            def body(i, streams):
                for stage in (turn, turn_v, g):
                    for s in streams:
                        stage(i, s)

            run_units(act, None, units, body)

        @block.tensor
        def _(pe):
            def turn(i, s):
                pe.wait_ge(h_ready, 2 * i + s + 1)
                for j in range(TG):
                    last = pe.transpose(PT[s][:, j, 0:R], HN[s][:, j, :], w.ident[0:R, 0:R])
                last.then_inc(turned, 1)

            def mm3(i, s):
                pe.wait_ge(ht_ready, 2 * i + s + 1)
                past(pe, g_ready, 2 * i + s - 1)
                for j in range(TG):
                    last = pe.matmul(PA[s][0:R, j, :], HT[s][:, j, 0:R], w.w3[:, 0:W3], start=True, stop=True)
                last.then_inc(mm_done, 1)

            def turn_v(i, s):
                pe.wait_ge(v_ready, 2 * i + s + 1)
                for c in range(C3):
                    for j in range(TG):
                        last = pe.transpose(halves(PA[s])[:, c, j, 0:R], V[s][:, j, c * P:(c + 1) * P],
                                            w.ident[0:R, 0:R])
                last.then_inc(v_turned, 1)

            def mm4(i, s):
                pe.wait_ge(vt_ready, 2 * i + s + 1)
                for j in range(TG):
                    for c in range(C3):
                        last = pe.matmul(PA[s][0:R, j, 0:D + 2], VT[s][:, c, j, 0:R], w.w4[:, c, :],
                                         start=(c == 0), stop=(c == C3 - 1))
                last.then_inc(mm4_done, 1)

            def body(i, streams):
                for stage in (turn, mm3, turn_v, mm4):
                    for s in streams:
                        stage(i, s)

            run_units(pe, None, units, body)

        @block.vector
        def _(dve):
            chain = Chain(dve, dve_step)
            v_at = [0, 0]

            def stats(i, s):
                dve.wait_ge(loaded[s], 16 * (i + 1))
                layer_stats(chain, X[s], ST[s], MV[s], TG).then_inc(stats_ready, 1)

            def norm(i, s):
                u = 2 * i + s
                dve.wait_ge(rstd_ready, u + 1)
                layer_norm(chain, X[s], MV[s], RS[s], HN[s], TG).then_inc(h_ready, 1)
                dve.wait_ge(h_ready, u + 1)
                past(dve, kept[s], 16 * i)
                dve.scalar_tensor_tensor(out=XH[s][:, :, :], in0=HN[s][:, :, :], scalar=0.0, in1=X[s][:, :, :],
                                         op0=ALU.max, op1=ALU.add).then_inc(xh_ready, 1)

            def edge_part(i, s):
                u = 2 * i + s
                past(dve, v_turned, u - 1)
                alone(dve)
                n = chain.add(dve.tensor_tensor(heads(V[s][:, :, :], H), heads(tiles(run, u), H),
                                                per_head(sm.rd, u, W3 // H), ALU.mult))
                dve.wait_ge(c_ready, u + 1)
                chain.upto(n)
                v_at[s] = chain.add(dve.tensor_tensor(V[s][:, :, :], V[s][:, :, :], CR[s][:, :, :], ALU.add))

            def self_part(i, s):
                u = 2 * i + s
                dve.wait_ge(mm_done, u + 1)
                alone(dve)
                dve.tensor_tensor(heads(SELF[s][:, :, :], H), heads(PA[s][0:R, :, :], H),
                                  per_head(sm.ws, u, W3 // H), ALU.mult).then_inc(self_ready, 1)
                dve.wait_ge(self_ready, u + 1)
                chain.upto(v_at[s])
                n = chain.add(dve.tensor_tensor(V[s][:, :, :], V[s][:, :, :], SELF[s][:, :, :], ALU.add))
                chain.upto(n)
                n = chain.add(dve.tensor_tensor(V[s][:, :, :], V[s][:, :, :],
                                                w.b3row[0:R, None, :].to_broadcast([R, TG, W3]), ALU.add))
                chain.upto(n)
                dve.scalar_tensor_tensor(out=V[s][:, :, :], in0=V[s][:, :, :], scalar=SLOPE, in1=V[s][:, :, :],
                                         op0=ALU.mult, op1=ALU.max).then_inc(v_ready, 1)

            def body(i, streams):
                for stage in (stats, norm, edge_part, self_part):
                    for s in streams:
                        stage(i, s)

            run_units(dve, chain, units, body)
    ph.end()


def gather_last(nc, w, e, name, table, out):
    R, units = e.R, e.units
    ph = Phase(nc, name)
    XG = ph.sb2("xg", [R, TG, D + 2])
    IDX = ph.sb2("idx", [R, TG], I32)
    gathered = ph.sem2("gathered")
    pool_step, stored = ph.sem("pool_step"), ph.sem("stored")
    with nc.Block() as block:
        @block.gpsimd
        def _(pool):
            chain = Chain(pool, pool_step)

            def body(i, streams):
                for s in streams:
                    u = 2 * i + s
                    past(pool, stored, u - 1)
                    gather_rows(pool, chain, table, e.src, IDX[s], XG[s], gathered[s], u)

            run_units(pool, chain, units, body)

        @block.scalar
        def _(act):
            def body(i, streams):
                for s in streams:
                    act.wait_ge(gathered[s], 16 * TG * (i + 1))
                    alone(act)
                    act.activation(tiles(out, 2 * i + s), XG[s][:, :, :], ACT.Copy).then_inc(stored, 1)

            run_units(act, None, units, body)
    ph.end()


def layer3_second(nc, w, e, name, run, own, sm, carried, out_dram):
    R, units = e.R, e.units
    ph = Phase(nc, name)
    X, CR, SELF, V, Z, L, Y, OUT = (ph.sb2(n, [R, TG, D]) for n in ("x", "cr", "self", "v", "z", "l", "y", "out"))
    IDX = ph.sb2("idx", [R, TG], I32)
    scattered, loaded = ph.sem2("scattered"), ph.sem2("loaded")
    pool_step, dve_step, c_ready, y_ready, out_ready = (
        ph.sem(n) for n in ("pool_step", "dve_step", "c_ready", "y_ready", "out_ready"))
    with nc.Block() as block:
        @block.sync
        def _(sp):
            move_rows(sp, units, e.x, X, out_ready, loaded)

        @block.gpsimd
        def _(pool):
            chain = Chain(pool, pool_step)

            def parts(i, s):
                u = 2 * i + s
                past(pool, y_ready, u - 1)
                alone(pool)
                pool.tensor_tensor(CR[s][:, :, :], carried[:, None, :].to_broadcast([R, TG, D]),
                                   per_head(sm.lrd, u, D)[:, :, 0, :], ALU.mult)
                alone(pool)
                pool.tensor_tensor(SELF[s][:, :, :], tiles(own, u)[:, :, 0:D],
                                   per_head(sm.ws, u, D)[:, :, 0, :], ALU.mult).then_inc(c_ready, 1)

            def scatter(i, s):
                pool.wait_ge(out_ready, 2 * i + s + 1)
                past(pool, scattered[s], 16 * TG * i)
                scatter_rows(pool, chain, out_dram, e.row, IDX[s], OUT[s], scattered[s], 2 * i + s)

            def body(i, streams):
                for stage in (parts, scatter):
                    for s in streams:
                        stage(i, s)

            run_units(pool, chain, units, body)
            pool.wait_ge(scattered[0], 16 * TG * (units - units // 2))
            pool.wait_ge(scattered[1], 16 * TG * (units // 2))

        @block.vector
        def _(dve):
            chain = Chain(dve, dve_step)

            def link(ins):
                chain.upto(chain.add(ins))

            def body(i, streams):
                at = {}
                for s in streams:
                    u = 2 * i + s
                    alone(dve)
                    at[s] = chain.add(dve.tensor_tensor(V[s][:, :, :], tiles(run, u),
                                                        per_head(sm.rd, u, D)[:, :, 0, :], ALU.mult))
                for s in streams:
                    u = 2 * i + s
                    dve.wait_ge(c_ready, u + 1)
                    chain.upto(at[s])
                    link(dve.tensor_tensor(Z[s][:, :, :], V[s][:, :, :], CR[s][:, :, :], ALU.add))
                    dve.tensor_tensor(Y[s][:, :, :], Z[s][:, :, :], SELF[s][:, :, :], ALU.add).then_inc(y_ready, 1)
                    dve.wait_ge(y_ready, u + 1)
                    link(dve.tensor_tensor(Z[s][:, :, :], Y[s][:, :, :],
                                           w.b4[0:R, None, :].to_broadcast([R, TG, D]), ALU.add))
                    link(dve.scalar_tensor_tensor(out=L[s][:, :, :], in0=Z[s][:, :, :], scalar=SLOPE,
                                                  in1=Z[s][:, :, :], op0=ALU.mult, op1=ALU.max))
                    dve.wait_ge(loaded[s], 16 * (i + 1))
                    past(dve, scattered[s], 16 * TG * i)
                    dve.tensor_tensor(OUT[s][:, :, :], X[s][:, :, :], L[s][:, :, :], ALU.add).then_inc(out_ready, 1)

            run_units(dve, chain, units, body)
    ph.end()


class Weights:

    def __init__(self, nc, ctx, name, e, H):
        self.w, self.ws, self.rd, self.lrd = (
            ctx.enter_context(nc.sbuf_tensor(f"{name}_{n}", [e.R, H, e.T], F32)) for n in ("w", "ws", "rd", "lrd"))


def sparse_pass(nc, ctx, w, a, tables, out_dram):
    t2, t3, t4 = tables
    e = load_edges(nc, ctx, w, a)
    R, T = e.R, e.T
    e.x = nc.dram_tensor("dst_rows", (R, T, D), F32).ap()
    H0, H3, W3 = w.H0, w.H3, w.C3 * P
    ns = D + H0
    big = ctx.enter_context(nc.sbuf_tensor("big", [R, T, max(ns + D + 2 * H0, W3 + H3, 2 * (D + 2))], F32))
    al = ctx.enter_context(nc.sbuf_tensor("al", [R, T, 2 * H3], F32))
    c0 = ctx.enter_context(nc.sbuf_tensor("c0", [R, D], F32))
    c1 = ctx.enter_context(nc.sbuf_tensor("c1", [R, D], F32))
    c3 = ctx.enter_context(nc.sbuf_tensor("c3", [R, W3], F32))
    sm4 = Weights(nc, ctx, "sm4", e, max(H0, H3))
    sm1 = sm4_as(sm4, 1)

    src0, dst0 = big[:, :, 0:ns], big[:, :, ns:ns + D + 2 * H0]
    project_ends(nc, w, e, "p0", a["x"], True, (w.w0[:, 0:ns], w.w0[:, :]), (ns, D + 2 * H0), (src0, dst0))
    edge_softmax(nc, w, e, "q0", H0, src0[:, :, D:D + H0], dst0[:, :, D:D + H0], dst0[:, :, D + H0:D + 2 * H0],
                 1e-16, sm4, False)
    sum_layer0(nc, w, e, "s0", src0[:, :, 0:D], dst0[:, :, 0:D], a["edge_attr_128"], sm4, c0, c1)
    layers01(nc, w, e, "l01", src0[:, :, 0:D], dst0[:, :, 0:D], sm4, c0, c1, t2)
    gather_norm(nc, w, e, "g2", t2, big[:, :, 0:D], c0)
    layer2(nc, w, e, "l2", big[:, :, 0:D], c0, t3)
    src3 = big[:, :, 0:W3 + H3]
    project_ends(nc, w, e, "p3", t3, False, (w.w3[:, 0:W3 + H3], w.w3[:, W3:W3 + 2 * H3]),
                 (W3 + H3, 2 * H3), (src3, al[:, :, :]))
    edge_softmax(nc, w, e, "q3", H3, src3[:, :, W3:W3 + H3], al[:, :, 0:H3], al[:, :, H3:2 * H3], 0.0, sm4, True)
    sum_runs(nc, w, e, "s3", src3[:, :, 0:W3], H3, sm4, c3)
    own = big[:, :, 0:D + 2]
    layer3_first(nc, w, e, "l3", src3[:, :, 0:W3], own, sm4, c3, t4)
    src4 = big[:, :, D + 2:2 * (D + 2)]
    gather_last(nc, w, e, "g4", t4, src4)
    edge_softmax(nc, w, e, "q4", 1, src4[:, :, D:D + 1], own[:, :, D:D + 1], own[:, :, D + 1:D + 2], 0.0, sm1, True)
    sum_runs(nc, w, e, "s4", src4[:, :, 0:D], 1, sm1, c0)
    layer3_second(nc, w, e, "l4", src4[:, :, 0:D], own, sm1, c0, out_dram)


class sm4_as:

    def __init__(self, sm, H):
        self.w, self.ws, self.rd, self.lrd = (t[:, 0:H, :] for t in (sm.w, sm.ws, sm.rd, sm.lrd))


def gnn_kernel(nc, a, out):
    N = a["x"].shape[0]
    with ExitStack() as ctx:
        t2 = nc.dram_tensor("t2", (N, D), F32).ap()
        t3 = nc.dram_tensor("t3", (N, D), F32).ap()
        t4 = nc.dram_tensor("t4", (N, D + 2), F32).ap()
        w = load_weights(nc, ctx, a)
        dense_pass(nc, w, a["x"], (t2, t3, t4), out)
        sparse_pass(nc, ctx, w, a, (t2, t3, t4), out)


_INS = ['x', 'src', 'dst', 'edge_attr_128', 'L0_gnn_W', 'L0_gnn_att_src', 'L0_gnn_att_dst', 'L0_gnn_bias',
        'L1_gnn_W1', 'L1_gnn_b1', 'L1_gnn_W2', 'L1_gnn_b2', 'L2_gnn_W', 'L2_gnn_b', 'L3_gnn_W1',
        'L3_gnn_att_src1', 'L3_gnn_att_dst1', 'L3_gnn_bias1', 'L3_gnn_W2', 'L3_gnn_att_src2',
        'L3_gnn_att_dst2', 'L3_gnn_bias2']


def kernel(**inputs):
    import numpy as _np
    import concourse.bacc as _bacc
    from concourse import mybir as _mybir
    from concourse.bass_utils import run_bass_kernel_spmd as _run

    nc = _bacc.Bacc("TRN2", target_bir_lowering=False, num_devices=1)
    arrays, args = {}, {}
    for name in _INS:
        a = _np.ascontiguousarray(inputs[name])
        arrays[f"in_{name}_dram"] = a
        args[name] = nc.dram_tensor(f"in_{name}_dram", a.shape, _mybir.dt.from_np(a.dtype), kind="ExternalInput").ap()
    out = nc.dram_tensor("out_0_dram", inputs["x"].shape, _mybir.dt.float32, kind="ExternalOutput").ap()
    gnn_kernel(nc, args, out)
    r = _run(nc, [arrays], core_ids=[0])
    return r.results[0]["out_0_dram"]
```

```python
from contextlib import ExitStack

import concourse.bass as bass
from concourse import mybir

F32 = mybir.dt.float32
I32 = mybir.dt.int32
BF16 = mybir.dt.bfloat16
ALU = mybir.AluOpType
ACT = mybir.ActivationFunctionType
AX = mybir.AxisListType.X

P = 128
D = 128
TG = 4
NS = 4
GROUP = P * TG
EPS = 1e-5
SLOPE = 0.2
BIG = 1e30


def past(eng, sem, value):
    if isinstance(value, int) and value <= 0:
        return
    eng.wait_ge(sem, value)


class Chain:

    def __init__(self, eng, sem):
        self.eng, self.sem, self.base, self.n, self.before, self.per_body, self.i = eng, sem, 0, 0, 0, None, None

    def body(self, i):
        if isinstance(i, int) and i == 0:
            self.before = self.base = self.n
        elif isinstance(i, int) and self.i == i - 1:
            self.base = self.base + self.n
        else:
            self.per_body = self.per_body or self.n
            self.base = self.before + i * self.per_body
        self.n, self.i = 0, i if isinstance(i, int) else None

    def add(self, ins):
        ins.then_inc(self.sem, 1)
        self.n += 1
        return self.n

    def upto(self, n):
        self.eng.wait_ge(self.sem, self.base + n)


def alone(eng):
    eng.nop(nofuse=True)


def run_slots(eng, chain, units, order, ns=NS):
    lags = [lag for _, lag in order]
    chain = chain or Chain(eng, None)

    def slot(i, c):
        for stage, lag in order:
            u, r = ns * i + (c - lag), i + (c - lag) // ns
            if not (isinstance(u, int) and not 0 <= u < units):
                stage(u, (c - lag) % ns, r)

    peeled = 1 - (-max(lags) // ns) if max(lags) > 0 else 1
    assert units // ns > peeled and min(lags) >= -(units % ns)
    for n in range(min(lags), ns * peeled):
        before = chain.n
        slot(n // ns, n % ns)
    per_body = ns * (chain.n - before)
    ahead = chain.n
    with eng.Fori(peeled, units // ns) as i:
        chain.base, chain.n = ahead + (i - peeled) * per_body, 0
        for c in range(ns):
            slot(i, c)
        assert chain.n == per_body
    chain.base, chain.n = ahead + (units // ns - peeled) * per_body, 0
    for n in range(units // ns * ns, units + max(lags)):
        slot(n // ns, n % ns)


def layer_stats(chain, x, stats, mv, tiles):
    for j in range(tiles):
        last = chain.add(chain.eng.bn_stats(stats[:, j, :], x[:, j, :]))
    chain.upto(last)
    alone(chain.eng)
    for j in range(tiles):
        last = chain.eng.bn_aggr(mv[:, j, :], stats[:, j, :])
    return last


def layer_rstd(chain, mv, ve, rs, half):
    alone(chain.eng)
    n = chain.add(chain.eng.tensor_scalar(ve, mv[:, :, 1], EPS, None, ALU.add))
    chain.upto(n)
    return chain.eng.tensor_tensor(rs, ve, half[:, 0:ve.shape[1]], ALU.pow)


def layer_norm(chain, x, mv, rs, h, tiles):
    for j in range(tiles):
        last = chain.eng.tensor_scalar(h[:, j, :], x[:, j, :], mv[:, j, 0:1], rs[:, j:j + 1],
                                       ALU.subtract, ALU.mult)
    return last


def layer_shift(eng, nm, mv, rs):
    return eng.scalar_tensor_tensor(out=nm[:, :], in0=mv[:, :, 0], scalar=-1.0, in1=rs[:, :],
                                    op0=ALU.mult, op1=ALU.mult)


def norm_rows(act, out, x, rs, nm):
    for j in range(TG):
        last = act.activation(out[:, j, :], x[:, j, :], ACT.Relu, bias=nm[:, j:j + 1], scale=rs[:, j:j + 1])
    return last


def leaky_relu(dve, out, z):
    return dve.scalar_tensor_tensor(out=out, in0=z, scalar=SLOPE, in1=z, op0=ALU.mult, op1=ALU.max)


def bias_rows(pe, w, R, out, k):
    pe.matmul(out, w.ones[:, 0:R], w.bias_parts[:, k, None, :].to_broadcast([3, TG, D]), start=True, stop=False)


class Net:
    pass


def load_weights(nc, ctx, a):
    w = Net()

    def sb(name, shape, dt=F32):
        return ctx.enter_context(nc.sbuf_tensor(name, shape, dt))

    H0 = a["L0_gnn_att_src"].shape[0]
    H3 = a["L3_gnn_att_src1"].shape[0]
    C3 = a["L3_gnn_W1"].shape[1] // P
    w.H0, w.H3, w.C3 = H0, H3, C3
    w.w0 = sb("w0", [P, D + 2 * H0])
    w.w1x = sb("w1x", [P, D])
    w.w1e = sb("w1e", [P, D])
    w.w1b = sb("w1b", [P, D])
    w.w2 = sb("w2", [P, D])
    w.w2raw = sb("w2raw", [P, D])
    w.w3 = sb("w3", [P, C3 * P + 2 * H3])
    w.w4 = sb("w4", [P, C3, D + 2])
    w.b0 = sb("b0", [P, D])
    w.b1 = sb("b1", [P, 1])
    w.b1b = sb("b1b", [P, D])
    w.b2 = sb("b2", [P, D])
    w.b3 = sb("b3", [P, C3])
    w.b3row = sb("b3row", [P, C3 * P])
    w.b4 = sb("b4", [P, D])
    w.ident = sb("ident", [P, P])
    w.ones = sb("ones", [3, P], BF16)
    w.bias_parts = sb("bias_parts", [3, 3, D], BF16)
    w.half = sb("half", [P, 2 * TG])
    with ExitStack() as tmp:
        att = [tmp.enter_context(nc.sbuf_tensor(f"att{k}", [P, n], F32))
               for k, n in enumerate((D, D, C3 * P, C3 * P, D, D))]
        prod = tmp.enter_context(nc.sbuf_tensor("prod", [P, 8, C3 * P], F32))
        w2t = tmp.enter_context(nc.psum_tensor("w2t", [P, D], F32))
        part = [tmp.enter_context(nc.sbuf_tensor(f"part{k}", [3, 3, D], BF16)) for k in range(3)]
        partf = [tmp.enter_context(nc.sbuf_tensor(f"partf{k}", [3, 3, D], F32)) for k in range(3)]
        rest = tmp.enter_context(nc.sbuf_tensor("rest", [3, 3, D], F32))
        parts_sum = tmp.enter_context(nc.sbuf_tensor("parts_sum", [3, 3, D], F32))
        part_step = tmp.enter_context(nc.semaphore("part_step"))
        loaded = tmp.enter_context(nc.semaphore("weights_loaded"))
        ident_step = tmp.enter_context(nc.semaphore("ident_step"))
        prod_ready = tmp.enter_context(nc.semaphore("prod_ready"))
        w2_turned = tmp.enter_context(nc.semaphore("w2_turned"))
        block = tmp.enter_context(nc.Block())

        def rows(ap):
            return ap.rearrange("(a n) -> a n", a=1).to_broadcast([P, ap.shape[0]])

        loads = [
            (w.w0[:, 0:D], a["L0_gnn_W"]), (w.w1x[:, :], a["L1_gnn_W1"][0:D, :]),
            (w.w1e[:, :], a["L1_gnn_W1"][D:2 * D, :]), (w.w1b[:, :], a["L1_gnn_W2"]),
            (w.w2raw[:, :], a["L2_gnn_W"]), (w.w3[:, 0:C3 * P], a["L3_gnn_W1"]),
            (w.w4[:, :, 0:D], a["L3_gnn_W2"].rearrange("(c p) n -> p c n", p=P)),
            (w.b0[:, :], rows(a["L0_gnn_bias"])), (w.b1[:, :], a["L1_gnn_b1"].rearrange("(p a) -> p a", a=1)),
            (w.b1b[:, :], rows(a["L1_gnn_b2"])), (w.b2[:, :], rows(a["L2_gnn_b"])),
            (w.b3row[:, :], rows(a["L3_gnn_bias1"])), (w.b4[:, :], rows(a["L3_gnn_bias2"])),
        ] + [(w.b3[:, c:c + 1], a["L3_gnn_bias1"][c * P:(c + 1) * P].rearrange("(p a) -> p a", a=1))
             for c in range(C3)] + [
            (t[:, :], rows(a[n].rearrange("h d -> (h d)"))) for t, n in zip(att, (
                "L0_gnn_att_src", "L0_gnn_att_dst", "L3_gnn_att_src1", "L3_gnn_att_dst1",
                "L3_gnn_att_src2", "L3_gnn_att_dst2"))]

        @block.sync
        def _(sp):
            for dst, src in loads:
                sp.dma_start(dst, src).then_inc(loaded, 16)

        @block.gpsimd
        def _(pool):
            pool.memset(w.half[:, :], -0.5)
            pool.memset(w.ones[:, :], 1.0)
            pool.memset(w.ident[:, :], 0.0).then_inc(ident_step, 1)
            pool.wait_ge(ident_step, 1)
            pool.affine_select(out=w.ident[:, :], in_=w.ident[:, :], compare_op=ALU.not_equal, fill=1.0,
                               base=0, pattern=[[-1, P]], channel_multiplier=1).then_inc(ident_step, 1)
        @block.tensor
        def _(pe):
            pe.wait_ge(ident_step, 2)
            pe.wait_ge(loaded, 16 * len(loads))
            pe.transpose(w2t[:, :], w.w2raw[:, :], w.ident[:, :]).then_inc(w2_turned, 1)

        @block.vector
        def _(dve):
            dve.wait_ge(loaded, 16 * len(loads))
            folds = [(w.w0[:, 0:D], att[0][:, :], H0, w.w0[:, D:D + H0]),
                     (w.w0[:, 0:D], att[1][:, :], H0, w.w0[:, D + H0:D + 2 * H0]),
                     (w.w3[:, 0:C3 * P], att[2][:, :], H3, w.w3[:, C3 * P:C3 * P + H3]),
                     (w.w3[:, 0:C3 * P], att[3][:, :], H3, w.w3[:, C3 * P + H3:C3 * P + 2 * H3])]
            for c in range(C3):
                folds.append((w.w4[:, c, 0:D], att[4][:, :], 1, w.w4[:, c, D:D + 1]))
                folds.append((w.w4[:, c, 0:D], att[5][:, :], 1, w.w4[:, c, D + 1:D + 2]))
            for n, (weight, row, heads, out) in enumerate(folds):
                width = weight.shape[1]
                dve.tensor_tensor(prod[:, n, 0:width], weight, row, ALU.mult).then_inc(prod_ready, 1)
            for n, (weight, row, heads, out) in enumerate(folds):
                width = weight.shape[1]
                dve.wait_ge(prod_ready, n + 1)
                dve.tensor_reduce(out, prod[:, n, 0:width].rearrange("p (h d) -> p h d", h=heads), AX, ALU.add)
            dve.wait_ge(w2_turned, 1)
            dve.tensor_copy(w.w2[:, :], w2t[:, :])
            chain = Chain(dve, part_step)

            def link(ins):
                chain.upto(chain.add(ins))

            dve.wait_ge(ident_step, 2)
            for k, bias in enumerate((w.b0, w.b1b, w.b2)):
                link(dve.tensor_copy(rest[:, k, :], bias[0:3, :]))
            for k in range(3):
                link(dve.tensor_copy(part[k][:, :, :], rest[:, :, :]))
                link(dve.tensor_copy(partf[k][:, :, :], part[k][:, :, :]))
                if k < 2:
                    link(dve.tensor_tensor(rest[:, :, :], rest[:, :, :], partf[k][:, :, :], ALU.subtract))
            link(dve.tensor_scalar(parts_sum[:, :, :], partf[0][:, :, :], w.ident[0:3, 0:1], None, ALU.mult))
            for k in (1, 2):
                link(dve.scalar_tensor_tensor(out=parts_sum[:, :, :], in0=partf[k][:, :, :], scalar=w.ident[0:3, k:k + 1],
                                              in1=parts_sum[:, :, :], op0=ALU.mult, op1=ALU.add))
            dve.tensor_copy(w.bias_parts[:, :, :], parts_sum[:, :, :])
    return w


def dense_pass(nc, w, x_dram, tables, out_dram):
    t2_dram, t3_dram, t4_dram = tables
    N = x_dram.shape[0]
    groups = -(-N // GROUP)
    C3 = w.C3
    short = groups * GROUP - N
    assert 0 <= short < GROUP and short % TG == 0
    skip = short // TG

    with ExitStack() as ctx:
        def sb(name, shape, n=NS):
            return in_turn([ctx.enter_context(nc.sbuf_tensor(f"d_{name}{s}", shape, F32)) for s in range(n)])

        def pb(name, shape, n):
            return in_turn([ctx.enter_context(nc.psum_tensor(f"d_{name}{s}", shape, F32)) for s in range(n)])

        def sem(name):
            return ctx.enter_context(nc.semaphore("d_" + name))

        def in_turn(tiles):
            return (tiles * NS)[:NS]

        X = sb("x", [P, TG, D])
        X1 = sb("x1", [P, TG, D])
        X2 = sb("x2", [P, TG, D])
        X3 = sb("x3", [P, TG, D])
        XH = sb("xh", [P, TG, D])
        OUT = sb("out", [P, TG, D])
        H = [sb("h", [P, TG, D])] * 3 + [sb("h3", [P, TG, D])]
        HT = [sb("ht", [P, TG, P])] * 3 + [sb("ht3", [P, TG, P], 2)]
        Y0 = sb("y0", [P, TG, D])
        S0 = sb("s0", [P, TG, D])
        Z1T = sb("z1t", [P, TG, P])
        Z2 = sb("z2", [P, TG, D])
        L2 = sb("l2", [P, TG, D])
        C1Z = sb("c1z", [P, C3, TG * P], 2)
        C1T = sb("c1t", [P, C3, TG, P], 2)
        G = sb("g", [P, TG, D + 2])
        Z4 = sb("z4", [P, TG, D])
        L4 = sb("l4", [P, TG, D])
        ST = [sb(f"st{k}", [P, TG, 6]) for k in range(4)]
        MV = [sb(f"mv{k}", [P, TG, 2]) for k in range(4)]
        VE = [sb(f"ve{k}", [P, TG]) for k in range(4)]
        RS = [sb(f"rs{k}", [P, TG]) for k in range(4)]
        NM = [sb(f"nm{k}", [P, TG]) for k in range(4)]
        P0 = pb("p0", [P, TG, D], 1)
        P1 = pb("p1", [P, TG, D], 2)
        P2 = pb("p2", [P, TG, D], 1)
        PA = pb("pa", [P, TG, 2 * D], 2)
        PT = [P0, P1, P2, [pa[:, :, :].rearrange("p t n -> p (t n)")[:, 0:TG * P].rearrange("p (t n) -> p t n", t=TG)
                           for pa in PA]]

        x_loaded = [sem(f"x_loaded{s}") for s in range(NS)]
        x2_stored = [sem(f"x2_stored{s}") for s in range(NS)]
        x3_stored = [sem(f"x3_stored{s}") for s in range(NS)]
        g_stored = [sem(f"g_stored{s}") for s in range(NS)]
        out_stored = [sem(f"out_stored{s}") for s in range(NS)]
        pool_step = sem("pool_step")
        bn_ready = [sem(f"bn_ready{k}") for k in range(4)]
        stats_ready = [sem(f"stats_ready{k}") for k in range(4)]
        rstd_ready = [sem(f"rstd_ready{k}") for k in range(4)]
        shift_ready = [sem(f"shift_ready{k}") for k in range(4)]
        h_ready = [sem(f"h_ready{k}") for k in range(4)]
        turned = [sem(f"turned{k}") for k in range(4)]
        ht_ready = [sem(f"ht_ready{k}") for k in range(4)]
        mm0_done, y0_ready, s0_ready, x1_ready = (sem(n) for n in ("mm0_done", "y0_ready", "s0_ready", "x1_ready"))
        mm1_done, z1_ready, mm1b_done, x2_ready = (
            sem(n) for n in ("mm1_done", "z1_ready", "mm1b_done", "x2_ready"))
        mm2_done, z2_ready, l2_ready, x3_ready, xh_ready = (
            sem(n) for n in ("mm2_done", "z2_ready", "l2_ready", "x3_ready", "xh_ready"))
        mm3_done, c1z_ready, c1_ready, mm4_done, g_ready, z4_ready, l4_ready, out_ready = (
            sem(n) for n in ("mm3_done", "c1z_ready", "c1_ready", "mm4_done", "g_ready", "z4_ready", "l4_ready", "out_ready"))
        layer_in = [X, X1, X2, X3]
        layer_in_ready = [None, x1_ready, x2_ready, x3_ready]

        block = ctx.enter_context(nc.Block())

        def rows(dram, u):
            start = N - GROUP if last_group(u) else u * GROUP
            return dram[bass.ds(start, GROUP), :].rearrange("(p t) n -> p t n", t=TG)

        def last_group(u):
            return isinstance(u, int) and u == groups - 1

        @block.sync
        def _(sp):
            def load(u, s, r):
                past(sp, x1_ready, u + 1 - NS)
                sp.dma_start(X[s][:, :, :], rows(x_dram, u)).then_inc(x_loaded[s], 16)

            def store(dram, tile, ready, stored):
                def stage(u, s, r):
                    sp.wait_ge(ready, u + 1)
                    lo = skip if last_group(u) else 0
                    sp.dma_start(rows(dram, u)[lo:P], tile[s][lo:P, :, :]).then_inc(stored[s], 16)
                return stage

            run_slots(sp, None, groups, [
                (load, -1), (store(t2_dram, X2, x2_ready, x2_stored), 3), (store(t3_dram, X3, x3_ready, x3_stored), 5),
                (store(t4_dram, G, g_ready, g_stored), 9), (store(out_dram, OUT, out_ready, out_stored), 10)])
            for stored in (x2_stored, x3_stored, g_stored, out_stored):
                for s in range(NS):
                    sp.wait_ge(stored[s], 16 * len(range(s, groups, NS)))

        @block.gpsimd
        def _(pool):
            chain = Chain(pool, pool_step)

            def rstd(k):
                def stage(u, s, r):
                    pool.wait_ge(stats_ready[k], u + 1)
                    layer_rstd(chain, MV[k][s], VE[k][s][:, :], RS[k][s][:, :], w.half[:, :])\
                        .then_inc(rstd_ready[k], 1)
                return stage

            def x3(u, s, r):
                pool.wait_ge(l2_ready, u + 1)
                past(pool, x3_stored[s], 16 * r)
                past(pool, xh_ready, u + 1 - NS)
                pool.tensor_tensor(X3[s][:, :, :], X2[s][:, :, :], L2[s][:, :, :], ALU.add).then_inc(x3_ready, 1)

            def xh(u, s, r):
                pool.wait_ge(h_ready[3], u + 1)
                pool.wait_ge(x3_ready, u + 1)
                past(pool, out_ready, u + 1 - NS)
                pool.tensor_tensor(XH[s][:, :, :], H[3][s][:, :, :], X3[s][:, :, :], ALU.add).then_inc(xh_ready, 1)

            def z4(u, s, r):
                pool.wait_ge(g_ready, u + 1)
                pool.tensor_tensor(Z4[s][:, :, :], G[s][:, :, 0:D],
                                   w.b4[:, None, :].to_broadcast([P, TG, D]), ALU.add).then_inc(z4_ready, 1)

            def final(u, s, r):
                pool.wait_ge(l4_ready, u + 1)
                past(pool, out_stored[s], 16 * r)
                pool.wait_ge(xh_ready, u + 1)
                pool.tensor_tensor(OUT[s][:, :, :], XH[s][:, :, :], L4[s][:, :, :], ALU.add).then_inc(out_ready, 1)

            run_slots(pool, chain, groups, [
                (rstd(2), 3), (rstd(0), 0), (rstd(3), 5), (xh, 6), (z4, 8), (rstd(1), 1), (x3, 4),
                (final, 9)])

        @block.scalar
        def _(act):
            def turn(k):
                def stage(u, s, r):
                    act.wait_ge(turned[k], u + 1)
                    if k == 0:
                        past(act, mm2_done, u + 1 - NS)
                    act.activation(HT[k][s][:, :, :], PT[k][s][:, :, :], ACT.Copy).then_inc(ht_ready[k], 1)
                return stage

            def norm(k):
                def stage(u, s, r):
                    act.wait_ge(shift_ready[k], u + 1)
                    if k == 0:
                        past(act, turned[2], u + 1 - NS)
                    if k == 3:
                        past(act, turned[3], u + 1 - NS)
                        past(act, xh_ready, u + 1 - NS)
                    last = norm_rows(act, H[k][s], layer_in[k][s], RS[k][s], NM[k][s])
                    last.then_inc(h_ready[k], 1)
                return stage

            def s0(u, s, r):
                act.wait_ge(mm0_done, u + 1)
                act.activation(S0[s][:, :, :], P0[s][:, :, :], ACT.Silu).then_inc(s0_ready, 1)

            def z1(u, s, r):
                act.wait_ge(mm1_done, u + 1)
                act.activation(Z1T[s][:, :, :], P1[s][:, :, :], ACT.Relu, bias=w.b1[:, 0:1]).then_inc(z1_ready, 1)

            def c1(u, s, r):
                act.wait_ge(mm3_done, u + 1)
                pa = PA[s][:, :, :].rearrange("p t n -> p (t n)").rearrange("p (c n) -> p c n", c=C3)
                for c in range(C3):
                    last = act.activation(C1Z[s][:, c, :], pa[:, c, :], ACT.Identity, bias=w.b3[:, c:c + 1])
                last.then_inc(c1z_ready, 1)

            def g(u, s, r):
                act.wait_ge(mm4_done, u + 1)
                past(act, g_stored[s], 16 * r)
                past(act, z4_ready, u + 1 - NS)
                act.activation(G[s][:, :, :], PA[s][:, :, 0:D + 2], ACT.Copy).then_inc(g_ready, 1)

            run_slots(act, None, groups, [
                (s0, 1), (norm(1), 2), (turn(2), 4), (g, 8), (turn(1), 2), (c1, 7), (norm(0), 0), (z1, 2),
                (turn(3), 6), (turn(0), 0), (norm(2), 3), (norm(3), 5)])

        @block.tensor
        def _(pe):
            def turn(k):
                def stage(u, s, r):
                    pe.wait_ge(h_ready[k], u + 1)
                    past(pe, *[(y0_ready, u), (x2_ready, u - 1), (z2_ready, u), (g_ready, u - 1)][k])
                    for j in range(TG):
                        last = pe.transpose(PT[k][s][:, j, :], H[k][s][:, j, :], w.ident[:, :])
                    last.then_inc(turned[k], 1)
                return stage

            def mm0(u, s, r):
                pe.wait_ge(ht_ready[0], u + 1)
                bias_rows(pe, w, P, P0[s][:, :, :], 0)
                for j in range(TG):
                    last = pe.matmul(P0[s][:, j, :], HT[0][s][:, j, :], w.w0[:, 0:D], start=False, stop=j == TG - 1)
                last.then_inc(mm0_done, 1)

            def mm2(u, s, r):
                pe.wait_ge(ht_ready[2], u + 1)
                for j in range(TG):
                    last = pe.matmul(P2[s][:, j, :], HT[2][s][:, j, :], w.w2[:, :], start=True, stop=True)
                last.then_inc(mm2_done, 1)

            def mm1(u, s, r):
                pe.wait_ge(ht_ready[1], u + 1)
                pe.matmul(P1[s][:, :, :], w.w1x[:, :], HT[1][s][:, :, :], start=True, stop=True).then_inc(mm1_done, 1)

            def mm1b(u, s, r):
                pe.wait_ge(z1_ready, u + 1)
                bias_rows(pe, w, P, P1[s][:, :, :], 1)
                for j in range(TG):
                    last = pe.matmul(P1[s][:, j, :], Z1T[s][:, j, :], w.w1b[:, :], start=False, stop=j == TG - 1)
                last.then_inc(mm1b_done, 1)

            def mm3(u, s, r):
                pe.wait_ge(ht_ready[3], u + 1)
                pa = PA[s][:, :, :].rearrange("p t n -> p (t n)").rearrange("p (c n) -> p c n", c=C3)
                for c in range(C3):
                    last = pe.matmul(pa[:, c, :], w.w3[:, c * P:(c + 1) * P],
                                     HT[3][s][:, :, :].rearrange("p t n -> p (t n)"), start=True, stop=True)
                last.then_inc(mm3_done, 1)

            def mm4(u, s, r):
                pe.wait_ge(c1_ready, u + 1)
                for j in range(TG):
                    for c in range(C3):
                        last = pe.matmul(PA[s][:, j, 0:D + 2], C1T[s][:, c, j, :], w.w4[:, c, :],
                                         start=(c == 0), stop=(c == C3 - 1))
                last.then_inc(mm4_done, 1)

            run_slots(pe, None, groups, [
                (turn(2), 4), (mm4, 8), (turn(1), 2), (mm2, 4), (turn(3), 6), (mm1, 2), (turn(0), 0),
                (mm1b, 2), (mm3, 6), (mm0, 0)])

        @block.vector
        def _(dve):
            def row(bias):
                return bias[:, None, :].to_broadcast([P, TG, D])

            def stats(k):
                def stage(u, s, r):
                    if k == 0:
                        dve.wait_ge(x_loaded[s], 16 * (r + 1))
                    else:
                        dve.wait_ge(layer_in_ready[k], u + 1)
                    for j in range(TG):
                        last = dve.bn_stats(ST[k][s][:, j, :], layer_in[k][s][:, j, :])
                    last.then_inc(bn_ready[k], 1)
                return stage

            def aggr(k):
                def stage(u, s, r):
                    dve.wait_ge(bn_ready[k], u + 1)
                    alone(dve)
                    for j in range(TG):
                        last = dve.bn_aggr(MV[k][s][:, j, :], ST[k][s][:, j, :])
                    last.then_inc(stats_ready[k], 1)
                return stage

            def shift(k):
                def stage(u, s, r):
                    dve.wait_ge(rstd_ready[k], u + 1)
                    layer_shift(dve, NM[k][s], MV[k][s], RS[k][s]).then_inc(shift_ready[k], 1)
                return stage

            def y0(u, s, r):
                dve.wait_ge(s0_ready, u + 1)
                dve.scalar_tensor_tensor(out=Y0[s][:, :, :], in0=P0[s][:, :, :], scalar=0.5, in1=X[s][:, :, :],
                                         op0=ALU.mult, op1=ALU.add).then_inc(y0_ready, 1)

            def x1(u, s, r):
                dve.wait_ge(s0_ready, u + 1)
                dve.wait_ge(y0_ready, u + 1)
                dve.scalar_tensor_tensor(out=X1[s][:, :, :], in0=S0[s][:, :, :], scalar=1.2 - 0.5,
                                         in1=Y0[s][:, :, :], op0=ALU.mult, op1=ALU.add).then_inc(x1_ready, 1)

            def x2(u, s, r):
                dve.wait_ge(mm1b_done, u + 1)
                dve.wait_ge(x1_ready, u + 1)
                past(dve, x2_stored[s], 16 * r)
                past(dve, x3_ready, u + 1 - NS)
                dve.tensor_tensor(X2[s][:, :, :], P1[s][:, :, :], X1[s][:, :, :], ALU.add).then_inc(x2_ready, 1)

            def z2(u, s, r):
                dve.wait_ge(mm2_done, u + 1)
                dve.scalar_tensor_tensor(out=Z2[s][:, :, :], in0=P2[s][:, :, :], scalar=0.5, in1=row(w.b2),
                                         op0=ALU.mult, op1=ALU.add).then_inc(z2_ready, 1)

            def l2(u, s, r):
                dve.wait_ge(z2_ready, u + 1)
                leaky_relu(dve, L2[s][:, :, :], Z2[s][:, :, :]).then_inc(l2_ready, 1)

            def c1(u, s, r):
                dve.wait_ge(c1z_ready, u + 1)
                leaky_relu(dve, C1T[s][:, :, :, :].rearrange("p c t n -> p (c t n)"),
                      C1Z[s][:, :, :].rearrange("p c n -> p (c n)")).then_inc(c1_ready, 1)

            def l4(u, s, r):
                dve.wait_ge(z4_ready, u + 1)
                past(dve, out_ready, u + 1 - NS)
                leaky_relu(dve, L4[s][:, :, :], Z4[s][:, :, :]).then_inc(l4_ready, 1)

            run_slots(dve, None, groups, [
                (stats(0), 0), (aggr(2), 3), (y0, 1), (stats(3), 5), (aggr(0), 0), (x1, 1), (shift(2), 3),
                (aggr(3), 5), (l4, 9), (shift(0), 0), (stats(1), 1), (z2, 4), (shift(3), 5), (c1, 7),
                (aggr(1), 1), (l2, 4), (x2, 2), (shift(1), 1), (stats(2), 2)])


class Phase:

    def __init__(self, nc, name, ns=NS):
        self.ns = ns
        self.nc, self.name, self.ctx, self.sems = nc, name, ExitStack(), []

    def sb(self, name, shape, dt=F32):
        return self.ctx.enter_context(self.nc.sbuf_tensor(f"{self.name}_{name}", shape, dt))

    def sb2(self, name, shape, dt=F32):
        return [self.sb(f"{name}{s}", shape, dt) for s in range(2)]

    def sbs(self, name, shape, dt=F32):
        return [self.sb(f"{name}{s}", shape, dt) for s in range(self.ns)]

    def pbs(self, name, shape):
        return [self.ctx.enter_context(self.nc.psum_tensor(f"{self.name}_{name}{s}", shape, F32)) for s in range(self.ns)]

    def stream_sems(self, name):
        return [self.sem(f"{name}{s}") for s in range(self.ns)]

    def pb2(self, name, shape):
        return [self.ctx.enter_context(self.nc.psum_tensor(f"{self.name}_{name}{s}", shape, F32)) for s in range(2)]

    def sem(self, name):
        self.sems.append(self.nc.alloc_semaphore(f"{self.name}_{name}"))
        return self.sems[-1]

    def sem2(self, name):
        return [self.sem(f"{name}{s}") for s in range(2)]

    def end(self):
        self.ctx.close()
        self.nc.clear_and_free_semaphores(self.sems)
        self.nc.all_engine_barrier(sem_only=True)


class Edges:
    pass


def run_units(eng, chain, units, body):
    def go(i, streams=(0, 1)):
        if chain:
            chain.body(i)
        body(i, streams)

    pairs = units // 2
    go(0)
    with eng.Fori(1, pairs - 1) as i:
        go(i)
    go(pairs - 1)
    if units % 2:
        go(pairs, (0,))


def load_edges(nc, ctx, w, a):
    e = Edges()
    E = a["dst"].shape[0]
    R = max(r for r in range(1, P + 1) if E % r == 0 and (E // r) % TG == 0)
    T = E // R
    assert (T // TG) >= 4
    e.R, e.T, e.units = R, T, T // TG

    def sb(name, shape, dt=F32):
        return ctx.enter_context(nc.sbuf_tensor("e_" + name, shape, dt))

    e.src = sb("src", [R, T], I32)
    e.dst = sb("dst", [R, T], I32)
    e.row = sb("row", [R, T], I32)
    e.cont = sb("cont", [R, T])
    e.pen = sb("pen", [R, T])
    e.shifts = [1 << k for k in range((T - 1).bit_length())]
    e.penr = sb("penr", [R, len(e.shifts), T])
    e.lastpen = sb("lastpen", [R, T])
    e.lead = sb("lead", [R, T])
    e.leadpen = sb("leadpen", [R, T])
    e.trailpen = sb("trailpen", [R, T])
    e.carry = sb("carry", [R, R])
    e.penf = sb("penf", [R, R])
    e.penb = sb("penb", [R, R])
    e.rcount = sb("rcount", [R, T])

    ph = Phase(nc, "mask")
    DX = ph.sb("dx", [R, T + 2], I32)
    DF = ph.sb("df", [R, T + 2])
    CONTN = ph.sb("contn", [R, T])
    TRAIL = ph.sb("trail", [R, T])
    ROWF = ph.sb("rowf", [R, T])
    SAME = ph.sb("same", [R, len(e.shifts), T])
    ONES = ph.sb("ones", [R, T])
    CNT = ph.sb("cnt", [R, T])
    HEADS = ph.sb("heads", [R, R])
    TAILS = ph.sb("tails", [R, R])
    EF = ph.sb("ef", [R, R])
    HB, TB = ph.pb2("pm", [R, R])
    CC = ph.ctx.enter_context(nc.psum_tensor("mask_cc", [R, 1], F32))
    edges_set, loaded, step = ph.sem("edges_set"), ph.sem("loaded"), ph.sem("dve_step")
    mats_ready, turned, eq_ready, tri_ready = (ph.sem(n) for n in ("mats_ready", "turned", "eq_ready", "tri_ready"))
    cnt_ready, cnt_carried = ph.sem("cnt_ready"), ph.sem("cnt_carried")
    dst = a["dst"].rearrange("(p t) -> p t", t=T)
    with nc.Block() as block, nc.allow_non_contiguous_dma("one index per partition"):
        @block.sync
        def _(sp):
            sp.dma_start(e.src[:, :], a["src"].rearrange("(p t) -> p t", t=T)).then_inc(loaded, 16)
            sp.dma_start(e.dst[:, :], dst).then_inc(loaded, 16)
            sp.dma_start(DX[:, 1:T + 1], dst).then_inc(loaded, 16)
            sp.wait_ge(edges_set, 1)
            sp.dma_start(DX[1:R, 0:1], dst[0:R - 1, T - 1:T]).then_inc(loaded, 16)
            sp.dma_start(DX[0:R - 1, T + 1:T + 2], dst[1:R, 0:1]).then_inc(loaded, 16)

        @block.gpsimd
        def _(pool):
            pool.memset(DX[:, 0:1], -1)
            pool.memset(DX[:, T + 1:T + 2], -1).then_inc(edges_set, 1)
            pool.wait_ge(eq_ready, 2)
            pool.affine_select(out=e.carry[:, :], in_=e.carry[:, :], compare_op=ALU.is_gt, fill=0.0,
                               base=0, pattern=[[1, R]], channel_multiplier=-1).then_inc(tri_ready, 1)
            pool.affine_select(out=EF[:, :], in_=EF[:, :], compare_op=ALU.is_gt, fill=0.0,
                               base=0, pattern=[[-1, R]], channel_multiplier=1).then_inc(tri_ready, 1)

        @block.tensor
        def _(pe):
            pe.wait_ge(mats_ready, 2)
            pe.transpose(HB[:, :], HEADS[:, :], w.ident[0:R, 0:R]).then_inc(turned, 1)
            pe.transpose(TB[:, :], TAILS[:, :], w.ident[0:R, 0:R]).then_inc(turned, 1)
            pe.wait_ge(tri_ready, 2)
            pe.wait_ge(cnt_ready, 1)
            pe.matmul(CC[:, :], e.carry[:, :], CNT[:, T - 1:T], start=True, stop=True).then_inc(cnt_carried, 1)

        @block.vector
        def _(dve):
            count = [0]

            def link(ins):
                count[0] += 1
                ins.then_inc(step, 1)
                dve.wait_ge(step, count[0])

            dve.memset(ONES[:, :], 1.0)
            dve.wait_ge(loaded, 80)
            link(dve.tensor_copy(DF[:, :], DX[:, :]))
            mid = DF[:, 1:T + 1]
            dve.tensor_copy(HEADS[:, :], DF[:, 1:2].to_broadcast([R, R])).then_inc(mats_ready, 1)
            dve.tensor_copy(TAILS[:, :], DF[:, T:T + 1].to_broadcast([R, R])).then_inc(mats_ready, 1)
            dve.tensor_tensor(e.cont[:, :], mid, DF[:, 0:T], ALU.is_equal)
            link(dve.tensor_tensor(CONTN[:, :], mid, DF[:, 2:T + 2], ALU.is_equal))
            dve.tensor_scalar(e.lastpen[:, :], CONTN[:, :], -BIG, None, ALU.mult)
            dve.tensor_scalar(e.pen[:, :], e.cont[:, :], -1.0, BIG, ALU.add, ALU.mult)
            for k, shift in enumerate(e.shifts):
                last = dve.tensor_tensor(SAME[:, k, 0:T - shift], DF[:, 1:T + 1 - shift], DF[:, 1 + shift:T + 1],
                                         ALU.is_equal)
            link(last)
            for k, shift in enumerate(e.shifts):
                dve.tensor_scalar(e.penr[:, k, 0:T - shift], SAME[:, k, 0:T - shift], -1.0, BIG, ALU.add, ALU.mult)
            dve.tensor_tensor_scan(e.lead[:, :], e.cont[:, :], e.cont[:, :], 1.0, ALU.mult, ALU.mult)
            dve.tensor_scalar(TRAIL[:, :], mid, DF[:, T:T + 1], None, ALU.is_equal)
            dve.tensor_tensor_scan(CNT[:, :], e.cont[:, :], ONES[:, :], 0.0, ALU.mult, ALU.add).then_inc(cnt_ready, 1)
            link(dve.scalar_tensor_tensor(out=ROWF[:, :], in0=CONTN[:, :], scalar=65536.0, in1=mid,
                                          op0=ALU.mult, op1=ALU.add))
            dve.tensor_copy(e.row[:, :], ROWF[:, :])
            dve.tensor_scalar(e.leadpen[:, :], e.lead[:, :], -1.0, BIG, ALU.add, ALU.mult)
            dve.tensor_scalar(e.trailpen[:, :], TRAIL[:, :], -1.0, BIG, ALU.add, ALU.mult)
            dve.wait_ge(turned, 2)
            dve.tensor_scalar(e.carry[:, :], HB[:, :], DF[:, T:T + 1], None, ALU.is_equal).then_inc(eq_ready, 1)
            dve.tensor_scalar(EF[:, :], TB[:, :], DF[:, 1:2], None, ALU.is_equal).then_inc(eq_ready, 1)
            dve.wait_ge(tri_ready, 2)
            dve.tensor_scalar(e.penf[:, :], EF[:, :], -1.0, BIG, ALU.add, ALU.mult)
            dve.tensor_scalar(e.penb[:, :], e.carry[:, :], -1.0, BIG, ALU.add, ALU.mult)
            dve.wait_ge(cnt_carried, 1)
            link(dve.scalar_tensor_tensor(out=CNT[:, :], in0=e.lead[:, :], scalar=CC[:, 0:1], in1=CNT[:, :],
                                          op0=ALU.mult, op1=ALU.add))
            link(dve.tensor_scalar(CNT[:, :], CNT[:, :], 1.0, 1.0, ALU.max, ALU.add))
            dve.reciprocal(e.rcount[:, :], CNT[:, :])
    ph.end()
    return e


def edge_softmax(nc, w, e, name, H, as_src, as_self, ad_self, eps, out, spread):
    R, T = e.R, e.T
    ph = Phase(nc, name)
    A = ph.sb("a", [R, H, T])
    AS = ph.sb("as", [R, H, T])
    L = ph.sb("l", [R, H, T])
    LS = ph.sb("ls", [R, H, T])
    F = ph.sb("f", [R, H, T])
    B = ph.sb("b", [R, H, T])
    FAR = ph.sb("far", [R, 2 * H, T])
    OWN = ph.sb("own", [R, 2 * H, T])
    ENDS = ph.sb("ends", [R, 2, H, R])
    PICK = ph.sb("pick", [R, 2, H, R])
    CM = ph.sb("cm", [R, 2, H])
    DEN = ph.sb("den", [R, H, T])
    DT = ph.sb("dt", [R, H])
    PE_ENDS = [ph.ctx.enter_context(nc.psum_tensor(f"{name}_pe{d}", [R, H, P], F32)) for d in range(2)]
    PE_OWN = [ph.ctx.enter_context(nc.psum_tensor(f"{name}_po{d}", [R, H, P], F32)) for d in range(2)]
    PD = ph.ctx.enter_context(nc.psum_tensor(f"{name}_pd", [R, H], F32))
    step, ends_ready, ends_turned = ph.sem("dve_step"), ph.sem("ends_ready"), ph.sem("ends_turned")
    arg_ready, exp_ready, tails_ready, tails_carried, own_ready, own_turned = (
        ph.sem(n) for n in ("arg_ready", "exp_ready", "tails_ready", "tails_carried", "own_ready", "own_turned"))

    def turned(ap):
        return ap.rearrange("p t h -> p h t")

    with nc.Block() as block:
        @block.tensor
        def _(pe):
            if spread:
                pe.wait_ge(own_ready, 2 * H)
                for d in range(2):
                    for h in range(H):
                        last = pe.transpose(PE_OWN[d][:, h, 0:R], ENDS[:, d, h, :], w.ident[0:R, 0:R])
                last.then_inc(own_turned, 1)
            pe.wait_ge(ends_ready, 2 * H)
            for d in range(2):
                for h in range(H):
                    last = pe.transpose(PE_ENDS[d][:, h, 0:R], ENDS[:, d, h, :], w.ident[0:R, 0:R])
            last.then_inc(ends_turned, 1)
            pe.wait_ge(tails_ready, 1)
            pe.matmul(PD[:, :], e.carry[:, :], DT[:, :], start=True, stop=True).then_inc(tails_carried, 1)

        @block.scalar
        def _(act):
            act.wait_ge(arg_ready, 2)
            act.activation(out.w[:, :, :], F[:, :, :], ACT.Exp).then_inc(exp_ready, 1)
            act.activation(AS[:, :, :], LS[:, :, :], ACT.Exp).then_inc(exp_ready, 1)

        @block.vector
        def _(dve):
            count = [0]

            def link(ins):
                count[0] += 1
                ins.then_inc(step, 1)
                dve.wait_ge(step, count[0])

            def from_slot_on(m, heads_):
                for k, shift in enumerate(e.shifts):
                    n = T - shift
                    link(dve.tensor_tensor(FAR[:, 0:heads_, 0:n], m[:, :, shift:T],
                                           e.penr[:, k, None, 0:n].to_broadcast([R, heads_, n]), ALU.add))
                    link(dve.tensor_tensor(m[:, :, 0:n], m[:, :, 0:n], FAR[:, 0:heads_, 0:n], ALU.max))

            link(dve.tensor_tensor(AS[:, :, :], turned(as_self), turned(ad_self), ALU.add))
            link(dve.scalar_tensor_tensor(out=LS[:, :, :], in0=AS[:, :, :], scalar=SLOPE, in1=AS[:, :, :],
                                          op0=ALU.mult, op1=ALU.max))
            ad = turned(ad_self)
            if spread:
                lastpen = e.lastpen[:, None, :].to_broadcast([R, H, T])
                dve.tensor_tensor(OWN[:, 0:H, :], ad, lastpen, ALU.add)
                link(dve.tensor_tensor(OWN[:, H:2 * H, :], LS[:, :, :], lastpen, ALU.add))
                from_slot_on(OWN, 2 * H)
                for h in range(2 * H):
                    dve.tensor_copy(ENDS[:, h // H, h % H, :], OWN[:, h, 0:1].to_broadcast([R, R]))\
                        .then_inc(own_ready, 1)
                dve.wait_ge(own_turned, 1)
                for d in range(2):
                    last = dve.tensor_tensor(PICK[:, d, :, :], PE_OWN[d][:, :, 0:R],
                                             e.penb[:, None, :].to_broadcast([R, H, R]), ALU.add)
                link(last)
                link(dve.tensor_reduce(CM[:, :, :].rearrange("p d h -> p (d h)"),
                                       PICK[:, :, :, :].rearrange("p d h q -> p (d h) q"), AX, ALU.max))
                for h in range(2 * H):
                    last = dve.scalar_tensor_tensor(out=OWN[:, h, :], in0=e.trailpen[:, :],
                                                    scalar=CM[:, h // H, h % H:h % H + 1], in1=OWN[:, h, :],
                                                    op0=ALU.add, op1=ALU.max)
                link(last)
                link(dve.tensor_copy(LS[:, :, :], OWN[:, H:2 * H, :]))
                ad = OWN[:, 0:H, :]
            link(dve.tensor_tensor(A[:, :, :], turned(as_src), ad, ALU.add))
            link(dve.scalar_tensor_tensor(out=L[:, :, :], in0=A[:, :, :], scalar=SLOPE, in1=A[:, :, :],
                                          op0=ALU.mult, op1=ALU.max))
            for h in range(H):
                dve.tensor_tensor_scan(F[:, h, :], e.pen[:, :], L[:, h, :], -BIG, ALU.add, ALU.max)
            link(dve.tensor_copy(B[:, :, :], L[:, :, :]))
            from_slot_on(B, H)
            for d, (m, t) in enumerate(((F, T - 1), (B, 0))):
                for h in range(H):
                    dve.tensor_copy(ENDS[:, d, h, :], m[:, h, t:t + 1].to_broadcast([R, R])).then_inc(ends_ready, 1)
            dve.wait_ge(ends_turned, 1)
            for d, pen in enumerate((e.penf, e.penb)):
                last = dve.tensor_tensor(PICK[:, d, :, :], PE_ENDS[d][:, :, 0:R],
                                         pen[:, None, :].to_broadcast([R, H, R]), ALU.add)
            link(last)
            link(dve.tensor_reduce(CM[:, :, :].rearrange("p d h -> p (d h)"),
                                   PICK[:, :, :, :].rearrange("p d h q -> p (d h) q"), AX, ALU.max))
            for h in range(H):
                dve.scalar_tensor_tensor(out=F[:, h, :], in0=e.leadpen[:, :], scalar=CM[:, 0, h:h + 1],
                                         in1=F[:, h, :], op0=ALU.add, op1=ALU.max)
                last = dve.scalar_tensor_tensor(out=B[:, h, :], in0=e.trailpen[:, :], scalar=CM[:, 1, h:h + 1],
                                                in1=B[:, h, :], op0=ALU.add, op1=ALU.max)
            link(last)
            link(dve.tensor_tensor(B[:, :, :], F[:, :, :], B[:, :, :], ALU.max))
            link(dve.tensor_tensor(B[:, :, :], B[:, :, :], LS[:, :, :], ALU.max))
            dve.tensor_tensor(F[:, :, :], L[:, :, :], B[:, :, :], ALU.subtract).then_inc(arg_ready, 1)
            dve.tensor_tensor(LS[:, :, :], LS[:, :, :], B[:, :, :], ALU.subtract).then_inc(arg_ready, 1)
            dve.wait_ge(exp_ready, 2)
            for h in range(H):
                last = dve.tensor_tensor_scan(DEN[:, h, :], e.cont[:, :], out.w[:, h, :], 0.0, ALU.mult, ALU.add)
            link(last)
            dve.tensor_copy(DT[:, :], DEN[:, :, T - 1]).then_inc(tails_ready, 1)
            dve.wait_ge(tails_carried, 1)
            for h in range(H):
                last = dve.scalar_tensor_tensor(out=DEN[:, h, :], in0=e.lead[:, :], scalar=PD[:, h:h + 1],
                                                in1=DEN[:, h, :], op0=ALU.mult, op1=ALU.add)
            link(last)
            link(dve.scalar_tensor_tensor(out=DEN[:, :, :], in0=DEN[:, :, :], scalar=eps, in1=AS[:, :, :],
                                          op0=ALU.add, op1=ALU.add))
            link(dve.reciprocal(out.rd[:, :, :], DEN[:, :, :]))
            dve.tensor_tensor(out.ws[:, :, :], AS[:, :, :], out.rd[:, :, :], ALU.mult)
            dve.tensor_tensor(out.lrd[:, :, :], out.rd[:, :, :],
                              e.lead[:, None, :].to_broadcast([R, H, T]), ALU.mult)
    ph.end()


def gather_rows(pool, chain, table, index, stage, tile, done, u):
    alone(pool)
    n = chain.add(pool.tensor_copy(stage[:, :], index[:, bass.ds(u * TG, TG)]))
    chain.upto(n)
    alone(pool)
    for j in range(TG):
        pool.indirect_dma_start(out=tile[:, j, :], out_offset=None, in_=table,
                                in_offset=bass.IndirectOffsetOnAxis(ap=stage[:, j:j + 1], axis=0)).then_inc(done, 16)


def scatter_rows(pool, chain, table, index, stage, tile, done, u):
    alone(pool)
    n = chain.add(pool.tensor_copy(stage[:, :], index[:, bass.ds(u * TG, TG)]))
    chain.upto(n)
    alone(pool)
    for j in range(TG):
        pool.indirect_dma_start(out=table, out_offset=bass.IndirectOffsetOnAxis(ap=stage[:, j:j + 1], axis=0),
                                in_=tile[:, j, :], in_offset=None, bounds_check=table.shape[0] - 1,
                                oob_is_err=False).then_inc(done, 16)


def project_ends(nc, w, e, name, source_table, keep_dst, weights, outs, normed):
    R, units = e.R, e.units
    ph = Phase(nc, name)
    XG, H = (ph.sbs(n, [R, 2, TG, D]) for n in ("xg", "h"))
    IDX = ph.sbs("idx", [R, 2, TG], I32)
    HT = ph.sbs("ht", [P, 2, TG, P])
    ST, MV, VE, RS = (ph.sbs(n, [R, 2 * TG] + d) for n, d in (("st", [6]), ("mv", [2]), ("ve", []), ("rs", [])))
    NM = ph.sbs("nm", [R, TG])
    widths = [weight.shape[1] for weight in weights]
    PT = ph.ctx.enter_context(nc.psum_tensor(f"{name}_pt", [P, 2, TG, P], F32))
    PW = [ph.ctx.enter_context(nc.psum_tensor(
        f"{name}_pw{side}", [R, TG, 1 << (width - 1).bit_length()], F32)) for side, width in enumerate(widths)]
    gathered_src, gathered_dst = ph.stream_sems("gathered_src"), ph.stream_sems("gathered_dst")
    kept = ph.stream_sems("kept")
    pool_step, dve_step = ph.sem("pool_step"), ph.sem("dve_step")
    stats_ready, rstd_ready, shift_ready, src_ready, dst_ready, turned, ht_ready, mm_done, saved = (
        ph.sem(n) for n in ("stats_ready", "rstd_ready", "shift_ready", "src_ready", "dst_ready", "turned",
                            "ht_ready", "mm_done", "saved"))

    with nc.Block() as block:
        @block.sync
        def _(sp):
            def keep(u, s, r):
                sp.wait_ge(gathered_dst[s], 16 * TG * (r + 1))
                sp.dma_start(tiles(e.x, u), XG[s][:, 1]).then_inc(kept[s], 16)

            def load(u, s, r):
                past(sp, dst_ready, u + 1 - NS)
                sp.dma_start(XG[s][:, 1], tiles(e.x, u)).then_inc(gathered_dst[s], 16)

            run_slots(sp, None, units, [(keep, 1)] if keep_dst else [(load, -1)])
            if keep_dst:
                wait_streams(sp, kept, units, 16)

        @block.gpsimd
        def _(pool):
            chain = Chain(pool, pool_step)

            def gather_src(u, s, r):
                past(pool, src_ready, u + 1 - NS)
                gather_rows(pool, chain, source_table, e.src, IDX[s][:, 0], XG[s][:, 0], gathered_src[s], u)

            def gather_dst(u, s, r):
                past(pool, dst_ready, u + 1 - NS)
                past(pool, kept[s], 16 * r)
                gather_rows(pool, chain, source_table, e.dst, IDX[s][:, 1], XG[s][:, 1], gathered_dst[s], u)

            def rstd(u, s, r):
                pool.wait_ge(stats_ready, u + 1)
                layer_rstd(chain, MV[s], VE[s][:, :], RS[s][:, :], w.half[0:R, :]).then_inc(rstd_ready, 1)

            run_slots(pool, chain, units, [(gather_src, 0)] + ([(gather_dst, 0)] if keep_dst else [])
                      + [(rstd, normed - 1)])

        @block.scalar
        def _(act):
            def norm(u, s, r):
                act.wait_ge(shift_ready, u + 1)
                past(act, turned, u + 1 - NS)
                norm_rows(act, H[s][:, 0], XG[s][:, 0], RS[s], NM[s]).then_inc(src_ready, 1)

            def turn(u, s, r):
                act.wait_ge(turned, u + 1)
                for side in (0, 1):
                    last = act.activation(HT[s][:, side, :, 0:R], PT[:, side, :, 0:R], ACT.Relu)
                last.then_inc(ht_ready, 1)

            def save(u, s, r):
                act.wait_ge(mm_done, u + 1)
                alone(act)
                for side in (0, 1):
                    last = act.activation(outs[side][:, bass.ds(u * TG, TG), :], PW[side][:, :, 0:widths[side]],
                                          ACT.Copy)
                last.then_inc(saved, 1)

            run_slots(act, None, units, [(norm, normed), (save, normed + 1), (turn, normed)])

        @block.tensor
        def _(pe):
            def turn(u, s, r):
                pe.wait_ge(src_ready, u + 1)
                pe.wait_ge(dst_ready, u + 1)
                past(pe, ht_ready, u)
                for side in (0, 1):
                    for j in range(TG):
                        last = pe.transpose(PT[:, side, j, 0:R], H[s][:, side, j, :], w.ident[0:R, 0:R])
                last.then_inc(turned, 1)

            def mm(u, s, r):
                pe.wait_ge(ht_ready, u + 1)
                past(pe, saved, u)
                for side in (0, 1):
                    for j in range(TG):
                        last = pe.matmul(PW[side][:, j, 0:widths[side]], HT[s][:, side, j, 0:R], weights[side],
                                         start=True, stop=True)
                last.then_inc(mm_done, 1)

            run_slots(pe, None, units, [(mm, normed + 1), (turn, normed)])

        @block.vector
        def _(dve):
            chain = Chain(dve, dve_step)

            def stats(u, s, r):
                dve.wait_ge(gathered_src[s], 16 * TG * (r + 1))
                dve.wait_ge(gathered_dst[s], (16 * TG if keep_dst else 16) * (r + 1))
                alone(dve)
                layer_stats(chain, XG[s][:, :, :, :].rearrange("p b t n -> p (b t) n"), ST[s], MV[s], 2 * TG)\
                    .then_inc(stats_ready, 1)

            def shift(u, s, r):
                dve.wait_ge(rstd_ready, u + 1)
                layer_shift(dve, NM[s], MV[s][:, 0:TG], RS[s][:, 0:TG]).then_inc(shift_ready, 1)

            def norm(u, s, r):
                dve.wait_ge(rstd_ready, u + 1)
                past(dve, turned, u + 1 - NS)
                layer_norm(chain, XG[s][:, 1], MV[s][:, TG:2 * TG], RS[s][:, TG:2 * TG], H[s][:, 1], TG)\
                    .then_inc(dst_ready, 1)

            run_slots(dve, chain, units, [(shift, normed), (norm, normed), (stats, 1)])
    ph.end()


def per_head(ap, u, d):
    v = ap[:, :, bass.ds(u * TG, TG)].rearrange("p h t -> p t h")
    return v[:, :, :, None].to_broadcast([v.shape[0], TG, ap.shape[1], d])


def heads(ap, h):
    return ap.rearrange("p t (h d) -> p t h d", h=h)


def tiles(ap, u):
    return ap[:, bass.ds(u * TG, TG)]


def sum_runs(nc, w, e, name, msg, H, sm, carried):
    R, units = e.R, e.units
    width = carried.shape[1]
    ph = Phase(nc, name)
    M = ph.sb2("m", [R, TG, width])
    RUN = ph.sb2("run", [R, TG, width])
    CS = ph.sb2("cs", [R, TG])
    PC = ph.ctx.enter_context(nc.psum_tensor(f"{name}_pc", [R, width], F32))
    step, run_ready, stored, tail_done = (ph.sem(n) for n in ("dve_step", "run_ready", "stored", "tail_done"))
    last_run = RUN[(units - 1) % 2][:, TG - 1, :]
    with nc.Block() as block:
        @block.vector
        def _(dve):
            chain = Chain(dve, step)
            chain.add(dve.memset(RUN[1][:, TG - 1, :], 0.0))

            def body(i, streams):
                for s in streams:
                    u = 2 * i + s
                    alone(dve)
                    chain.add(dve.tensor_copy(CS[s][:, :], tiles(e.cont, u)))
                    alone(dve)
                    n = chain.add(dve.tensor_tensor(heads(M[s][:, :, :], H), heads(tiles(msg, u), H),
                                                    per_head(sm.w, u, width // H), ALU.mult))
                    past(dve, stored, u - 1)
                    for j in range(TG):
                        chain.upto(n)
                        before = RUN[s][:, j - 1, :] if j else RUN[1 - s][:, TG - 1, :]
                        ins = dve.scalar_tensor_tensor(out=RUN[s][:, j, :], in0=before, scalar=CS[s][:, j:j + 1],
                                                       in1=M[s][:, j, :], op0=ALU.mult, op1=ALU.add)
                        if j < TG - 1:
                            n = chain.add(ins)
                    ins.then_inc(run_ready, 1)
                    dve.wait_ge(run_ready, u + 1)

            run_units(dve, chain, units, body)

        @block.scalar
        def _(act):
            def body(i, streams):
                for s in streams:
                    act.wait_ge(run_ready, 2 * i + s + 1)
                    alone(act)
                    act.activation(tiles(msg, 2 * i + s), RUN[s][:, :, :], ACT.Copy).then_inc(stored, 1)

            run_units(act, None, units, body)
            act.wait_ge(tail_done, 1)
            act.activation(carried[:, :], PC[:, :], ACT.Copy)

        @block.tensor
        def _(pe):
            pe.wait_ge(run_ready, units)
            pe.matmul(PC[:, :], e.carry[:, :], last_run, start=True, stop=True).then_inc(tail_done, 1)
    ph.end()


def sum_layer0(nc, w, e, name, xps, xpd, edge_attr, sm, carried0, carried1):
    R, units, H = e.R, e.units, w.H0
    ph = Phase(nc, name)
    M = ph.sb2("m", [R, TG, D])
    RUN = ph.sb2("run", [R, TG, D])
    EA = ph.sb2("ea", [R, TG, D])
    ER = ph.sb2("er", [R, TG, D])
    CS = ph.sb2("cs", [R, TG])
    A = ph.sb2("a", [R, TG, D])
    B = ph.sb2("b", [R, TG, D])
    PC = ph.pb2("pc", [R, D])
    ea_loaded = ph.sem2("ea_loaded")
    step, run_ready, er_ready, er_stored, a_ready, b_ready, sum_ready, tail_done = (
        ph.sem(n) for n in ("dve_step", "run_ready", "er_ready", "er_stored", "a_ready", "b_ready", "sum_ready",
                            "tail_done"))
    ea = edge_attr.rearrange("(p t) d -> p t d", p=R)
    odd = (units - 1) % 2
    with nc.Block() as block:
        @block.sync
        def _(sp):
            def body(i, streams):
                for s in streams:
                    u = 2 * i + s
                    past(sp, er_ready, u - 1)
                    sp.dma_start(EA[s][:, :, :], ea[:, bass.ds(u * TG, TG), :]).then_inc(ea_loaded[s], 16)

            run_units(sp, None, units, body)

        @block.gpsimd
        def _(pool):
            def body(i, streams):
                for s in streams:
                    u = 2 * i + s
                    past(pool, sum_ready, u - 1)
                    alone(pool)
                    pool.tensor_tensor(heads(B[s][:, :, :], H), heads(tiles(xpd, u), H),
                                       per_head(sm.ws, u, D // H), ALU.mult).then_inc(b_ready, 1)
                    pool.wait_ge(run_ready, u + 1)
                    alone(pool)
                    pool.tensor_tensor(heads(A[s][:, :, :], H), heads(RUN[s][:, :, :], H),
                                       per_head(sm.rd, u, D // H), ALU.mult).then_inc(a_ready, 1)

            run_units(pool, None, units, body)

        @block.scalar
        def _(act):
            def body(i, streams):
                for s in streams:
                    u = 2 * i + s
                    act.wait_ge(er_ready, u + 1)
                    act.wait_ge(b_ready, u + 1)
                    alone(act)
                    act.activation(tiles(xpd, u), ER[s][:, :, :], ACT.Copy).then_inc(er_stored, 1)

            run_units(act, None, units, body)
            act.wait_ge(tail_done, 1)
            act.activation(carried0[:, :], PC[0][:, :], ACT.Copy)
            act.activation(carried1[:, :], PC[1][:, :], ACT.Copy)

        @block.tensor
        def _(pe):
            pe.wait_ge(run_ready, units)
            pe.wait_ge(er_ready, units)
            pe.matmul(PC[0][:, :], e.carry[:, :], RUN[odd][:, TG - 1, :], start=True, stop=True)
            pe.matmul(PC[1][:, :], e.carry[:, :], ER[odd][:, TG - 1, :], start=True, stop=True).then_inc(tail_done, 1)

        @block.vector
        def _(dve):
            chain = Chain(dve, step)
            chain.add(dve.memset(RUN[1][:, TG - 1, :], 0.0))
            chain.add(dve.memset(ER[1][:, TG - 1, :], 0.0))

            def body(i, streams):
                for s in streams:
                    u = 2 * i + s
                    alone(dve)
                    chain.add(dve.tensor_copy(CS[s][:, :], tiles(e.cont, u)))
                    alone(dve)
                    n = chain.add(dve.tensor_tensor(heads(M[s][:, :, :], H), heads(tiles(xps, u), H),
                                                    per_head(sm.w, u, D // H), ALU.mult))
                    past(dve, a_ready, u - 1)
                    past(dve, er_stored, u - 1)
                    dve.wait_ge(ea_loaded[s], 16 * (i + 1))
                    for j in range(TG):
                        chain.upto(n)
                        for run, new in ((RUN, M), (ER, EA)):
                            before = run[s][:, j - 1, :] if j else run[1 - s][:, TG - 1, :]
                            ins = dve.scalar_tensor_tensor(out=run[s][:, j, :], in0=before, scalar=CS[s][:, j:j + 1],
                                                           in1=new[s][:, j, :], op0=ALU.mult, op1=ALU.add)
                            if j < TG - 1:
                                n = chain.add(ins)
                            else:
                                ins.then_inc(run_ready if run is RUN else er_ready, 1)
                    dve.wait_ge(run_ready, u + 1)
                    dve.wait_ge(er_ready, u + 1)
                for s in streams:
                    u = 2 * i + s
                    dve.wait_ge(a_ready, u + 1)
                    dve.wait_ge(b_ready, u + 1)
                    alone(dve)
                    dve.tensor_tensor(tiles(xps, u), A[s][:, :, :], B[s][:, :, :], ALU.add).then_inc(sum_ready, 1)

            run_units(dve, chain, units, body)
    ph.end()


def destination_moves(sp, units, dram, tile_in, loaded, load_after, tile_out=None, ready=None, kept=None, lag=0):
    def load(u, s, r):
        if load_after is not None:
            past(sp, load_after, u + 1 - NS)
        if tile_out is tile_in and tile_out is not None:
            past(sp, kept[s], 16 * r)
        sp.dma_start(tile_in[s][:, :, :], tiles(dram, u)).then_inc(loaded[s], 16)

    def keep(u, s, r):
        sp.wait_ge(ready, u + 1)
        sp.dma_start(tiles(dram, u), tile_out[s][:, :, :]).then_inc(kept[s], 16)

    run_slots(sp, None, units, [(load, -1)] + ([(keep, lag)] if ready is not None else []))
    if ready is not None:
        for s in range(NS):
            sp.wait_ge(kept[s], 16 * len(range(s, units, NS)))


def add_carried(dve, chain, out, run, carried, lead, lead_at, u):
    alone(dve)
    n = chain.add(dve.tensor_copy(lead_at[:, :], tiles(lead, u)))
    chain.upto(n)
    for j in range(TG):
        alone(dve)
        last = dve.scalar_tensor_tensor(out=out[:, j, :], in0=carried[:, :], scalar=lead_at[:, j:j + 1],
                                        in1=run[:, bass.ds(u * TG + j, 1), :].rearrange("p a n -> p (a n)"),
                                        op0=ALU.mult, op1=ALU.add)
    return last


def wait_streams(eng, sems, units, each):
    for s, sem in enumerate(sems):
        eng.wait_ge(sem, each * len(range(s, units, len(sems))))


def layers01(nc, w, e, name, out0, agg1, sm, carried0, carried1, table):
    R, units, H = e.R, e.units, w.H0
    ph = Phase(nc, name)
    X, Z0, X1, AG, HN = (ph.sbs(n, [R, TG, D]) for n in ("x", "z0", "x1", "ag", "h"))
    X2 = ph.sbs("x2", [R, TG, D])
    HT, AT = (ph.sbs(n, [P, TG, P]) for n in ("ht", "at"))
    IDX, LEAD = ph.sbs("idx", [R, TG], I32), ph.sbs("lead", [R, TG])
    ST, MV, VE, RS, NM = (ph.sbs(n, [R, TG] + d) for n, d in (
        ("st", [6]), ("mv", [2]), ("ve", []), ("rs", []), ("nm", [])))
    PH, PG = (ph.pbs(n, [P, TG, P]) for n in ("ph", "pg"))
    scattered, loaded, kept = ph.stream_sems("scattered"), ph.stream_sems("loaded"), ph.stream_sems("kept")
    pool_step, dve_step = ph.sem("pool_step"), ph.sem("dve_step")
    (z0a_ready, z0_ready, y0_ready, ag_ready, s0_ready, x1_ready, stats_ready, rstd_ready, shift_ready, h_ready,
     turned, ht_ready, mm1_done, z1_ready, mm1b_done, x2_ready) = (ph.sem(n) for n in (
         "z0a_ready", "z0_ready", "y0_ready", "ag_ready", "s0_ready", "x1_ready", "stats_ready",
         "rstd_ready", "shift_ready", "h_ready", "turned", "ht_ready", "mm1_done", "z1_ready", "mm1b_done",
         "x2_ready"))

    with nc.Block() as block:
        @block.sync
        def _(sp):
            destination_moves(sp, units, e.x, X, loaded, y0_ready, X2, x2_ready, kept, lag=4)

        @block.gpsimd
        def _(pool):
            chain = Chain(pool, pool_step)

            def rstd(u, s, r):
                pool.wait_ge(stats_ready, u + 1)
                layer_rstd(chain, MV[s], VE[s][:, :], RS[s][:, :], w.half[0:R, :]).then_inc(rstd_ready, 1)

            def scatter(u, s, r):
                pool.wait_ge(x2_ready, u + 1)
                past(pool, scattered[s], 16 * TG * r)
                scatter_rows(pool, chain, table, e.row, IDX[s], X2[s], scattered[s], u)

            run_slots(pool, chain, units, [(scatter, 4), (rstd, 1)])
            wait_streams(pool, scattered, units, 16 * TG)

        @block.scalar
        def _(act):
            def s0(u, s, r):
                act.wait_ge(z0_ready, u + 1)
                past(act, scattered[s], 16 * TG * r)
                past(act, kept[s], 16 * r)
                act.activation(X2[s][:, :, :], Z0[s][:, :, :], ACT.Silu).then_inc(s0_ready, 1)

            def norm(u, s, r):
                act.wait_ge(shift_ready, u + 1)
                past(act, turned, u + 1 - NS)
                norm_rows(act, HN[s], X1[s], RS[s], NM[s]).then_inc(h_ready, 1)

            def turn(u, s, r):
                act.wait_ge(turned, u + 1)
                act.activation(HT[s][:, :, 0:R], PH[s][:, :, 0:R], ACT.Copy)
                act.activation(AT[s][:, :, 0:R], PG[s][:, :, 0:R], ACT.Copy).then_inc(ht_ready, 1)

            def z1(u, s, r):
                act.wait_ge(mm1_done, u + 1)
                act.activation(HT[s][:, :, 0:R], PH[s][:, :, 0:R], ACT.Relu, bias=w.b1[:, 0:1]).then_inc(z1_ready, 1)

            run_slots(act, None, units, [(norm, 2), (turn, 2), (s0, 0), (z1, 2)])

        @block.tensor
        def _(pe):
            def turn(u, s, r):
                past(pe, x2_ready, u + 1 - NS)
                pe.wait_ge(ag_ready, u + 1)
                for j in range(TG):
                    pe.transpose(PG[s][:, j, 0:R], AG[s][:, j, :], w.ident[0:R, 0:R])
                pe.wait_ge(h_ready, u + 1)
                for j in range(TG):
                    last = pe.transpose(PH[s][:, j, 0:R], HN[s][:, j, :], w.ident[0:R, 0:R])
                last.then_inc(turned, 1)

            def mm1(u, s, r):
                pe.wait_ge(ht_ready, u + 1)
                pe.matmul(PH[s][:, :, 0:R], w.w1x[:, :], HT[s][:, :, 0:R], start=True, stop=False)
                pe.matmul(PH[s][:, :, 0:R], w.w1e[:, :], AT[s][:, :, 0:R], start=False, stop=True)\
                    .then_inc(mm1_done, 1)

            def mm1b(u, s, r):
                pe.wait_ge(z1_ready, u + 1)
                bias_rows(pe, w, R, PG[s][0:R, :, 0:D], 1)
                for j in range(TG):
                    last = pe.matmul(PG[s][0:R, j, 0:D], HT[s][:, j, 0:R], w.w1b[:, :], start=False, stop=j == TG - 1)
                last.then_inc(mm1b_done, 1)

            run_slots(pe, None, units, [(turn, 2), (mm1b, 3), (mm1, 2)])

        @block.vector
        def _(dve):
            chain = Chain(dve, dve_step)

            def carry(u, s, r):
                past(dve, turned, u + 1 - NS)
                add_carried(dve, chain, AG[s], agg1, carried1, e.lead, LEAD[s], u).then_inc(ag_ready, 1)
                past(dve, s0_ready, u + 1 - NS)
                alone(dve)
                dve.tensor_tensor(heads(Z0[s][:, :, :], H), heads(carried0[:, None, :].to_broadcast([R, TG, D]), H),
                                  per_head(sm.lrd, u, D // H), ALU.mult).then_inc(z0a_ready, 1)

            def z0(u, s, r):
                dve.wait_ge(z0a_ready, u + 1)
                alone(dve)
                n = chain.add(dve.tensor_tensor(Z0[s][:, :, :], tiles(out0, u), Z0[s][:, :, :], ALU.add))
                chain.upto(n)
                dve.tensor_tensor(Z0[s][:, :, :], Z0[s][:, :, :], w.b0[0:R, None, :].to_broadcast([R, TG, D]),
                                  ALU.add).then_inc(z0_ready, 1)

            def y0(u, s, r):
                dve.wait_ge(z0_ready, u + 1)
                dve.wait_ge(loaded[s], 16 * (r + 1))
                past(dve, h_ready, u + 1 - NS)
                dve.scalar_tensor_tensor(out=X1[s][:, :, :], in0=Z0[s][:, :, :], scalar=0.5, in1=X[s][:, :, :],
                                         op0=ALU.mult, op1=ALU.add).then_inc(y0_ready, 1)

            def x1(u, s, r):
                dve.wait_ge(s0_ready, u + 1)
                dve.wait_ge(y0_ready, u + 1)
                dve.scalar_tensor_tensor(out=X1[s][:, :, :], in0=X2[s][:, :, :], scalar=1.2 - 0.5,
                                         in1=X1[s][:, :, :], op0=ALU.mult, op1=ALU.add).then_inc(x1_ready, 1)

            def stats(u, s, r):
                dve.wait_ge(x1_ready, u + 1)
                layer_stats(chain, X1[s], ST[s], MV[s], TG).then_inc(stats_ready, 1)

            def shift(u, s, r):
                dve.wait_ge(rstd_ready, u + 1)
                layer_shift(dve, NM[s], MV[s], RS[s]).then_inc(shift_ready, 1)

            def x2(u, s, r):
                dve.wait_ge(mm1b_done, u + 1)
                dve.tensor_tensor(X2[s][:, :, :], PG[s][0:R, :, 0:D], X1[s][:, :, :], ALU.add).then_inc(x2_ready, 1)

            run_slots(dve, chain, units, [
                (carry, 0), (x1, 1), (stats, 1), (z0, 0), (y0, 0), (x2, 3), (shift, 1)])
    ph.end()


def gather_norm(nc, w, e, name, table, out, carried):
    R, units = e.R, e.units
    ph = Phase(nc, name)
    XG, HN, HR, RUN = (ph.sb2(n, [R, TG, D]) for n in ("xg", "h", "hr", "run"))
    IDX = ph.sb2("idx", [R, TG], I32)
    CS = ph.sb2("cs", [R, TG])
    ST, MV, VE, RS = ph.sb2("st", [R, TG, 6]), ph.sb2("mv", [R, TG, 2]), ph.sb2("ve", [R, TG]), ph.sb2("rs", [R, TG])
    PC = ph.ctx.enter_context(nc.psum_tensor(f"{name}_pc", [R, D], F32))
    gathered = ph.sem2("gathered")
    pool_step, dve_step, stats_ready, rstd_ready, h_ready, hr_ready, run_ready, stored, tail_done = (
        ph.sem(n) for n in ("pool_step", "dve_step", "stats_ready", "rstd_ready", "h_ready", "hr_ready", "run_ready",
                            "stored", "tail_done"))
    with nc.Block() as block:
        @block.gpsimd
        def _(pool):
            chain = Chain(pool, pool_step)

            def gather(i, s):
                gather_rows(pool, chain, table, e.src, IDX[s], XG[s], gathered[s], 2 * i + s)

            gather(0, 0)
            gather(0, 1)

            def body(i, streams):
                for s in streams:
                    pool.wait_ge(stats_ready, 2 * i + s + 1)
                    layer_rstd(chain, MV[s], VE[s][:, :], RS[s][:, :], w.half[0:R, :]).then_inc(rstd_ready, 1)
                for s in streams:
                    if not (isinstance(i, int) and 2 * (i + 1) + s >= units):
                        pool.wait_ge(h_ready, 2 * i + s + 1)
                        gather(i + 1, s)

            run_units(pool, chain, units, body)

        @block.scalar
        def _(act):
            def body(i, streams):
                for s in streams:
                    act.wait_ge(h_ready, 2 * i + s + 1)
                    past(act, run_ready, 2 * i + s - 1)
                    act.activation(HR[s][:, :, :], HN[s][:, :, :], ACT.Relu).then_inc(hr_ready, 1)
                for s in streams:
                    act.wait_ge(run_ready, 2 * i + s + 1)
                    alone(act)
                    act.activation(tiles(out, 2 * i + s), RUN[s][:, :, :], ACT.Copy).then_inc(stored, 1)

            run_units(act, None, units, body)
            act.wait_ge(tail_done, 1)
            act.activation(carried[:, :], PC[:, :], ACT.Copy)

        @block.tensor
        def _(pe):
            pe.wait_ge(run_ready, units)
            pe.matmul(PC[:, :], e.carry[:, :], RUN[(units - 1) % 2][:, TG - 1, :], start=True, stop=True)\
                .then_inc(tail_done, 1)

        @block.vector
        def _(dve):
            chain = Chain(dve, dve_step)
            chain.add(dve.memset(RUN[1][:, TG - 1, :], 0.0))

            def body(i, streams):
                for s in streams:
                    dve.wait_ge(gathered[s], 16 * TG * (i + 1))
                    alone(dve)
                    layer_stats(chain, XG[s], ST[s], MV[s], TG).then_inc(stats_ready, 1)
                for s in streams:
                    u = 2 * i + s
                    dve.wait_ge(rstd_ready, u + 1)
                    past(dve, hr_ready, u - 1)
                    layer_norm(chain, XG[s], MV[s], RS[s], HN[s], TG).then_inc(h_ready, 1)
                for s in streams:
                    u = 2 * i + s
                    alone(dve)
                    n = chain.add(dve.tensor_copy(CS[s][:, :], tiles(e.cont, u)))
                    dve.wait_ge(hr_ready, u + 1)
                    past(dve, stored, u - 1)
                    for j in range(TG):
                        chain.upto(n)
                        before = RUN[s][:, j - 1, :] if j else RUN[1 - s][:, TG - 1, :]
                        ins = dve.scalar_tensor_tensor(out=RUN[s][:, j, :], in0=before, scalar=CS[s][:, j:j + 1],
                                                       in1=HR[s][:, j, :], op0=ALU.mult, op1=ALU.add)
                        if j < TG - 1:
                            n = chain.add(ins)
                    ins.then_inc(run_ready, 1)
                    dve.wait_ge(run_ready, u + 1)

            run_units(dve, chain, units, body)
    ph.end()


def layer2(nc, w, e, name, run, carried, table):
    R, units = e.R, e.units
    ph = Phase(nc, name)
    X, HN, T, X3 = (ph.sbs(n, [R, TG, D]) for n in ("x", "h", "t", "x3"))
    HT = ph.sbs("ht", [P, TG, P])
    IDX, LEAD = ph.sbs("idx", [R, TG], I32), ph.sbs("lead", [R, TG])
    ST, MV, VE, RS, NM = (ph.sbs(n, [R, TG] + d) for n, d in (
        ("st", [6]), ("mv", [2]), ("ve", []), ("rs", []), ("nm", [])))
    PT, PB = (ph.pbs(n, [P, TG, P]) for n in ("pt", "pb"))
    scattered, loaded, kept = ph.stream_sems("scattered"), ph.stream_sems("loaded"), ph.stream_sems("kept")
    (pool_step, dve_step, carried_in, sum_ready, t_ready, z2_ready, l_ready, x3_ready, stats_ready,
     rstd_ready, shift_ready, h_ready, turned, ht_ready, mm_done) = (ph.sem(n) for n in (
         "pool_step", "dve_step", "carried_in", "sum_ready", "t_ready", "z2_ready", "l_ready", "x3_ready",
         "stats_ready", "rstd_ready", "shift_ready", "h_ready", "turned", "ht_ready", "mm_done"))
    with nc.Block() as block:
        @block.sync
        def _(sp):
            destination_moves(sp, units, e.x, X, loaded, x3_ready, X3, x3_ready, kept, lag=3)

        @block.gpsimd
        def _(pool):
            chain = Chain(pool, pool_step)

            def rstd(u, s, r):
                pool.wait_ge(stats_ready, u + 1)
                layer_rstd(chain, MV[s], VE[s][:, :], RS[s][:, :], w.half[0:R, :]).then_inc(rstd_ready, 1)

            def scatter(u, s, r):
                pool.wait_ge(x3_ready, u + 1)
                past(pool, scattered[s], 16 * TG * r)
                scatter_rows(pool, chain, table, e.row, IDX[s], X3[s], scattered[s], u)

            run_slots(pool, chain, units, [(rstd, 0), (scatter, 3)])
            wait_streams(pool, scattered, units, 16 * TG)

        @block.scalar
        def _(act):
            def norm(u, s, r):
                act.wait_ge(shift_ready, u + 1)
                past(act, t_ready, u + 1 - NS)
                norm_rows(act, HN[s], X[s], RS[s], NM[s]).then_inc(h_ready, 1)

            def turn(u, s, r):
                act.wait_ge(turned, u + 1)
                act.activation(HT[s][:, :, 0:R], PT[s][:, :, 0:R], ACT.Copy).then_inc(ht_ready, 1)

            def z2(u, s, r):
                act.wait_ge(mm_done, u + 1)
                past(act, scattered[s], 16 * TG * r)
                past(act, kept[s], 16 * r)
                act.activation(X3[s][:, :, :], PB[s][0:R, :, 0:D], ACT.Copy).then_inc(z2_ready, 1)

            run_slots(act, None, units, [(turn, 1), (z2, 2), (norm, 0)])

        @block.tensor
        def _(pe):
            def turn(u, s, r):
                pe.wait_ge(t_ready, u + 1)
                past(pe, ht_ready, u + 1 - NS)
                for j in range(TG):
                    last = pe.transpose(PT[s][:, j, 0:R], T[s][:, j, :], w.ident[0:R, 0:R])
                last.then_inc(turned, 1)

            def mm(u, s, r):
                pe.wait_ge(ht_ready, u + 1)
                past(pe, z2_ready, u + 1 - NS)
                bias_rows(pe, w, R, PB[s][0:R, :, 0:D], 2)
                for j in range(TG):
                    last = pe.matmul(PB[s][0:R, j, 0:D], HT[s][:, j, 0:R], w.w2[:, :], start=False, stop=j == TG - 1)
                last.then_inc(mm_done, 1)

            run_slots(pe, None, units, [(turn, 1), (mm, 1)])

        @block.vector
        def _(dve):
            chain = Chain(dve, dve_step)

            def stats(u, s, r):
                dve.wait_ge(loaded[s], 16 * (r + 1))
                layer_stats(chain, X[s], ST[s], MV[s], TG).then_inc(stats_ready, 1)

            def carry(u, s, r):
                past(dve, turned, u + 1 - NS)
                add_carried(dve, chain, T[s], run, carried, e.lead, LEAD[s], u).then_inc(carried_in, 1)

            def shift(u, s, r):
                dve.wait_ge(rstd_ready, u + 1)
                layer_shift(dve, NM[s], MV[s], RS[s]).then_inc(shift_ready, 1)

            def mean(u, s, r):
                dve.wait_ge(h_ready, u + 1)
                dve.wait_ge(carried_in, u + 1)
                dve.tensor_tensor(T[s][:, :, :], HN[s][:, :, :], T[s][:, :, :], ALU.add).then_inc(sum_ready, 1)
                dve.wait_ge(sum_ready, u + 1)
                alone(dve)
                dve.tensor_tensor(T[s][:, :, :], T[s][:, :, :],
                                  tiles(e.rcount, u)[:, :, None].to_broadcast([R, TG, D]), ALU.mult)\
                    .then_inc(t_ready, 1)

            def leaky(u, s, r):
                dve.wait_ge(z2_ready, u + 1)
                leaky_relu(dve, X3[s][:, :, :], X3[s][:, :, :]).then_inc(l_ready, 1)

            def x3(u, s, r):
                dve.wait_ge(l_ready, u + 1)
                dve.tensor_tensor(X3[s][:, :, :], X[s][:, :, :], X3[s][:, :, :], ALU.add).then_inc(x3_ready, 1)

            run_slots(dve, chain, units, [(stats, 0), (mean, 1), (carry, 0), (shift, 0), (leaky, 2), (x3, 2)])
    ph.end()


def layer3_first(nc, w, e, name, run, own, sm, carried, table):
    R, units, H, C3 = e.R, e.units, w.H3, w.C3
    W3 = C3 * P
    ph = Phase(nc, name)
    X, HN = (ph.sbs(n, [R, TG, D]) for n in ("x", "h"))
    V, SELF = (ph.sbs(n, [R, TG, W3]) for n in ("v", "self"))
    G = ph.sbs("g", [R, TG, D + 2])
    VT = ph.sbs("vt", [P, C3, TG, P])
    HT = [vt[:, 0] for vt in VT]
    IDX, LEAD = ph.sbs("idx", [R, TG], I32), ph.sbs("lead", [R, TG])
    ST, MV, VE, RS, NM = (ph.sbs(n, [R, TG] + d) for n, d in (
        ("st", [6]), ("mv", [2]), ("ve", []), ("rs", []), ("nm", [])))
    PA = ph.pbs("pa", [P, TG, W3])
    scattered, loaded, kept = ph.stream_sems("scattered"), ph.stream_sems("loaded"), ph.stream_sems("kept")
    (pool_step, dve_step, xh_ready, stats_ready, rstd_ready, shift_ready, h_ready, turned, ht_ready, mm_done,
     self_ready, v_carried, v_ready, v_turned, vt_ready, c_ready, mm4_done, g_ready, g_kept) = (ph.sem(n) for n in (
         "pool_step", "dve_step", "xh_ready", "stats_ready", "rstd_ready", "shift_ready", "h_ready", "turned",
         "ht_ready", "mm_done", "self_ready", "v_carried", "v_ready", "v_turned", "vt_ready", "c_ready",
         "mm4_done", "g_ready", "g_kept"))

    def halves(pa):
        return pa[:, :, :].rearrange("p t n -> p (t n)").rearrange("p (c t n) -> p c t n", c=C3, t=TG)

    with nc.Block() as block:
        @block.sync
        def _(sp):
            destination_moves(sp, units, e.x, X, loaded, None, X, xh_ready, kept, lag=1)

        @block.gpsimd
        def _(pool):
            chain = Chain(pool, pool_step)

            def rstd(u, s, r):
                pool.wait_ge(stats_ready, u + 1)
                layer_rstd(chain, MV[s], VE[s][:, :], RS[s][:, :], w.half[0:R, :]).then_inc(rstd_ready, 1)

            def xh(u, s, r):
                pool.wait_ge(h_ready, u + 1)
                pool.tensor_tensor(X[s][:, :, :], HN[s][:, :, :], X[s][:, :, :], ALU.add).then_inc(xh_ready, 1)

            def scatter(u, s, r):
                pool.wait_ge(g_ready, u + 1)
                past(pool, scattered[s], 16 * TG * r)
                scatter_rows(pool, chain, table, e.row, IDX[s], G[s], scattered[s], u)

            run_slots(pool, chain, units, [(rstd, 0), (xh, 1), (scatter, 4)])
            wait_streams(pool, scattered, units, 16 * TG)

        @block.scalar
        def _(act):
            def norm(u, s, r):
                act.wait_ge(shift_ready, u + 1)
                past(act, turned, u + 1 - NS)
                past(act, xh_ready, u + 1 - NS)
                norm_rows(act, HN[s], X[s], RS[s], NM[s]).then_inc(h_ready, 1)

            def turn(u, s, r):
                act.wait_ge(turned, u + 1)
                act.activation(HT[s][:, :, 0:R], halves(PA[s])[:, 0, :, 0:R], ACT.Copy).then_inc(ht_ready, 1)

            def turn_v(u, s, r):
                act.wait_ge(v_turned, u + 1)
                for c in range(C3):
                    last = act.activation(VT[s][:, c, :, 0:R], halves(PA[s])[:, c, :, 0:R], ACT.Identity,
                                          bias=w.b3[:, c:c + 1])
                last.then_inc(vt_ready, 1)

            def g(u, s, r):
                act.wait_ge(mm4_done, u + 1)
                past(act, scattered[s], 16 * TG * r)
                act.activation(G[s][:, :, :], PA[s][0:R, :, 0:D + 2], ACT.Copy).then_inc(g_ready, 1)
                act.wait_ge(g_ready, u + 1)
                alone(act)
                act.activation(tiles(own, u), G[s][:, :, :], ACT.Copy).then_inc(g_kept, 1)

            run_slots(act, None, units, [(turn, 1), (turn_v, 3), (g, 4), (norm, 0)])

        @block.tensor
        def _(pe):
            def turn(u, s, r):
                pe.wait_ge(h_ready, u + 1)
                past(pe, g_ready, u + 1 - NS)
                for j in range(TG):
                    last = pe.transpose(halves(PA[s])[:, 0, j, 0:R], HN[s][:, j, :], w.ident[0:R, 0:R])
                last.then_inc(turned, 1)

            def mm3(u, s, r):
                pe.wait_ge(ht_ready, u + 1)
                for j in range(TG):
                    last = pe.matmul(PA[s][0:R, j, :], HT[s][:, j, 0:R], w.w3[:, 0:W3], start=True, stop=True)
                last.then_inc(mm_done, 1)

            def turn_v(u, s, r):
                pe.wait_ge(v_ready, u + 1)
                pe.wait_ge(self_ready, u + 1)
                for c in range(C3):
                    for j in range(TG):
                        cols = slice(c * P, (c + 1) * P)
                        pe.matmul(halves(PA[s])[:, c, j, 0:R], V[s][:, j, cols], w.ident[0:R, 0:R],
                                  start=True, stop=False)
                        last = pe.matmul(halves(PA[s])[:, c, j, 0:R], SELF[s][:, j, cols], w.ident[0:R, 0:R],
                                         start=False, stop=True)
                last.then_inc(v_turned, 1)

            def mm4(u, s, r):
                pe.wait_ge(c_ready, u + 1)
                for j in range(TG):
                    for c in range(C3):
                        last = pe.matmul(PA[s][0:R, j, 0:D + 2], VT[s][:, c, j, 0:R], w.w4[:, c, :],
                                         start=(c == 0), stop=(c == C3 - 1))
                last.then_inc(mm4_done, 1)

            run_slots(pe, None, units, [(turn, 1), (mm4, 4), (mm3, 1), (turn_v, 2)])

        @block.vector
        def _(dve):
            chain = Chain(dve, dve_step)

            def stats(u, s, r):
                dve.wait_ge(loaded[s], 16 * (r + 1))
                layer_stats(chain, X[s], ST[s], MV[s], TG).then_inc(stats_ready, 1)

            def shift(u, s, r):
                dve.wait_ge(rstd_ready, u + 1)
                layer_shift(dve, NM[s], MV[s], RS[s]).then_inc(shift_ready, 1)

            def edge_part(u, s, r):
                past(dve, v_turned, u + 1 - NS)
                add_carried(dve, chain, V[s], run, carried, e.lead, LEAD[s], u).then_inc(v_carried, 1)
                dve.wait_ge(v_carried, u + 1)
                alone(dve)
                dve.tensor_tensor(heads(V[s][:, :, :], H), heads(V[s][:, :, :], H),
                                  per_head(sm.rd, u, W3 // H), ALU.mult).then_inc(v_ready, 1)

            def own_part(u, s, r):
                dve.wait_ge(mm_done, u + 1)
                alone(dve)
                dve.tensor_tensor(heads(SELF[s][:, :, :], H), heads(PA[s][0:R, :, :], H),
                                  per_head(sm.ws, u, W3 // H), ALU.mult).then_inc(self_ready, 1)

            def leaky(u, s, r):
                dve.wait_ge(vt_ready, u + 1)
                leaky_relu(dve, VT[s][:, :, :, 0:R].rearrange("p c t n -> p (c t) n"),
                           VT[s][:, :, :, 0:R].rearrange("p c t n -> p (c t) n")).then_inc(c_ready, 1)

            run_slots(dve, chain, units, [(stats, 0), (edge_part, 0), (shift, 0), (own_part, 1), (leaky, 3)])
    ph.end()


def gather_last(nc, w, e, name, table, out):
    R, units = e.R, e.units
    ph = Phase(nc, name)
    XG = ph.sb2("xg", [R, TG, D + 2])
    IDX = ph.sb2("idx", [R, TG], I32)
    gathered = ph.sem2("gathered")
    pool_step, stored = ph.sem("pool_step"), ph.sem("stored")
    with nc.Block() as block:
        @block.gpsimd
        def _(pool):
            chain = Chain(pool, pool_step)

            def body(i, streams):
                for s in streams:
                    u = 2 * i + s
                    past(pool, stored, u - 1)
                    gather_rows(pool, chain, table, e.src, IDX[s], XG[s], gathered[s], u)

            run_units(pool, chain, units, body)

        @block.scalar
        def _(act):
            def body(i, streams):
                for s in streams:
                    act.wait_ge(gathered[s], 16 * TG * (i + 1))
                    alone(act)
                    act.activation(tiles(out, 2 * i + s), XG[s][:, :, :], ACT.Copy).then_inc(stored, 1)

            run_units(act, None, units, body)
    ph.end()


def layer3_second(nc, w, e, name, run, own, sm, carried, out_dram):
    R, units = e.R, e.units
    ph = Phase(nc, name)
    X, V, SELF, Y, OUT = (ph.sbs(n, [R, TG, D]) for n in ("x", "v", "self", "y", "out"))
    IDX, LEAD = ph.sbs("idx", [R, TG], I32), ph.sbs("lead", [R, TG])
    scattered, loaded = ph.stream_sems("scattered"), ph.stream_sems("loaded")
    pool_step, dve_step, carried_in, v_ready, self_ready, y_ready, l_ready, out_ready = (
        ph.sem(n) for n in ("pool_step", "dve_step", "carried_in", "v_ready", "self_ready", "y_ready", "l_ready",
                            "out_ready"))
    with nc.Block() as block:
        @block.sync
        def _(sp):
            destination_moves(sp, units, e.x, X, loaded, out_ready)

        @block.gpsimd
        def _(pool):
            chain = Chain(pool, pool_step)

            def scatter(u, s, r):
                pool.wait_ge(out_ready, u + 1)
                past(pool, scattered[s], 16 * TG * r)
                scatter_rows(pool, chain, out_dram, e.row, IDX[s], OUT[s], scattered[s], u)

            run_slots(pool, chain, units, [(scatter, 2)])
            wait_streams(pool, scattered, units, 16 * TG)

        @block.vector
        def _(dve):
            chain = Chain(dve, dve_step)

            def edge_part(u, s, r):
                add_carried(dve, chain, V[s], run, carried, e.lead, LEAD[s], u).then_inc(carried_in, 1)
                dve.wait_ge(carried_in, u + 1)
                alone(dve)
                dve.tensor_tensor(V[s][:, :, :], V[s][:, :, :], per_head(sm.rd, u, D)[:, :, 0, :], ALU.mult)\
                    .then_inc(v_ready, 1)

            def own_part(u, s, r):
                alone(dve)
                dve.tensor_tensor(SELF[s][:, :, :], tiles(own, u)[:, :, 0:D],
                                  per_head(sm.ws, u, D)[:, :, 0, :], ALU.mult).then_inc(self_ready, 1)

            def both(u, s, r):
                dve.wait_ge(v_ready, u + 1)
                dve.wait_ge(self_ready, u + 1)
                n = chain.add(dve.tensor_tensor(Y[s][:, :, :], V[s][:, :, :], SELF[s][:, :, :], ALU.add))
                chain.upto(n)
                dve.tensor_tensor(Y[s][:, :, :], Y[s][:, :, :], w.b4[0:R, None, :].to_broadcast([R, TG, D]),
                                  ALU.add).then_inc(y_ready, 1)

            def leaky(u, s, r):
                dve.wait_ge(y_ready, u + 1)
                leaky_relu(dve, V[s][:, :, :], Y[s][:, :, :]).then_inc(l_ready, 1)

            def final(u, s, r):
                dve.wait_ge(l_ready, u + 1)
                dve.wait_ge(loaded[s], 16 * (r + 1))
                past(dve, scattered[s], 16 * TG * r)
                dve.tensor_tensor(OUT[s][:, :, :], X[s][:, :, :], V[s][:, :, :], ALU.add).then_inc(out_ready, 1)

            run_slots(dve, chain, units, [(edge_part, 0), (own_part, 0), (leaky, 1), (both, 0), (final, 1)])
    ph.end()


class Weights:

    def __init__(self, nc, ctx, name, e, H):
        self.w, self.ws, self.rd, self.lrd = (
            ctx.enter_context(nc.sbuf_tensor(f"{name}_{n}", [e.R, H, e.T], F32)) for n in ("w", "ws", "rd", "lrd"))


def sparse_pass(nc, ctx, w, a, tables, out_dram):
    t2, t3, t4 = tables
    e = load_edges(nc, ctx, w, a)
    R, T = e.R, e.T
    e.x = nc.dram_tensor("dst_rows", (R, T, D), F32).ap()
    H0, H3, W3 = w.H0, w.H3, w.C3 * P
    ns = D + H0
    big = ctx.enter_context(nc.sbuf_tensor("big", [R, T, max(ns + D + 2 * H0, W3 + H3, 2 * (D + 2))], F32))
    al = ctx.enter_context(nc.sbuf_tensor("al", [R, T, 2 * H3], F32))
    c0 = ctx.enter_context(nc.sbuf_tensor("c0", [R, D], F32))
    c1 = ctx.enter_context(nc.sbuf_tensor("c1", [R, D], F32))
    c3 = ctx.enter_context(nc.sbuf_tensor("c3", [R, W3], F32))
    sm4 = Weights(nc, ctx, "sm4", e, max(H0, H3))
    sm1 = sm4_as(sm4, 1)

    src0, dst0 = big[:, :, 0:ns], big[:, :, ns:ns + D + 2 * H0]
    project_ends(nc, w, e, "p0", a["x"], True, (w.w0[:, 0:ns], w.w0[:, :]), (src0, dst0), 2)
    edge_softmax(nc, w, e, "q0", H0, src0[:, :, D:D + H0], dst0[:, :, D:D + H0], dst0[:, :, D + H0:D + 2 * H0],
                 1e-16, sm4, False)
    sum_layer0(nc, w, e, "s0", src0[:, :, 0:D], dst0[:, :, 0:D], a["edge_attr_128"], sm4, c0, c1)
    layers01(nc, w, e, "l01", src0[:, :, 0:D], dst0[:, :, 0:D], sm4, c0, c1, t2)
    gather_norm(nc, w, e, "g2", t2, big[:, :, 0:D], c0)
    layer2(nc, w, e, "l2", big[:, :, 0:D], c0, t3)
    src3 = big[:, :, 0:W3 + H3]
    project_ends(nc, w, e, "p3", t3, False, (w.w3[:, 0:W3 + H3], w.w3[:, W3:W3 + 2 * H3]),
                 (src3, al[:, :, :]), 3)
    edge_softmax(nc, w, e, "q3", H3, src3[:, :, W3:W3 + H3], al[:, :, 0:H3], al[:, :, H3:2 * H3], 0.0, sm4, True)
    sum_runs(nc, w, e, "s3", src3[:, :, 0:W3], H3, sm4, c3)
    own = big[:, :, 0:D + 2]
    layer3_first(nc, w, e, "l3", src3[:, :, 0:W3], own, sm4, c3, t4)
    src4 = big[:, :, D + 2:2 * (D + 2)]
    gather_last(nc, w, e, "g4", t4, src4)
    edge_softmax(nc, w, e, "q4", 1, src4[:, :, D:D + 1], own[:, :, D:D + 1], own[:, :, D + 1:D + 2], 0.0, sm1, True)
    sum_runs(nc, w, e, "s4", src4[:, :, 0:D], 1, sm1, c0)
    layer3_second(nc, w, e, "l4", src4[:, :, 0:D], own, sm1, c0, out_dram)


class sm4_as:

    def __init__(self, sm, H):
        self.w, self.ws, self.rd, self.lrd = (t[:, 0:H, :] for t in (sm.w, sm.ws, sm.rd, sm.lrd))


def gnn_kernel(nc, a, out):
    N = a["x"].shape[0]
    with ExitStack() as ctx:
        t2 = nc.dram_tensor("t2", (N, D), F32).ap()
        t3 = nc.dram_tensor("t3", (N, D), F32).ap()
        t4 = nc.dram_tensor("t4", (N, D + 2), F32).ap()
        w = load_weights(nc, ctx, a)
        dense_pass(nc, w, a["x"], (t2, t3, t4), out)
        sparse_pass(nc, ctx, w, a, (t2, t3, t4), out)


_INS = ['x', 'src', 'dst', 'edge_attr_128', 'L0_gnn_W', 'L0_gnn_att_src', 'L0_gnn_att_dst', 'L0_gnn_bias',
        'L1_gnn_W1', 'L1_gnn_b1', 'L1_gnn_W2', 'L1_gnn_b2', 'L2_gnn_W', 'L2_gnn_b', 'L3_gnn_W1',
        'L3_gnn_att_src1', 'L3_gnn_att_dst1', 'L3_gnn_bias1', 'L3_gnn_W2', 'L3_gnn_att_src2',
        'L3_gnn_att_dst2', 'L3_gnn_bias2']


def kernel(**inputs):
    import numpy as _np
    import concourse.bacc as _bacc
    from concourse import mybir as _mybir
    from concourse.bass_utils import run_bass_kernel_spmd as _run

    nc = _bacc.Bacc("TRN2", target_bir_lowering=False, num_devices=1)
    arrays, args = {}, {}
    for name in _INS:
        a = _np.ascontiguousarray(inputs[name])
        arrays[f"in_{name}_dram"] = a
        args[name] = nc.dram_tensor(f"in_{name}_dram", a.shape, _mybir.dt.from_np(a.dtype), kind="ExternalInput").ap()
    out = nc.dram_tensor("out_0_dram", inputs["x"].shape, _mybir.dt.float32, kind="ExternalOutput").ap()
    gnn_kernel(nc, args, out)
    r = _run(nc, [arrays], core_ids=[0])
    return r.results[0]["out_0_dram"]
```

```python
from contextlib import ExitStack

import concourse.bass as bass
from concourse import mybir

F32 = mybir.dt.float32
I32 = mybir.dt.int32
BF16 = mybir.dt.bfloat16
ALU = mybir.AluOpType
ACT = mybir.ActivationFunctionType
AX = mybir.AxisListType.X

P = 128
D = 128
TG = 4
NS = 4
GROUP = P * TG
EPS = 1e-5
SLOPE = 0.2
BIG = 1e30


def past(eng, sem, value):
    if isinstance(value, int) and value <= 0:
        return
    eng.wait_ge(sem, value)


class Chain:

    def __init__(self, eng, sem):
        self.eng, self.sem, self.base, self.n = eng, sem, 0, 0

    def add(self, ins):
        ins.then_inc(self.sem, 1)
        self.n += 1
        return self.n

    def upto(self, n):
        self.eng.wait_ge(self.sem, self.base + n)


def alone(eng):
    eng.nop(nofuse=True)


def run_slots(eng, chain, units, order):
    lags = [lag for _, lag in order]
    chain = chain or Chain(eng, None)

    def slot(i, c):
        for stage, lag in order:
            u, r = NS * i + (c - lag), i + (c - lag) // NS
            if not (isinstance(u, int) and not 0 <= u < units):
                stage(u, (c - lag) % NS, r)

    peeled = 1 - (-max(lags) // NS) if max(lags) > 0 else 1
    assert units // NS > peeled and min(lags) >= -(units % NS)
    for n in range(min(lags), NS * peeled):
        before = chain.n
        slot(n // NS, n % NS)
    per_body = NS * (chain.n - before)
    ahead = chain.n
    with eng.Fori(peeled, units // NS) as i:
        chain.base, chain.n = ahead + (i - peeled) * per_body, 0
        for c in range(NS):
            slot(i, c)
        assert chain.n == per_body
    chain.base, chain.n = ahead + (units // NS - peeled) * per_body, 0
    for n in range(units // NS * NS, units + max(lags)):
        slot(n // NS, n % NS)


def layer_stats(chain, x, stats, mv, tiles):
    for j in range(tiles):
        last = chain.add(chain.eng.bn_stats(stats[:, j, :], x[:, j, :]))
    chain.upto(last)
    alone(chain.eng)
    for j in range(tiles):
        last = chain.eng.bn_aggr(mv[:, j, :], stats[:, j, :])
    return last


def layer_rstd(chain, mv, ve, rs, half):
    alone(chain.eng)
    n = chain.add(chain.eng.tensor_scalar(ve, mv[:, :, 1], EPS, None, ALU.add))
    chain.upto(n)
    return chain.eng.tensor_tensor(rs, ve, half[:, 0:ve.shape[1]], ALU.pow)


def layer_norm(chain, x, mv, rs, h, tiles):
    for j in range(tiles):
        last = chain.eng.tensor_scalar(h[:, j, :], x[:, j, :], mv[:, j, 0:1], rs[:, j:j + 1],
                                       ALU.subtract, ALU.mult)
    return last


def layer_shift(eng, nm, mv, rs):
    return eng.scalar_tensor_tensor(out=nm[:, :], in0=mv[:, :, 0], scalar=-1.0, in1=rs[:, :],
                                    op0=ALU.mult, op1=ALU.mult)


def norm_rows(act, out, x, rs, nm):
    for j in range(TG):
        last = act.activation(out[:, j, :], x[:, j, :], ACT.Relu, bias=nm[:, j:j + 1], scale=rs[:, j:j + 1])
    return last


def leaky_relu(dve, out, z):
    return dve.scalar_tensor_tensor(out=out, in0=z, scalar=SLOPE, in1=z, op0=ALU.mult, op1=ALU.max)


def bias_rows(pe, w, R, out, k):
    pe.matmul(out, w.ones[:, 0:R], w.bias_parts[:, k, None, :].to_broadcast([3, TG, D]), start=True, stop=False)


class Net:
    pass


def load_weights(nc, ctx, a):
    w = Net()

    def sb(name, shape, dt=F32):
        return ctx.enter_context(nc.sbuf_tensor(name, shape, dt))

    H0 = a["L0_gnn_att_src"].shape[0]
    H3 = a["L3_gnn_att_src1"].shape[0]
    C3 = a["L3_gnn_W1"].shape[1] // P
    w.H0, w.H3, w.C3 = H0, H3, C3
    w.w0 = sb("w0", [P, D + 2 * H0])
    w.w1x = sb("w1x", [P, D])
    w.w1e = sb("w1e", [P, D])
    w.w1b = sb("w1b", [P, D])
    w.w2 = sb("w2", [P, D])
    w.w2raw = sb("w2raw", [P, D])
    w.w3 = sb("w3", [P, C3 * P + 2 * H3])
    w.w4 = sb("w4", [P, C3, D + 2])
    w.b0 = sb("b0", [P, D])
    w.b1 = sb("b1", [P, 1])
    w.b1b = sb("b1b", [P, D])
    w.b2 = sb("b2", [P, D])
    w.b3 = sb("b3", [P, C3])
    w.b3row = sb("b3row", [P, C3 * P])
    w.b4 = sb("b4", [P, D])
    w.ident = sb("ident", [P, P])
    w.ones = sb("ones", [3, P], BF16)
    w.bias_parts = sb("bias_parts", [3, 3, D], BF16)
    w.half = sb("half", [P, 2 * TG])
    with ExitStack() as tmp:
        att = [tmp.enter_context(nc.sbuf_tensor(f"att{k}", [P, n], F32))
               for k, n in enumerate((D, D, C3 * P, C3 * P, D, D))]
        prod = tmp.enter_context(nc.sbuf_tensor("prod", [P, 8, C3 * P], F32))
        w2t = tmp.enter_context(nc.psum_tensor("w2t", [P, D], F32))
        part = [tmp.enter_context(nc.sbuf_tensor(f"part{k}", [3, 3, D], BF16)) for k in range(3)]
        partf = [tmp.enter_context(nc.sbuf_tensor(f"partf{k}", [3, 3, D], F32)) for k in range(3)]
        rest = tmp.enter_context(nc.sbuf_tensor("rest", [3, 3, D], F32))
        parts_sum = tmp.enter_context(nc.sbuf_tensor("parts_sum", [3, 3, D], F32))
        part_step = tmp.enter_context(nc.semaphore("part_step"))
        loaded = tmp.enter_context(nc.semaphore("weights_loaded"))
        ident_step = tmp.enter_context(nc.semaphore("ident_step"))
        prod_ready = tmp.enter_context(nc.semaphore("prod_ready"))
        w2_turned = tmp.enter_context(nc.semaphore("w2_turned"))
        block = tmp.enter_context(nc.Block())

        def rows(ap):
            return ap.rearrange("(a n) -> a n", a=1).to_broadcast([P, ap.shape[0]])

        loads = [
            (w.w0[:, 0:D], a["L0_gnn_W"]), (w.w1x[:, :], a["L1_gnn_W1"][0:D, :]),
            (w.w1e[:, :], a["L1_gnn_W1"][D:2 * D, :]), (w.w1b[:, :], a["L1_gnn_W2"]),
            (w.w2raw[:, :], a["L2_gnn_W"]), (w.w3[:, 0:C3 * P], a["L3_gnn_W1"]),
            (w.w4[:, :, 0:D], a["L3_gnn_W2"].rearrange("(c p) n -> p c n", p=P)),
            (w.b0[:, :], rows(a["L0_gnn_bias"])), (w.b1[:, :], a["L1_gnn_b1"].rearrange("(p a) -> p a", a=1)),
            (w.b1b[:, :], rows(a["L1_gnn_b2"])), (w.b2[:, :], rows(a["L2_gnn_b"])),
            (w.b3row[:, :], rows(a["L3_gnn_bias1"])), (w.b4[:, :], rows(a["L3_gnn_bias2"])),
        ] + [(w.b3[:, c:c + 1], a["L3_gnn_bias1"][c * P:(c + 1) * P].rearrange("(p a) -> p a", a=1))
             for c in range(C3)] + [
            (t[:, :], rows(a[n].rearrange("h d -> (h d)"))) for t, n in zip(att, (
                "L0_gnn_att_src", "L0_gnn_att_dst", "L3_gnn_att_src1", "L3_gnn_att_dst1",
                "L3_gnn_att_src2", "L3_gnn_att_dst2"))]

        @block.sync
        def _(sp):
            for dst, src in loads:
                sp.dma_start(dst, src).then_inc(loaded, 16)

        @block.gpsimd
        def _(pool):
            pool.memset(w.half[:, :], -0.5)
            pool.memset(w.ones[:, :], 1.0)
            pool.memset(w.ident[:, :], 0.0).then_inc(ident_step, 1)
            pool.wait_ge(ident_step, 1)
            pool.affine_select(out=w.ident[:, :], in_=w.ident[:, :], compare_op=ALU.not_equal, fill=1.0,
                               base=0, pattern=[[-1, P]], channel_multiplier=1).then_inc(ident_step, 1)

        @block.tensor
        def _(pe):
            pe.wait_ge(ident_step, 2)
            pe.wait_ge(loaded, 16 * len(loads))
            pe.transpose(w2t[:, :], w.w2raw[:, :], w.ident[:, :]).then_inc(w2_turned, 1)

        @block.vector
        def _(dve):
            dve.wait_ge(loaded, 16 * len(loads))
            folds = [(w.w0[:, 0:D], att[0][:, :], H0, w.w0[:, D:D + H0]),
                     (w.w0[:, 0:D], att[1][:, :], H0, w.w0[:, D + H0:D + 2 * H0]),
                     (w.w3[:, 0:C3 * P], att[2][:, :], H3, w.w3[:, C3 * P:C3 * P + H3]),
                     (w.w3[:, 0:C3 * P], att[3][:, :], H3, w.w3[:, C3 * P + H3:C3 * P + 2 * H3])]
            for c in range(C3):
                folds.append((w.w4[:, c, 0:D], att[4][:, :], 1, w.w4[:, c, D:D + 1]))
                folds.append((w.w4[:, c, 0:D], att[5][:, :], 1, w.w4[:, c, D + 1:D + 2]))
            for n, (weight, row, heads, out) in enumerate(folds):
                width = weight.shape[1]
                dve.tensor_tensor(prod[:, n, 0:width], weight, row, ALU.mult).then_inc(prod_ready, 1)
            for n, (weight, row, heads, out) in enumerate(folds):
                width = weight.shape[1]
                dve.wait_ge(prod_ready, n + 1)
                dve.tensor_reduce(out, prod[:, n, 0:width].rearrange("p (h d) -> p h d", h=heads), AX, ALU.add)
            dve.wait_ge(w2_turned, 1)
            dve.tensor_copy(w.w2[:, :], w2t[:, :])
            chain = Chain(dve, part_step)

            def link(ins):
                chain.upto(chain.add(ins))

            dve.wait_ge(ident_step, 2)
            for k, bias in enumerate((w.b0, w.b1b, w.b2)):
                link(dve.tensor_copy(rest[:, k, :], bias[0:3, :]))
            for k in range(3):
                link(dve.tensor_copy(part[k][:, :, :], rest[:, :, :]))
                link(dve.tensor_copy(partf[k][:, :, :], part[k][:, :, :]))
                if k < 2:
                    link(dve.tensor_tensor(rest[:, :, :], rest[:, :, :], partf[k][:, :, :], ALU.subtract))
            link(dve.tensor_scalar(parts_sum[:, :, :], partf[0][:, :, :], w.ident[0:3, 0:1], None, ALU.mult))
            for k in (1, 2):
                link(dve.scalar_tensor_tensor(out=parts_sum[:, :, :], in0=partf[k][:, :, :], scalar=w.ident[0:3, k:k + 1],
                                              in1=parts_sum[:, :, :], op0=ALU.mult, op1=ALU.add))
            dve.tensor_copy(w.bias_parts[:, :, :], parts_sum[:, :, :])
    return w


def dense_pass(nc, w, x_dram, tables, out_dram):
    t2_dram, t3_dram, t4_dram = tables
    N = x_dram.shape[0]
    groups = -(-N // GROUP)
    C3 = w.C3
    short = groups * GROUP - N
    assert 0 <= short < GROUP and short % TG == 0
    skip = short // TG

    with ExitStack() as ctx:
        def sb(name, shape, n=NS):
            return in_turn([ctx.enter_context(nc.sbuf_tensor(f"d_{name}{s}", shape, F32)) for s in range(n)])

        def pb(name, shape, n):
            return in_turn([ctx.enter_context(nc.psum_tensor(f"d_{name}{s}", shape, F32)) for s in range(n)])

        def sem(name):
            return ctx.enter_context(nc.semaphore("d_" + name))

        def in_turn(tiles):
            return (tiles * NS)[:NS]

        X = sb("x", [P, TG, D])
        X1 = sb("x1", [P, TG, D])
        X2 = sb("x2", [P, TG, D])
        X3 = sb("x3", [P, TG, D])
        XH = sb("xh", [P, TG, D])
        OUT = sb("out", [P, TG, D])
        H = [sb("h", [P, TG, D])] * 3 + [sb("h3", [P, TG, D])]
        HT = [sb("ht", [P, TG, P])] * 3 + [sb("ht3", [P, TG, P], 2)]
        Y0 = sb("y0", [P, TG, D])
        S0 = sb("s0", [P, TG, D])
        Z1T = sb("z1t", [P, TG, P])
        Z2 = sb("z2", [P, TG, D])
        L2 = sb("l2", [P, TG, D])
        C1Z = sb("c1z", [P, C3, TG * P], 2)
        C1T = sb("c1t", [P, C3, TG, P], 2)
        G = sb("g", [P, TG, D + 2])
        Z4 = sb("z4", [P, TG, D])
        L4 = sb("l4", [P, TG, D])
        ST = [sb(f"st{k}", [P, TG, 6]) for k in range(4)]
        MV = [sb(f"mv{k}", [P, TG, 2]) for k in range(4)]
        VE = [sb(f"ve{k}", [P, TG]) for k in range(4)]
        RS = [sb(f"rs{k}", [P, TG]) for k in range(4)]
        NM = [sb(f"nm{k}", [P, TG]) for k in range(4)]
        P0 = pb("p0", [P, TG, D], 1)
        P1 = pb("p1", [P, TG, D], 2)
        P2 = pb("p2", [P, TG, D], 1)
        PA = pb("pa", [P, TG, 2 * D], 2)
        PT = [P0, P1, P2, [pa[:, :, :].rearrange("p t n -> p (t n)")[:, 0:TG * P].rearrange("p (t n) -> p t n", t=TG)
                           for pa in PA]]

        x_loaded = [sem(f"x_loaded{s}") for s in range(NS)]
        x2_stored = [sem(f"x2_stored{s}") for s in range(NS)]
        x3_stored = [sem(f"x3_stored{s}") for s in range(NS)]
        g_stored = [sem(f"g_stored{s}") for s in range(NS)]
        out_stored = [sem(f"out_stored{s}") for s in range(NS)]
        pool_step = sem("pool_step")
        bn_ready = [sem(f"bn_ready{k}") for k in range(4)]
        stats_ready = [sem(f"stats_ready{k}") for k in range(4)]
        rstd_ready = [sem(f"rstd_ready{k}") for k in range(4)]
        shift_ready = [sem(f"shift_ready{k}") for k in range(4)]
        h_ready = [sem(f"h_ready{k}") for k in range(4)]
        turned = [sem(f"turned{k}") for k in range(4)]
        ht_ready = [sem(f"ht_ready{k}") for k in range(4)]
        mm0_done, y0_ready, s0_ready, x1_ready = (sem(n) for n in ("mm0_done", "y0_ready", "s0_ready", "x1_ready"))
        mm1_done, z1_ready, mm1b_done, x2_ready = (
            sem(n) for n in ("mm1_done", "z1_ready", "mm1b_done", "x2_ready"))
        mm2_done, z2_ready, l2_ready, x3_ready, xh_ready = (
            sem(n) for n in ("mm2_done", "z2_ready", "l2_ready", "x3_ready", "xh_ready"))
        mm3_done, c1z_ready, c1_ready, mm4_done, g_ready, z4_ready, l4_ready, out_ready = (
            sem(n) for n in ("mm3_done", "c1z_ready", "c1_ready", "mm4_done", "g_ready", "z4_ready", "l4_ready", "out_ready"))
        layer_in = [X, X1, X2, X3]
        layer_in_ready = [None, x1_ready, x2_ready, x3_ready]

        block = ctx.enter_context(nc.Block())

        def rows(dram, u):
            start = N - GROUP if last_group(u) else u * GROUP
            return dram[bass.ds(start, GROUP), :].rearrange("(p t) n -> p t n", t=TG)

        def last_group(u):
            return isinstance(u, int) and u == groups - 1

        @block.sync
        def _(sp):
            def load(u, s, r):
                past(sp, x1_ready, u + 1 - NS)
                sp.dma_start(X[s][:, :, :], rows(x_dram, u)).then_inc(x_loaded[s], 16)

            def store(dram, tile, ready, stored):
                def stage(u, s, r):
                    sp.wait_ge(ready, u + 1)
                    lo = skip if last_group(u) else 0
                    sp.dma_start(rows(dram, u)[lo:P], tile[s][lo:P, :, :]).then_inc(stored[s], 16)
                return stage

            run_slots(sp, None, groups, [
                (load, -1), (store(t2_dram, X2, x2_ready, x2_stored), 3), (store(t3_dram, X3, x3_ready, x3_stored), 5),
                (store(t4_dram, G, g_ready, g_stored), 9), (store(out_dram, OUT, out_ready, out_stored), 10)])
            for stored in (x2_stored, x3_stored, g_stored, out_stored):
                for s in range(NS):
                    sp.wait_ge(stored[s], 16 * len(range(s, groups, NS)))

        @block.gpsimd
        def _(pool):
            chain = Chain(pool, pool_step)

            def rstd(k):
                def stage(u, s, r):
                    pool.wait_ge(stats_ready[k], u + 1)
                    layer_rstd(chain, MV[k][s], VE[k][s][:, :], RS[k][s][:, :], w.half[:, :])\
                        .then_inc(rstd_ready[k], 1)
                return stage

            def x3(u, s, r):
                pool.wait_ge(l2_ready, u + 1)
                past(pool, x3_stored[s], 16 * r)
                past(pool, xh_ready, u + 1 - NS)
                pool.tensor_tensor(X3[s][:, :, :], X2[s][:, :, :], L2[s][:, :, :], ALU.add).then_inc(x3_ready, 1)

            def xh(u, s, r):
                pool.wait_ge(h_ready[3], u + 1)
                pool.wait_ge(x3_ready, u + 1)
                past(pool, out_ready, u + 1 - NS)
                pool.tensor_tensor(XH[s][:, :, :], H[3][s][:, :, :], X3[s][:, :, :], ALU.add).then_inc(xh_ready, 1)

            def z4(u, s, r):
                pool.wait_ge(g_ready, u + 1)
                pool.tensor_tensor(Z4[s][:, :, :], G[s][:, :, 0:D],
                                   w.b4[:, None, :].to_broadcast([P, TG, D]), ALU.add).then_inc(z4_ready, 1)

            def final(u, s, r):
                pool.wait_ge(l4_ready, u + 1)
                past(pool, out_stored[s], 16 * r)
                pool.wait_ge(xh_ready, u + 1)
                pool.tensor_tensor(OUT[s][:, :, :], XH[s][:, :, :], L4[s][:, :, :], ALU.add).then_inc(out_ready, 1)

            run_slots(pool, chain, groups, [
                (rstd(2), 3), (rstd(0), 0), (rstd(3), 5), (xh, 6), (z4, 8), (rstd(1), 1), (x3, 4),
                (final, 9)])

        @block.scalar
        def _(act):
            def turn(k):
                def stage(u, s, r):
                    act.wait_ge(turned[k], u + 1)
                    if k == 0:
                        past(act, mm2_done, u + 1 - NS)
                    act.activation(HT[k][s][:, :, :], PT[k][s][:, :, :], ACT.Copy).then_inc(ht_ready[k], 1)
                return stage

            def norm(k):
                def stage(u, s, r):
                    act.wait_ge(shift_ready[k], u + 1)
                    if k == 0:
                        past(act, turned[2], u + 1 - NS)
                    if k == 3:
                        past(act, turned[3], u + 1 - NS)
                        past(act, xh_ready, u + 1 - NS)
                    last = norm_rows(act, H[k][s], layer_in[k][s], RS[k][s], NM[k][s])
                    last.then_inc(h_ready[k], 1)
                return stage

            def s0(u, s, r):
                act.wait_ge(mm0_done, u + 1)
                act.activation(S0[s][:, :, :], P0[s][:, :, :], ACT.Silu).then_inc(s0_ready, 1)

            def z1(u, s, r):
                act.wait_ge(mm1_done, u + 1)
                act.activation(Z1T[s][:, :, :], P1[s][:, :, :], ACT.Relu, bias=w.b1[:, 0:1]).then_inc(z1_ready, 1)

            def c1(u, s, r):
                act.wait_ge(mm3_done, u + 1)
                pa = PA[s][:, :, :].rearrange("p t n -> p (t n)").rearrange("p (c n) -> p c n", c=C3)
                for c in range(C3):
                    last = act.activation(C1Z[s][:, c, :], pa[:, c, :], ACT.Identity, bias=w.b3[:, c:c + 1])
                last.then_inc(c1z_ready, 1)

            def g(u, s, r):
                act.wait_ge(mm4_done, u + 1)
                past(act, g_stored[s], 16 * r)
                past(act, z4_ready, u + 1 - NS)
                act.activation(G[s][:, :, :], PA[s][:, :, 0:D + 2], ACT.Copy).then_inc(g_ready, 1)

            run_slots(act, None, groups, [
                (s0, 1), (norm(1), 2), (turn(2), 4), (g, 8), (turn(1), 2), (c1, 7), (norm(0), 0), (z1, 2),
                (turn(3), 6), (turn(0), 0), (norm(2), 3), (norm(3), 5)])

        @block.tensor
        def _(pe):
            def turn(k):
                def stage(u, s, r):
                    pe.wait_ge(h_ready[k], u + 1)
                    past(pe, *[(y0_ready, u), (x2_ready, u - 1), (z2_ready, u), (g_ready, u - 1)][k])
                    for j in range(TG):
                        last = pe.transpose(PT[k][s][:, j, :], H[k][s][:, j, :], w.ident[:, :])
                    last.then_inc(turned[k], 1)
                return stage

            def mm0(u, s, r):
                pe.wait_ge(ht_ready[0], u + 1)
                bias_rows(pe, w, P, P0[s][:, :, :], 0)
                for j in range(TG):
                    last = pe.matmul(P0[s][:, j, :], HT[0][s][:, j, :], w.w0[:, 0:D], start=False, stop=j == TG - 1)
                last.then_inc(mm0_done, 1)

            def mm2(u, s, r):
                pe.wait_ge(ht_ready[2], u + 1)
                for j in range(TG):
                    last = pe.matmul(P2[s][:, j, :], HT[2][s][:, j, :], w.w2[:, :], start=True, stop=True)
                last.then_inc(mm2_done, 1)

            def mm1(u, s, r):
                pe.wait_ge(ht_ready[1], u + 1)
                pe.matmul(P1[s][:, :, :], w.w1x[:, :], HT[1][s][:, :, :], start=True, stop=True).then_inc(mm1_done, 1)

            def mm1b(u, s, r):
                pe.wait_ge(z1_ready, u + 1)
                bias_rows(pe, w, P, P1[s][:, :, :], 1)
                for j in range(TG):
                    last = pe.matmul(P1[s][:, j, :], Z1T[s][:, j, :], w.w1b[:, :], start=False, stop=j == TG - 1)
                last.then_inc(mm1b_done, 1)

            def mm3(u, s, r):
                pe.wait_ge(ht_ready[3], u + 1)
                pa = PA[s][:, :, :].rearrange("p t n -> p (t n)").rearrange("p (c n) -> p c n", c=C3)
                for c in range(C3):
                    last = pe.matmul(pa[:, c, :], w.w3[:, c * P:(c + 1) * P],
                                     HT[3][s][:, :, :].rearrange("p t n -> p (t n)"), start=True, stop=True)
                last.then_inc(mm3_done, 1)

            def mm4(u, s, r):
                pe.wait_ge(c1_ready, u + 1)
                for j in range(TG):
                    for c in range(C3):
                        last = pe.matmul(PA[s][:, j, 0:D + 2], C1T[s][:, c, j, :], w.w4[:, c, :],
                                         start=(c == 0), stop=(c == C3 - 1))
                last.then_inc(mm4_done, 1)

            run_slots(pe, None, groups, [
                (turn(2), 4), (mm4, 8), (turn(1), 2), (mm2, 4), (turn(3), 6), (mm1, 2), (turn(0), 0),
                (mm1b, 2), (mm3, 6), (mm0, 0)])

        @block.vector
        def _(dve):
            def row(bias):
                return bias[:, None, :].to_broadcast([P, TG, D])

            def stats(k):
                def stage(u, s, r):
                    if k == 0:
                        dve.wait_ge(x_loaded[s], 16 * (r + 1))
                    else:
                        dve.wait_ge(layer_in_ready[k], u + 1)
                    for j in range(TG):
                        last = dve.bn_stats(ST[k][s][:, j, :], layer_in[k][s][:, j, :])
                    last.then_inc(bn_ready[k], 1)
                return stage

            def aggr(k):
                def stage(u, s, r):
                    dve.wait_ge(bn_ready[k], u + 1)
                    alone(dve)
                    for j in range(TG):
                        last = dve.bn_aggr(MV[k][s][:, j, :], ST[k][s][:, j, :])
                    last.then_inc(stats_ready[k], 1)
                return stage

            def shift(k):
                def stage(u, s, r):
                    dve.wait_ge(rstd_ready[k], u + 1)
                    layer_shift(dve, NM[k][s], MV[k][s], RS[k][s]).then_inc(shift_ready[k], 1)
                return stage

            def y0(u, s, r):
                dve.wait_ge(s0_ready, u + 1)
                dve.scalar_tensor_tensor(out=Y0[s][:, :, :], in0=P0[s][:, :, :], scalar=0.5, in1=X[s][:, :, :],
                                         op0=ALU.mult, op1=ALU.add).then_inc(y0_ready, 1)

            def x1(u, s, r):
                dve.wait_ge(s0_ready, u + 1)
                dve.wait_ge(y0_ready, u + 1)
                dve.scalar_tensor_tensor(out=X1[s][:, :, :], in0=S0[s][:, :, :], scalar=1.2 - 0.5,
                                         in1=Y0[s][:, :, :], op0=ALU.mult, op1=ALU.add).then_inc(x1_ready, 1)

            def x2(u, s, r):
                dve.wait_ge(mm1b_done, u + 1)
                dve.wait_ge(x1_ready, u + 1)
                past(dve, x2_stored[s], 16 * r)
                past(dve, x3_ready, u + 1 - NS)
                dve.tensor_tensor(X2[s][:, :, :], P1[s][:, :, :], X1[s][:, :, :], ALU.add).then_inc(x2_ready, 1)

            def z2(u, s, r):
                dve.wait_ge(mm2_done, u + 1)
                dve.scalar_tensor_tensor(out=Z2[s][:, :, :], in0=P2[s][:, :, :], scalar=0.5, in1=row(w.b2),
                                         op0=ALU.mult, op1=ALU.add).then_inc(z2_ready, 1)

            def l2(u, s, r):
                dve.wait_ge(z2_ready, u + 1)
                leaky_relu(dve, L2[s][:, :, :], Z2[s][:, :, :]).then_inc(l2_ready, 1)

            def c1(u, s, r):
                dve.wait_ge(c1z_ready, u + 1)
                leaky_relu(dve, C1T[s][:, :, :, :].rearrange("p c t n -> p (c t n)"),
                      C1Z[s][:, :, :].rearrange("p c n -> p (c n)")).then_inc(c1_ready, 1)

            def l4(u, s, r):
                dve.wait_ge(z4_ready, u + 1)
                past(dve, out_ready, u + 1 - NS)
                leaky_relu(dve, L4[s][:, :, :], Z4[s][:, :, :]).then_inc(l4_ready, 1)

            run_slots(dve, None, groups, [
                (stats(0), 0), (aggr(2), 3), (y0, 1), (stats(3), 5), (aggr(0), 0), (x1, 1), (shift(2), 3),
                (aggr(3), 5), (l4, 9), (shift(0), 0), (stats(1), 1), (z2, 4), (shift(3), 5), (c1, 7),
                (aggr(1), 1), (l2, 4), (x2, 2), (shift(1), 1), (stats(2), 2)])


class Phase:

    def __init__(self, nc, name):
        self.nc, self.name, self.ctx, self.sems = nc, name, ExitStack(), []

    def sb(self, name, shape, dt=F32):
        return self.ctx.enter_context(self.nc.sbuf_tensor(f"{self.name}_{name}", shape, dt))

    def sbs(self, name, shape, dt=F32):
        return [self.sb(f"{name}{s}", shape, dt) for s in range(NS)]

    def pbs(self, name, shape):
        return [self.ctx.enter_context(self.nc.psum_tensor(f"{self.name}_{name}{s}", shape, F32)) for s in range(NS)]

    def stream_sems(self, name):
        return [self.sem(f"{name}{s}") for s in range(NS)]

    def pb2(self, name, shape):
        return [self.ctx.enter_context(self.nc.psum_tensor(f"{self.name}_{name}{s}", shape, F32)) for s in range(2)]

    def sem(self, name):
        self.sems.append(self.nc.alloc_semaphore(f"{self.name}_{name}"))
        return self.sems[-1]

    def end(self):
        self.ctx.close()
        self.nc.clear_and_free_semaphores(self.sems)
        self.nc.all_engine_barrier(sem_only=True)


class Edges:
    pass


def load_edges(nc, ctx, w, a):
    e = Edges()
    E = a["dst"].shape[0]
    R = max(r for r in range(1, P + 1) if E % r == 0 and (E // r) % TG == 0)
    T = E // R
    assert (T // TG) >= 4
    e.R, e.T, e.units = R, T, T // TG

    def sb(name, shape, dt=F32):
        return ctx.enter_context(nc.sbuf_tensor("e_" + name, shape, dt))

    e.src = sb("src", [R, T], I32)
    e.dst = sb("dst", [R, T], I32)
    e.row = sb("row", [R, T], I32)
    e.cont = sb("cont", [R, T])
    e.pen = sb("pen", [R, T])
    e.shifts = [1 << k for k in range((T - 1).bit_length())]
    e.penr = sb("penr", [R, len(e.shifts), T])
    e.lastpen = sb("lastpen", [R, T])
    e.lead = sb("lead", [R, T])
    e.leadpen = sb("leadpen", [R, T])
    e.trailpen = sb("trailpen", [R, T])
    e.carry = sb("carry", [R, R])
    e.penf = sb("penf", [R, R])
    e.penb = sb("penb", [R, R])
    e.rcount = sb("rcount", [R, T])

    ph = Phase(nc, "mask")
    DX = ph.sb("dx", [R, T + 2], I32)
    DF = ph.sb("df", [R, T + 2])
    CONTN = ph.sb("contn", [R, T])
    TRAIL = ph.sb("trail", [R, T])
    ROWF = ph.sb("rowf", [R, T])
    SAME = ph.sb("same", [R, len(e.shifts), T])
    ONES = ph.sb("ones", [R, T])
    CNT = ph.sb("cnt", [R, T])
    HEADS = ph.sb("heads", [R, R])
    TAILS = ph.sb("tails", [R, R])
    EF = ph.sb("ef", [R, R])
    HB, TB = ph.pb2("pm", [R, R])
    CC = ph.ctx.enter_context(nc.psum_tensor("mask_cc", [R, 1], F32))
    edges_set, loaded, step = ph.sem("edges_set"), ph.sem("loaded"), ph.sem("dve_step")
    mats_ready, turned, eq_ready, tri_ready = (ph.sem(n) for n in ("mats_ready", "turned", "eq_ready", "tri_ready"))
    cnt_ready, cnt_carried = ph.sem("cnt_ready"), ph.sem("cnt_carried")
    dst = a["dst"].rearrange("(p t) -> p t", t=T)
    with nc.Block() as block, nc.allow_non_contiguous_dma("one index per partition"):
        @block.sync
        def _(sp):
            sp.dma_start(e.src[:, :], a["src"].rearrange("(p t) -> p t", t=T)).then_inc(loaded, 16)
            sp.dma_start(e.dst[:, :], dst).then_inc(loaded, 16)
            sp.dma_start(DX[:, 1:T + 1], dst).then_inc(loaded, 16)
            sp.wait_ge(edges_set, 1)
            sp.dma_start(DX[1:R, 0:1], dst[0:R - 1, T - 1:T]).then_inc(loaded, 16)
            sp.dma_start(DX[0:R - 1, T + 1:T + 2], dst[1:R, 0:1]).then_inc(loaded, 16)

        @block.gpsimd
        def _(pool):
            pool.memset(DX[:, 0:1], -1)
            pool.memset(DX[:, T + 1:T + 2], -1).then_inc(edges_set, 1)
            pool.wait_ge(eq_ready, 2)
            pool.affine_select(out=e.carry[:, :], in_=e.carry[:, :], compare_op=ALU.is_gt, fill=0.0,
                               base=0, pattern=[[1, R]], channel_multiplier=-1).then_inc(tri_ready, 1)
            pool.affine_select(out=EF[:, :], in_=EF[:, :], compare_op=ALU.is_gt, fill=0.0,
                               base=0, pattern=[[-1, R]], channel_multiplier=1).then_inc(tri_ready, 1)

        @block.tensor
        def _(pe):
            pe.wait_ge(mats_ready, 2)
            pe.transpose(HB[:, :], HEADS[:, :], w.ident[0:R, 0:R]).then_inc(turned, 1)
            pe.transpose(TB[:, :], TAILS[:, :], w.ident[0:R, 0:R]).then_inc(turned, 1)
            pe.wait_ge(tri_ready, 2)
            pe.wait_ge(cnt_ready, 1)
            pe.matmul(CC[:, :], e.carry[:, :], CNT[:, T - 1:T], start=True, stop=True).then_inc(cnt_carried, 1)

        @block.vector
        def _(dve):
            count = [0]

            def link(ins):
                count[0] += 1
                ins.then_inc(step, 1)
                dve.wait_ge(step, count[0])

            dve.memset(ONES[:, :], 1.0)
            dve.wait_ge(loaded, 80)
            link(dve.tensor_copy(DF[:, :], DX[:, :]))
            mid = DF[:, 1:T + 1]
            dve.tensor_copy(HEADS[:, :], DF[:, 1:2].to_broadcast([R, R])).then_inc(mats_ready, 1)
            dve.tensor_copy(TAILS[:, :], DF[:, T:T + 1].to_broadcast([R, R])).then_inc(mats_ready, 1)
            dve.tensor_tensor(e.cont[:, :], mid, DF[:, 0:T], ALU.is_equal)
            link(dve.tensor_tensor(CONTN[:, :], mid, DF[:, 2:T + 2], ALU.is_equal))
            dve.tensor_scalar(e.lastpen[:, :], CONTN[:, :], -BIG, None, ALU.mult)
            dve.tensor_scalar(e.pen[:, :], e.cont[:, :], -1.0, BIG, ALU.add, ALU.mult)
            for k, shift in enumerate(e.shifts):
                last = dve.tensor_tensor(SAME[:, k, 0:T - shift], DF[:, 1:T + 1 - shift], DF[:, 1 + shift:T + 1],
                                         ALU.is_equal)
            link(last)
            for k, shift in enumerate(e.shifts):
                dve.tensor_scalar(e.penr[:, k, 0:T - shift], SAME[:, k, 0:T - shift], -1.0, BIG, ALU.add, ALU.mult)
            dve.tensor_tensor_scan(e.lead[:, :], e.cont[:, :], e.cont[:, :], 1.0, ALU.mult, ALU.mult)
            dve.tensor_scalar(TRAIL[:, :], mid, DF[:, T:T + 1], None, ALU.is_equal)
            dve.tensor_tensor_scan(CNT[:, :], e.cont[:, :], ONES[:, :], 0.0, ALU.mult, ALU.add).then_inc(cnt_ready, 1)
            link(dve.scalar_tensor_tensor(out=ROWF[:, :], in0=CONTN[:, :], scalar=65536.0, in1=mid,
                                          op0=ALU.mult, op1=ALU.add))
            dve.tensor_copy(e.row[:, :], ROWF[:, :])
            dve.tensor_scalar(e.leadpen[:, :], e.lead[:, :], -1.0, BIG, ALU.add, ALU.mult)
            dve.tensor_scalar(e.trailpen[:, :], TRAIL[:, :], -1.0, BIG, ALU.add, ALU.mult)
            dve.wait_ge(turned, 2)
            dve.tensor_scalar(e.carry[:, :], HB[:, :], DF[:, T:T + 1], None, ALU.is_equal).then_inc(eq_ready, 1)
            dve.tensor_scalar(EF[:, :], TB[:, :], DF[:, 1:2], None, ALU.is_equal).then_inc(eq_ready, 1)
            dve.wait_ge(tri_ready, 2)
            dve.tensor_scalar(e.penf[:, :], EF[:, :], -1.0, BIG, ALU.add, ALU.mult)
            dve.tensor_scalar(e.penb[:, :], e.carry[:, :], -1.0, BIG, ALU.add, ALU.mult)
            dve.wait_ge(cnt_carried, 1)
            link(dve.scalar_tensor_tensor(out=CNT[:, :], in0=e.lead[:, :], scalar=CC[:, 0:1], in1=CNT[:, :],
                                          op0=ALU.mult, op1=ALU.add))
            link(dve.tensor_scalar(CNT[:, :], CNT[:, :], 1.0, 1.0, ALU.max, ALU.add))
            dve.reciprocal(e.rcount[:, :], CNT[:, :])
    ph.end()
    return e


def edge_softmax(nc, w, e, name, H, as_src, as_self, ad_self, eps, out, spread):
    R, T = e.R, e.T
    ph = Phase(nc, name)
    A = ph.sb("a", [R, H, T])
    AS = ph.sb("as", [R, H, T])
    L = ph.sb("l", [R, H, T])
    LS = ph.sb("ls", [R, H, T])
    F = ph.sb("f", [R, H, T])
    B = ph.sb("b", [R, H, T])
    FAR = ph.sb("far", [R, 2 * H, T])
    OWN = ph.sb("own", [R, 2 * H, T])
    ENDS = ph.sb("ends", [R, 2, H, R])
    PICK = ph.sb("pick", [R, 2, H, R])
    CM = ph.sb("cm", [R, 2, H])
    DEN = ph.sb("den", [R, H, T])
    DT = ph.sb("dt", [R, H])
    PE_ENDS = [ph.ctx.enter_context(nc.psum_tensor(f"{name}_pe{d}", [R, H, P], F32)) for d in range(2)]
    PE_OWN = [ph.ctx.enter_context(nc.psum_tensor(f"{name}_po{d}", [R, H, P], F32)) for d in range(2)]
    PD = ph.ctx.enter_context(nc.psum_tensor(f"{name}_pd", [R, H], F32))
    step, ends_ready, ends_turned = ph.sem("dve_step"), ph.sem("ends_ready"), ph.sem("ends_turned")
    arg_ready, exp_ready, tails_ready, tails_carried, own_ready, own_turned = (
        ph.sem(n) for n in ("arg_ready", "exp_ready", "tails_ready", "tails_carried", "own_ready", "own_turned"))

    def turned(ap):
        return ap.rearrange("p t h -> p h t")

    with nc.Block() as block:
        @block.tensor
        def _(pe):
            if spread:
                pe.wait_ge(own_ready, 2 * H)
                for d in range(2):
                    for h in range(H):
                        last = pe.transpose(PE_OWN[d][:, h, 0:R], ENDS[:, d, h, :], w.ident[0:R, 0:R])
                last.then_inc(own_turned, 1)
            pe.wait_ge(ends_ready, 2 * H)
            for d in range(2):
                for h in range(H):
                    last = pe.transpose(PE_ENDS[d][:, h, 0:R], ENDS[:, d, h, :], w.ident[0:R, 0:R])
            last.then_inc(ends_turned, 1)
            pe.wait_ge(tails_ready, 1)
            pe.matmul(PD[:, :], e.carry[:, :], DT[:, :], start=True, stop=True).then_inc(tails_carried, 1)

        @block.scalar
        def _(act):
            act.wait_ge(arg_ready, 2)
            act.activation(out.w[:, :, :], F[:, :, :], ACT.Exp).then_inc(exp_ready, 1)
            act.activation(AS[:, :, :], LS[:, :, :], ACT.Exp).then_inc(exp_ready, 1)

        @block.vector
        def _(dve):
            count = [0]

            def link(ins):
                count[0] += 1
                ins.then_inc(step, 1)
                dve.wait_ge(step, count[0])

            def from_slot_on(m, heads_):
                for k, shift in enumerate(e.shifts):
                    n = T - shift
                    link(dve.tensor_tensor(FAR[:, 0:heads_, 0:n], m[:, :, shift:T],
                                           e.penr[:, k, None, 0:n].to_broadcast([R, heads_, n]), ALU.add))
                    link(dve.tensor_tensor(m[:, :, 0:n], m[:, :, 0:n], FAR[:, 0:heads_, 0:n], ALU.max))

            link(dve.tensor_tensor(AS[:, :, :], turned(as_self), turned(ad_self), ALU.add))
            link(dve.scalar_tensor_tensor(out=LS[:, :, :], in0=AS[:, :, :], scalar=SLOPE, in1=AS[:, :, :],
                                          op0=ALU.mult, op1=ALU.max))
            ad = turned(ad_self)
            if spread:
                lastpen = e.lastpen[:, None, :].to_broadcast([R, H, T])
                dve.tensor_tensor(OWN[:, 0:H, :], ad, lastpen, ALU.add)
                link(dve.tensor_tensor(OWN[:, H:2 * H, :], LS[:, :, :], lastpen, ALU.add))
                from_slot_on(OWN, 2 * H)
                for h in range(2 * H):
                    dve.tensor_copy(ENDS[:, h // H, h % H, :], OWN[:, h, 0:1].to_broadcast([R, R]))\
                        .then_inc(own_ready, 1)
                dve.wait_ge(own_turned, 1)
                for d in range(2):
                    last = dve.tensor_tensor(PICK[:, d, :, :], PE_OWN[d][:, :, 0:R],
                                             e.penb[:, None, :].to_broadcast([R, H, R]), ALU.add)
                link(last)
                link(dve.tensor_reduce(CM[:, :, :].rearrange("p d h -> p (d h)"),
                                       PICK[:, :, :, :].rearrange("p d h q -> p (d h) q"), AX, ALU.max))
                for h in range(2 * H):
                    last = dve.scalar_tensor_tensor(out=OWN[:, h, :], in0=e.trailpen[:, :],
                                                    scalar=CM[:, h // H, h % H:h % H + 1], in1=OWN[:, h, :],
                                                    op0=ALU.add, op1=ALU.max)
                link(last)
                link(dve.tensor_copy(LS[:, :, :], OWN[:, H:2 * H, :]))
                ad = OWN[:, 0:H, :]
            link(dve.tensor_tensor(A[:, :, :], turned(as_src), ad, ALU.add))
            link(dve.scalar_tensor_tensor(out=L[:, :, :], in0=A[:, :, :], scalar=SLOPE, in1=A[:, :, :],
                                          op0=ALU.mult, op1=ALU.max))
            for h in range(H):
                dve.tensor_tensor_scan(F[:, h, :], e.pen[:, :], L[:, h, :], -BIG, ALU.add, ALU.max)
            link(dve.tensor_copy(B[:, :, :], L[:, :, :]))
            from_slot_on(B, H)
            for d, (m, t) in enumerate(((F, T - 1), (B, 0))):
                for h in range(H):
                    dve.tensor_copy(ENDS[:, d, h, :], m[:, h, t:t + 1].to_broadcast([R, R])).then_inc(ends_ready, 1)
            dve.wait_ge(ends_turned, 1)
            for d, pen in enumerate((e.penf, e.penb)):
                last = dve.tensor_tensor(PICK[:, d, :, :], PE_ENDS[d][:, :, 0:R],
                                         pen[:, None, :].to_broadcast([R, H, R]), ALU.add)
            link(last)
            link(dve.tensor_reduce(CM[:, :, :].rearrange("p d h -> p (d h)"),
                                   PICK[:, :, :, :].rearrange("p d h q -> p (d h) q"), AX, ALU.max))
            for h in range(H):
                dve.scalar_tensor_tensor(out=F[:, h, :], in0=e.leadpen[:, :], scalar=CM[:, 0, h:h + 1],
                                         in1=F[:, h, :], op0=ALU.add, op1=ALU.max)
                last = dve.scalar_tensor_tensor(out=B[:, h, :], in0=e.trailpen[:, :], scalar=CM[:, 1, h:h + 1],
                                                in1=B[:, h, :], op0=ALU.add, op1=ALU.max)
            link(last)
            link(dve.tensor_tensor(B[:, :, :], F[:, :, :], B[:, :, :], ALU.max))
            link(dve.tensor_tensor(B[:, :, :], B[:, :, :], LS[:, :, :], ALU.max))
            dve.tensor_tensor(F[:, :, :], L[:, :, :], B[:, :, :], ALU.subtract).then_inc(arg_ready, 1)
            dve.tensor_tensor(LS[:, :, :], LS[:, :, :], B[:, :, :], ALU.subtract).then_inc(arg_ready, 1)
            dve.wait_ge(exp_ready, 2)
            for h in range(H):
                last = dve.tensor_tensor_scan(DEN[:, h, :], e.cont[:, :], out.w[:, h, :], 0.0, ALU.mult, ALU.add)
            link(last)
            dve.tensor_copy(DT[:, :], DEN[:, :, T - 1]).then_inc(tails_ready, 1)
            dve.wait_ge(tails_carried, 1)
            for h in range(H):
                last = dve.scalar_tensor_tensor(out=DEN[:, h, :], in0=e.lead[:, :], scalar=PD[:, h:h + 1],
                                                in1=DEN[:, h, :], op0=ALU.mult, op1=ALU.add)
            link(last)
            link(dve.scalar_tensor_tensor(out=DEN[:, :, :], in0=DEN[:, :, :], scalar=eps, in1=AS[:, :, :],
                                          op0=ALU.add, op1=ALU.add))
            link(dve.reciprocal(out.rd[:, :, :], DEN[:, :, :]))
            dve.tensor_tensor(out.ws[:, :, :], AS[:, :, :], out.rd[:, :, :], ALU.mult)
            dve.tensor_tensor(out.lrd[:, :, :], out.rd[:, :, :],
                              e.lead[:, None, :].to_broadcast([R, H, T]), ALU.mult)
    ph.end()


def place_indices(pool, chain, index, stage, u):
    alone(pool)
    return chain.add(pool.tensor_copy(stage[:, :], index[:, bass.ds(u * TG, TG)]))


def gather_rows(pool, table, stage, tile, done):
    alone(pool)
    for j in range(TG):
        pool.indirect_dma_start(out=tile[:, j, :], out_offset=None, in_=table,
                                in_offset=bass.IndirectOffsetOnAxis(ap=stage[:, j:j + 1], axis=0)).then_inc(done, 16)


def scatter_rows(pool, table, stage, tile, done):
    alone(pool)
    for j in range(TG):
        pool.indirect_dma_start(out=table, out_offset=bass.IndirectOffsetOnAxis(ap=stage[:, j:j + 1], axis=0),
                                in_=tile[:, j, :], in_offset=None, bounds_check=table.shape[0] - 1,
                                oob_is_err=False).then_inc(done, 16)


def project_ends(nc, w, e, name, source_table, keep_dst, weights, outs, normed):
    R, units = e.R, e.units
    ph = Phase(nc, name)
    XG, H = (ph.sbs(n, [R, 2, TG, D]) for n in ("xg", "h"))
    IDX = ph.sbs("idx", [R, 2, TG], I32)
    HT = ph.sbs("ht", [P, 2, TG, P])
    ST, MV, VE, RS = (ph.sbs(n, [R, 2 * TG] + d) for n, d in (("st", [6]), ("mv", [2]), ("ve", []), ("rs", [])))
    NM = ph.sbs("nm", [R, TG])
    widths = [weight.shape[1] for weight in weights]
    PT = ph.ctx.enter_context(nc.psum_tensor(f"{name}_pt", [P, 2, TG, P], F32))
    PW = [ph.ctx.enter_context(nc.psum_tensor(
        f"{name}_pw{side}", [R, TG, 1 << (width - 1).bit_length()], F32)) for side, width in enumerate(widths)]
    gathered_src, gathered_dst = ph.stream_sems("gathered_src"), ph.stream_sems("gathered_dst")
    kept = ph.stream_sems("kept")
    pool_step, dve_step = ph.sem("pool_step"), ph.sem("dve_step")
    stats_ready, rstd_ready, shift_ready, src_ready, dst_ready, turned, ht_ready, mm_done, saved = (
        ph.sem(n) for n in ("stats_ready", "rstd_ready", "shift_ready", "src_ready", "dst_ready", "turned",
                            "ht_ready", "mm_done", "saved"))

    with nc.Block() as block:
        @block.sync
        def _(sp):
            def keep(u, s, r):
                sp.wait_ge(gathered_dst[s], 16 * TG * (r + 1))
                sp.dma_start(tiles(e.x, u), XG[s][:, 1]).then_inc(kept[s], 16)

            def load(u, s, r):
                past(sp, dst_ready, u + 1 - NS)
                sp.dma_start(XG[s][:, 1], tiles(e.x, u)).then_inc(gathered_dst[s], 16)

            run_slots(sp, None, units, [(keep, 1)] if keep_dst else [(load, -1)])
            if keep_dst:
                wait_streams(sp, kept, units, 16)

        @block.gpsimd
        def _(pool):
            chain = Chain(pool, pool_step)

            def gather_src(u, s, r):
                n = place_indices(pool, chain, e.src, IDX[s][:, 0], u)
                past(pool, src_ready, u + 1 - NS)
                chain.upto(n)
                gather_rows(pool, source_table, IDX[s][:, 0], XG[s][:, 0], gathered_src[s])

            def gather_dst(u, s, r):
                n = place_indices(pool, chain, e.dst, IDX[s][:, 1], u)
                past(pool, dst_ready, u + 1 - NS)
                past(pool, kept[s], 16 * r)
                chain.upto(n)
                gather_rows(pool, source_table, IDX[s][:, 1], XG[s][:, 1], gathered_dst[s])

            def rstd(u, s, r):
                pool.wait_ge(stats_ready, u + 1)
                layer_rstd(chain, MV[s], VE[s][:, :], RS[s][:, :], w.half[0:R, :]).then_inc(rstd_ready, 1)

            run_slots(pool, chain, units, [(gather_src, 0)] + ([(gather_dst, 0)] if keep_dst else [])
                      + [(rstd, normed - 1)])

        @block.scalar
        def _(act):
            def norm(u, s, r):
                act.wait_ge(shift_ready, u + 1)
                past(act, turned, u + 1 - NS)
                norm_rows(act, H[s][:, 0], XG[s][:, 0], RS[s], NM[s]).then_inc(src_ready, 1)

            def turn(u, s, r):
                act.wait_ge(turned, u + 1)
                for side in (0, 1):
                    last = act.activation(HT[s][:, side, :, 0:R], PT[:, side, :, 0:R], ACT.Relu)
                last.then_inc(ht_ready, 1)

            def save(u, s, r):
                act.wait_ge(mm_done, u + 1)
                alone(act)
                for side in (0, 1):
                    last = act.activation(outs[side][:, bass.ds(u * TG, TG), :], PW[side][:, :, 0:widths[side]],
                                          ACT.Copy)
                last.then_inc(saved, 1)

            run_slots(act, None, units, [(norm, normed), (save, normed + 1), (turn, normed)])

        @block.tensor
        def _(pe):
            def turn(u, s, r):
                pe.wait_ge(src_ready, u + 1)
                pe.wait_ge(dst_ready, u + 1)
                past(pe, ht_ready, u)
                for side in (0, 1):
                    for j in range(TG):
                        last = pe.transpose(PT[:, side, j, 0:R], H[s][:, side, j, :], w.ident[0:R, 0:R])
                last.then_inc(turned, 1)

            def mm(u, s, r):
                pe.wait_ge(ht_ready, u + 1)
                past(pe, saved, u)
                for side in (0, 1):
                    for j in range(TG):
                        last = pe.matmul(PW[side][:, j, 0:widths[side]], HT[s][:, side, j, 0:R], weights[side],
                                         start=True, stop=True)
                last.then_inc(mm_done, 1)

            run_slots(pe, None, units, [(mm, normed + 1), (turn, normed)])

        @block.vector
        def _(dve):
            chain = Chain(dve, dve_step)

            def stats(u, s, r):
                dve.wait_ge(gathered_src[s], 16 * TG * (r + 1))
                dve.wait_ge(gathered_dst[s], (16 * TG if keep_dst else 16) * (r + 1))
                alone(dve)
                layer_stats(chain, XG[s][:, :, :, :].rearrange("p b t n -> p (b t) n"), ST[s], MV[s], 2 * TG)\
                    .then_inc(stats_ready, 1)

            def shift(u, s, r):
                dve.wait_ge(rstd_ready, u + 1)
                layer_shift(dve, NM[s], MV[s][:, 0:TG], RS[s][:, 0:TG]).then_inc(shift_ready, 1)

            def norm(u, s, r):
                dve.wait_ge(rstd_ready, u + 1)
                past(dve, turned, u + 1 - NS)
                layer_norm(chain, XG[s][:, 1], MV[s][:, TG:2 * TG], RS[s][:, TG:2 * TG], H[s][:, 1], TG)\
                    .then_inc(dst_ready, 1)

            run_slots(dve, chain, units, [(shift, normed), (norm, normed), (stats, 1)])
    ph.end()


def per_head(ap, u, d):
    v = ap[:, :, bass.ds(u * TG, TG)].rearrange("p h t -> p t h")
    return v[:, :, :, None].to_broadcast([v.shape[0], TG, ap.shape[1], d])


def heads(ap, h):
    return ap.rearrange("p t (h d) -> p t h d", h=h)


def tiles(ap, u):
    return ap[:, bass.ds(u * TG, TG)]


def sum_runs(nc, w, e, name, msg, H, sm, carried):
    R, T = e.R, e.T
    width = carried.shape[1]
    CH = 32
    chunks = width // CH
    ph = Phase(nc, name)
    M = [ph.sb(f"m{b}", [R, CH, T]) for b in range(4)]
    GO_ON = ph.sb("go_on", [R, CH, T])
    PC = ph.ctx.enter_context(nc.psum_tensor(f"{name}_pc", [R, width], F32))
    masked, summed, stored, tail_done = (ph.sem(n) for n in ("masked", "summed", "stored", "tail_done"))
    weighted = [ph.sem("dve_weighted"), ph.sem("pool_weighted")]

    def features(c):
        return msg[:, :, c * CH:(c + 1) * CH].rearrange("p t d -> p d t")

    def weight(eng, c):
        past(eng, stored, c + 1 - len(M))
        head = c * CH * H // width
        eng.tensor_tensor(M[c % len(M)][:, :, :], features(c), sm.w[:, head, None, :].to_broadcast([R, CH, T]),
                          ALU.mult).then_inc(weighted[c % 2], 1)

    def flat(tile):
        return tile[:, :, :].rearrange("p d t -> p (d t)")

    with nc.Block() as block:
        @block.gpsimd
        def _(pool):
            for c in range(1, chunks, 2):
                weight(pool, c)

        @block.vector
        def _(dve):
            dve.tensor_copy(GO_ON[:, :, :], e.cont[:, None, :].to_broadcast([R, CH, T])).then_inc(masked, 1)
            dve.wait_ge(masked, 1)
            dve.memset(GO_ON[:, :, 0:1], 0.0).then_inc(masked, 1)
            weight(dve, 0)
            dve.wait_ge(masked, 2)
            for c in range(chunks):
                if c % 2 and c + 1 < chunks:
                    weight(dve, c + 1)
                dve.wait_ge(weighted[c % 2], c // 2 + 1)
                m = flat(M[c % len(M)])
                dve.tensor_tensor_scan(m, flat(GO_ON), m, 0.0, ALU.mult, ALU.add).then_inc(summed, 1)

        @block.scalar
        def _(act):
            for c in range(chunks):
                act.wait_ge(summed, c + 1)
                act.activation(features(c), M[c % len(M)][:, :, :], ACT.Copy).then_inc(stored, 1)
            act.wait_ge(tail_done, 1)
            act.activation(carried[:, :], PC[:, :], ACT.Copy)

        @block.tensor
        def _(pe):
            pe.wait_ge(stored, chunks)
            pe.matmul(PC[:, :], e.carry[:, :], msg[:, T - 1, :], start=True, stop=True).then_inc(tail_done, 1)
    ph.end()


def sum_layer0(nc, w, e, name, xps, xpd, edge_attr, sm, carried0, carried1):
    R, T, H = e.R, e.T, w.H0
    CH = D // H
    ph = Phase(nc, name)
    M = [ph.sb(f"m{b}", [R, CH, T]) for b in range(2)]
    OWN = [ph.sb(f"own{b}", [R, CH, T]) for b in range(2)]
    GO_ON = ph.sb("go_on", [R, CH, T])
    TAIL = ph.sb("tail", [R, D])
    PC = ph.pb2("pc", [R, D])
    (ea_loaded, masked, weighted, summed, divided, tail_ready, tail_done, own_ready, sum_ready, ea_turned, ea_summed,
     ea_stored, tail1_done) = (ph.sem(n) for n in (
         "ea_loaded", "masked", "weighted", "summed", "divided", "tail_ready", "tail_done", "own_ready", "sum_ready",
         "ea_turned", "ea_summed", "ea_stored", "tail1_done"))

    def features(ap, c):
        return ap[:, :, c * CH:(c + 1) * CH].rearrange("p t d -> p d t")

    def over(weights, c):
        return weights[:, c, None, :].to_broadcast([R, CH, T])

    def flat(tile):
        return tile[:, :, :].rearrange("p d t -> p (d t)")

    with nc.Block() as block:
        @block.sync
        def _(sp):
            sp.wait_ge(own_ready, H)
            sp.dma_start(xpd, edge_attr.rearrange("(p t) d -> p t d", p=R)).then_inc(ea_loaded, 16)

        @block.gpsimd
        def _(pool):
            for c in range(H):
                past(pool, sum_ready, c - 1)
                pool.tensor_tensor(OWN[c % 2][:, :, :], features(xpd, c), over(sm.ws, c), ALU.mult)\
                    .then_inc(own_ready, 1)

        @block.scalar
        def _(act):
            for c in range(H):
                act.wait_ge(summed, c + 1)
                act.activation(TAIL[:, c * CH:(c + 1) * CH], M[c % 2][:, :, T - 1], ACT.Copy).then_inc(tail_ready, 1)
            act.wait_ge(tail_done, 1)
            act.activation(carried0[:, :], PC[0][:, :], ACT.Copy)
            act.wait_ge(ea_loaded, 16)
            for c in range(H + 1):
                if c < H:
                    act.wait_ge(sum_ready, H - 1 + c % 2)
                    past(act, ea_stored, c - 1)
                    act.activation(M[c % 2][:, :, :], features(xpd, c), ACT.Copy).then_inc(ea_turned, 1)
                if c:
                    act.wait_ge(ea_summed, c)
                    act.activation(features(xpd, c - 1), M[(c - 1) % 2][:, :, :], ACT.Copy).then_inc(ea_stored, 1)
            act.wait_ge(tail1_done, 1)
            act.activation(carried1[:, :], PC[1][:, :], ACT.Copy)

        @block.tensor
        def _(pe):
            pe.wait_ge(tail_ready, H)
            pe.matmul(PC[0][:, :], e.carry[:, :], TAIL[:, :], start=True, stop=True).then_inc(tail_done, 1)
            pe.wait_ge(ea_stored, H)
            pe.matmul(PC[1][:, :], e.carry[:, :], xpd[:, T - 1, :], start=True, stop=True).then_inc(tail1_done, 1)

        @block.vector
        def _(dve):
            dve.tensor_copy(GO_ON[:, :, :], e.cont[:, None, :].to_broadcast([R, CH, T])).then_inc(masked, 1)
            dve.wait_ge(masked, 1)
            dve.memset(GO_ON[:, :, 0:1], 0.0).then_inc(masked, 1)
            for c in range(H + 1):
                if c < H:
                    past(dve, sum_ready, c - 1)
                    dve.tensor_tensor(M[c % 2][:, :, :], features(xps, c), over(sm.w, c), ALU.mult)\
                        .then_inc(weighted, 1)
                if c:
                    m = M[(c - 1) % 2]
                    dve.wait_ge(tail_ready, c)
                    dve.tensor_tensor(m[:, :, :], m[:, :, :], over(sm.rd, c - 1), ALU.mult).then_inc(divided, 1)
                if c < H:
                    dve.wait_ge(weighted, c + 1)
                    dve.wait_ge(masked, 2)
                    m = flat(M[c % 2])
                    dve.tensor_tensor_scan(m, flat(GO_ON), m, 0.0, ALU.mult, ALU.add).then_inc(summed, 1)
                if c:
                    dve.wait_ge(divided, c)
                    dve.wait_ge(own_ready, c)
                    dve.tensor_tensor(features(xps, c - 1), M[(c - 1) % 2][:, :, :], OWN[(c - 1) % 2][:, :, :],
                                      ALU.add).then_inc(sum_ready, 1)
            for c in range(H):
                dve.wait_ge(ea_turned, c + 1)
                m = flat(M[c % 2])
                dve.tensor_tensor_scan(m, flat(GO_ON), m, 0.0, ALU.mult, ALU.add).then_inc(ea_summed, 1)
    ph.end()


def destination_moves(sp, units, dram, tile_in, loaded, load_after, tile_out=None, ready=None, kept=None, lag=0):
    def load(u, s, r):
        if load_after is not None:
            past(sp, load_after, u + 1 - NS)
        if tile_out is tile_in and tile_out is not None:
            past(sp, kept[s], 16 * r)
        sp.dma_start(tile_in[s][:, :, :], tiles(dram, u)).then_inc(loaded[s], 16)

    def keep(u, s, r):
        sp.wait_ge(ready, u + 1)
        sp.dma_start(tiles(dram, u), tile_out[s][:, :, :]).then_inc(kept[s], 16)

    run_slots(sp, None, units, [(load, -1)] + ([(keep, lag)] if ready is not None else []))
    if ready is not None:
        for s in range(NS):
            sp.wait_ge(kept[s], 16 * len(range(s, units, NS)))


def add_carried(dve, chain, out, run, carried, lead, lead_at, u):
    alone(dve)
    n = chain.add(dve.tensor_copy(lead_at[:, :], tiles(lead, u)))
    chain.upto(n)
    for j in range(TG):
        alone(dve)
        last = dve.scalar_tensor_tensor(out=out[:, j, :], in0=carried[:, :], scalar=lead_at[:, j:j + 1],
                                        in1=run[:, bass.ds(u * TG + j, 1), :].rearrange("p a n -> p (a n)"),
                                        op0=ALU.mult, op1=ALU.add)
    return last


def wait_streams(eng, sems, units, each):
    for s, sem in enumerate(sems):
        eng.wait_ge(sem, each * len(range(s, units, len(sems))))


def layers01(nc, w, e, name, out0, agg1, sm, carried0, carried1, table):
    R, units, H = e.R, e.units, w.H0
    ph = Phase(nc, name)
    X, Z0, X1, AG, HN = (ph.sbs(n, [R, TG, D]) for n in ("x", "z0", "x1", "ag", "h"))
    X2 = ph.sbs("x2", [R, TG, D])
    HT, AT = (ph.sbs(n, [P, TG, P]) for n in ("ht", "at"))
    IDX, LEAD = ph.sbs("idx", [R, TG], I32), ph.sbs("lead", [R, TG])
    ST, MV, VE, RS, NM = (ph.sbs(n, [R, TG] + d) for n, d in (
        ("st", [6]), ("mv", [2]), ("ve", []), ("rs", []), ("nm", [])))
    PH, PG = (ph.pbs(n, [P, TG, P]) for n in ("ph", "pg"))
    scattered, loaded, kept = ph.stream_sems("scattered"), ph.stream_sems("loaded"), ph.stream_sems("kept")
    pool_step, dve_step = ph.sem("pool_step"), ph.sem("dve_step")
    (z0a_ready, z0_ready, y0_ready, ag_ready, s0_ready, x1_ready, stats_ready, rstd_ready, shift_ready, h_ready,
     turned, ht_ready, mm1_done, z1_ready, mm1b_done, x2_ready) = (ph.sem(n) for n in (
         "z0a_ready", "z0_ready", "y0_ready", "ag_ready", "s0_ready", "x1_ready", "stats_ready",
         "rstd_ready", "shift_ready", "h_ready", "turned", "ht_ready", "mm1_done", "z1_ready", "mm1b_done",
         "x2_ready"))

    with nc.Block() as block:
        @block.sync
        def _(sp):
            destination_moves(sp, units, e.x, X, loaded, y0_ready, X2, x2_ready, kept, lag=4)

        @block.gpsimd
        def _(pool):
            chain = Chain(pool, pool_step)

            def rstd(u, s, r):
                pool.wait_ge(stats_ready, u + 1)
                layer_rstd(chain, MV[s], VE[s][:, :], RS[s][:, :], w.half[0:R, :]).then_inc(rstd_ready, 1)

            def scatter(u, s, r):
                past(pool, scattered[s], 16 * TG * r)
                n = place_indices(pool, chain, e.row, IDX[s], u)
                pool.wait_ge(x2_ready, u + 1)
                chain.upto(n)
                scatter_rows(pool, table, IDX[s], X2[s], scattered[s])

            run_slots(pool, chain, units, [(scatter, 4), (rstd, 1)])
            wait_streams(pool, scattered, units, 16 * TG)

        @block.scalar
        def _(act):
            def s0(u, s, r):
                act.wait_ge(z0_ready, u + 1)
                past(act, scattered[s], 16 * TG * r)
                past(act, kept[s], 16 * r)
                act.activation(X2[s][:, :, :], Z0[s][:, :, :], ACT.Silu).then_inc(s0_ready, 1)

            def norm(u, s, r):
                act.wait_ge(shift_ready, u + 1)
                past(act, turned, u + 1 - NS)
                norm_rows(act, HN[s], X1[s], RS[s], NM[s]).then_inc(h_ready, 1)

            def turn(u, s, r):
                act.wait_ge(turned, u + 1)
                act.activation(HT[s][:, :, 0:R], PH[s][:, :, 0:R], ACT.Copy)
                act.activation(AT[s][:, :, 0:R], PG[s][:, :, 0:R], ACT.Copy).then_inc(ht_ready, 1)

            def z1(u, s, r):
                act.wait_ge(mm1_done, u + 1)
                act.activation(HT[s][:, :, 0:R], PH[s][:, :, 0:R], ACT.Relu, bias=w.b1[:, 0:1]).then_inc(z1_ready, 1)

            run_slots(act, None, units, [(norm, 2), (turn, 2), (s0, 0), (z1, 2)])

        @block.tensor
        def _(pe):
            def turn(u, s, r):
                past(pe, x2_ready, u + 1 - NS)
                pe.wait_ge(ag_ready, u + 1)
                for j in range(TG):
                    pe.transpose(PG[s][:, j, 0:R], AG[s][:, j, :], w.ident[0:R, 0:R])
                pe.wait_ge(h_ready, u + 1)
                for j in range(TG):
                    last = pe.transpose(PH[s][:, j, 0:R], HN[s][:, j, :], w.ident[0:R, 0:R])
                last.then_inc(turned, 1)

            def mm1(u, s, r):
                pe.wait_ge(ht_ready, u + 1)
                pe.matmul(PH[s][:, :, 0:R], w.w1x[:, :], HT[s][:, :, 0:R], start=True, stop=False)
                pe.matmul(PH[s][:, :, 0:R], w.w1e[:, :], AT[s][:, :, 0:R], start=False, stop=True)\
                    .then_inc(mm1_done, 1)

            def mm1b(u, s, r):
                pe.wait_ge(z1_ready, u + 1)
                bias_rows(pe, w, R, PG[s][0:R, :, 0:D], 1)
                for j in range(TG):
                    last = pe.matmul(PG[s][0:R, j, 0:D], HT[s][:, j, 0:R], w.w1b[:, :], start=False, stop=j == TG - 1)
                last.then_inc(mm1b_done, 1)

            run_slots(pe, None, units, [(turn, 2), (mm1b, 3), (mm1, 2)])

        @block.vector
        def _(dve):
            chain = Chain(dve, dve_step)

            def carry(u, s, r):
                past(dve, turned, u + 1 - NS)
                add_carried(dve, chain, AG[s], agg1, carried1, e.lead, LEAD[s], u).then_inc(ag_ready, 1)
                past(dve, s0_ready, u + 1 - NS)
                alone(dve)
                dve.tensor_tensor(heads(Z0[s][:, :, :], H), heads(carried0[:, None, :].to_broadcast([R, TG, D]), H),
                                  per_head(sm.lrd, u, D // H), ALU.mult).then_inc(z0a_ready, 1)

            def z0(u, s, r):
                dve.wait_ge(z0a_ready, u + 1)
                alone(dve)
                n = chain.add(dve.tensor_tensor(Z0[s][:, :, :], tiles(out0, u), Z0[s][:, :, :], ALU.add))
                chain.upto(n)
                dve.tensor_tensor(Z0[s][:, :, :], Z0[s][:, :, :], w.b0[0:R, None, :].to_broadcast([R, TG, D]),
                                  ALU.add).then_inc(z0_ready, 1)

            def y0(u, s, r):
                dve.wait_ge(z0_ready, u + 1)
                dve.wait_ge(loaded[s], 16 * (r + 1))
                past(dve, h_ready, u + 1 - NS)
                dve.scalar_tensor_tensor(out=X1[s][:, :, :], in0=Z0[s][:, :, :], scalar=0.5, in1=X[s][:, :, :],
                                         op0=ALU.mult, op1=ALU.add).then_inc(y0_ready, 1)

            def x1(u, s, r):
                dve.wait_ge(s0_ready, u + 1)
                dve.wait_ge(y0_ready, u + 1)
                dve.scalar_tensor_tensor(out=X1[s][:, :, :], in0=X2[s][:, :, :], scalar=1.2 - 0.5,
                                         in1=X1[s][:, :, :], op0=ALU.mult, op1=ALU.add).then_inc(x1_ready, 1)

            def stats(u, s, r):
                dve.wait_ge(x1_ready, u + 1)
                layer_stats(chain, X1[s], ST[s], MV[s], TG).then_inc(stats_ready, 1)

            def shift(u, s, r):
                dve.wait_ge(rstd_ready, u + 1)
                layer_shift(dve, NM[s], MV[s], RS[s]).then_inc(shift_ready, 1)

            def x2(u, s, r):
                dve.wait_ge(mm1b_done, u + 1)
                dve.tensor_tensor(X2[s][:, :, :], PG[s][0:R, :, 0:D], X1[s][:, :, :], ALU.add).then_inc(x2_ready, 1)

            run_slots(dve, chain, units, [
                (carry, 0), (x1, 1), (z0, 0), (stats, 1), (y0, 0), (x2, 3), (shift, 1)])
    ph.end()


def gather_norm(nc, w, e, name, table, out, carried):
    R, units = e.R, e.units
    ph = Phase(nc, name)
    XG, H, RUN = (ph.sbs(n, [R, TG, D]) for n in ("xg", "h", "run"))
    IDX, CONT = ph.sbs("idx", [R, TG], I32), ph.sbs("cont", [R, TG])
    ST, MV, VE, RS, NM = (ph.sbs(n, [R, TG] + d) for n, d in (
        ("st", [6]), ("mv", [2]), ("ve", []), ("rs", []), ("nm", [])))
    PC = ph.ctx.enter_context(nc.psum_tensor(f"{name}_pc", [R, D], F32))
    gathered = ph.stream_sems("gathered")
    pool_step, dve_step, stats_ready, rstd_ready, shift_ready, h_ready, run_ready, stored, tail_done = (
        ph.sem(n) for n in ("pool_step", "dve_step", "stats_ready", "rstd_ready", "shift_ready", "h_ready",
                            "run_ready", "stored", "tail_done"))
    with nc.Block() as block:
        @block.gpsimd
        def _(pool):
            chain = Chain(pool, pool_step)

            def gather(u, s, r):
                n = place_indices(pool, chain, e.src, IDX[s], u)
                past(pool, h_ready, u + 1 - NS)
                chain.upto(n)
                gather_rows(pool, table, IDX[s], XG[s], gathered[s])

            def rstd(u, s, r):
                pool.wait_ge(stats_ready, u + 1)
                layer_rstd(chain, MV[s], VE[s][:, :], RS[s][:, :], w.half[0:R, :]).then_inc(rstd_ready, 1)

            run_slots(pool, chain, units, [(gather, 0), (rstd, 2)])

        @block.scalar
        def _(act):
            def norm(u, s, r):
                act.wait_ge(shift_ready, u + 1)
                past(act, run_ready, u + 1 - NS)
                norm_rows(act, H[s], XG[s], RS[s], NM[s]).then_inc(h_ready, 1)

            def store(u, s, r):
                act.wait_ge(run_ready, u + 1)
                alone(act)
                act.activation(tiles(out, u), RUN[s][:, :, :], ACT.Copy).then_inc(stored, 1)

            run_slots(act, None, units, [(norm, 3), (store, 4)])
            act.wait_ge(tail_done, 1)
            act.activation(carried[:, :], PC[:, :], ACT.Copy)

        @block.tensor
        def _(pe):
            pe.wait_ge(run_ready, units)
            pe.matmul(PC[:, :], e.carry[:, :], RUN[(units - 1) % NS][:, TG - 1, :], start=True, stop=True)\
                .then_inc(tail_done, 1)

        @block.vector
        def _(dve):
            chain = Chain(dve, dve_step)
            chain.upto(chain.add(dve.memset(RUN[NS - 1][:, TG - 1, :], 0.0)))

            def stats(u, s, r):
                dve.wait_ge(gathered[s], 16 * TG * (r + 1))
                alone(dve)
                layer_stats(chain, XG[s], ST[s], MV[s], TG).then_inc(stats_ready, 1)

            def shift(u, s, r):
                dve.wait_ge(rstd_ready, u + 1)
                layer_shift(dve, NM[s], MV[s], RS[s]).then_inc(shift_ready, 1)

            def run(u, s, r):
                alone(dve)
                n = chain.add(dve.tensor_copy(CONT[s][:, :], tiles(e.cont, u)))
                dve.wait_ge(h_ready, u + 1)
                past(dve, stored, u + 1 - NS)
                past(dve, run_ready, u)
                for j in range(TG):
                    chain.upto(n)
                    before = RUN[s][:, j - 1, :] if j else RUN[(s - 1) % NS][:, TG - 1, :]
                    ins = dve.scalar_tensor_tensor(out=RUN[s][:, j, :], in0=before, scalar=CONT[s][:, j:j + 1],
                                                   in1=H[s][:, j, :], op0=ALU.mult, op1=ALU.add)
                    if j < TG - 1:
                        n = chain.add(ins)
                ins.then_inc(run_ready, 1)

            run_slots(dve, chain, units, [(shift, 3), (stats, 1), (run, 4)])
    ph.end()


def layer2(nc, w, e, name, run, carried, table):
    R, units = e.R, e.units
    ph = Phase(nc, name)
    X, HN, T, X3 = (ph.sbs(n, [R, TG, D]) for n in ("x", "h", "t", "x3"))
    HT = ph.sbs("ht", [P, TG, P])
    IDX, LEAD = ph.sbs("idx", [R, TG], I32), ph.sbs("lead", [R, TG])
    ST, MV, VE, RS, NM = (ph.sbs(n, [R, TG] + d) for n, d in (
        ("st", [6]), ("mv", [2]), ("ve", []), ("rs", []), ("nm", [])))
    PT, PB = (ph.pbs(n, [P, TG, P]) for n in ("pt", "pb"))
    scattered, loaded, kept = ph.stream_sems("scattered"), ph.stream_sems("loaded"), ph.stream_sems("kept")
    (pool_step, dve_step, carried_in, sum_ready, t_ready, z2_ready, l_ready, x3_ready, stats_ready,
     rstd_ready, shift_ready, h_ready, turned, ht_ready, mm_done) = (ph.sem(n) for n in (
         "pool_step", "dve_step", "carried_in", "sum_ready", "t_ready", "z2_ready", "l_ready", "x3_ready",
         "stats_ready", "rstd_ready", "shift_ready", "h_ready", "turned", "ht_ready", "mm_done"))
    with nc.Block() as block:
        @block.sync
        def _(sp):
            destination_moves(sp, units, e.x, X, loaded, x3_ready, X3, x3_ready, kept, lag=3)

        @block.gpsimd
        def _(pool):
            chain = Chain(pool, pool_step)

            def rstd(u, s, r):
                pool.wait_ge(stats_ready, u + 1)
                layer_rstd(chain, MV[s], VE[s][:, :], RS[s][:, :], w.half[0:R, :]).then_inc(rstd_ready, 1)

            def scatter(u, s, r):
                past(pool, scattered[s], 16 * TG * r)
                n = place_indices(pool, chain, e.row, IDX[s], u)
                pool.wait_ge(x3_ready, u + 1)
                chain.upto(n)
                scatter_rows(pool, table, IDX[s], X3[s], scattered[s])

            run_slots(pool, chain, units, [(rstd, 0), (scatter, 3)])
            wait_streams(pool, scattered, units, 16 * TG)

        @block.scalar
        def _(act):
            def norm(u, s, r):
                act.wait_ge(shift_ready, u + 1)
                past(act, t_ready, u + 1 - NS)
                norm_rows(act, HN[s], X[s], RS[s], NM[s]).then_inc(h_ready, 1)

            def turn(u, s, r):
                act.wait_ge(turned, u + 1)
                act.activation(HT[s][:, :, 0:R], PT[s][:, :, 0:R], ACT.Copy).then_inc(ht_ready, 1)

            def z2(u, s, r):
                act.wait_ge(mm_done, u + 1)
                past(act, scattered[s], 16 * TG * r)
                past(act, kept[s], 16 * r)
                act.activation(X3[s][:, :, :], PB[s][0:R, :, 0:D], ACT.Copy).then_inc(z2_ready, 1)

            run_slots(act, None, units, [(z2, 2), (turn, 1), (norm, 0)])

        @block.tensor
        def _(pe):
            def turn(u, s, r):
                pe.wait_ge(t_ready, u + 1)
                past(pe, ht_ready, u + 1 - NS)
                for j in range(TG):
                    last = pe.transpose(PT[s][:, j, 0:R], T[s][:, j, :], w.ident[0:R, 0:R])
                last.then_inc(turned, 1)

            def mm(u, s, r):
                pe.wait_ge(ht_ready, u + 1)
                past(pe, z2_ready, u + 1 - NS)
                bias_rows(pe, w, R, PB[s][0:R, :, 0:D], 2)
                for j in range(TG):
                    last = pe.matmul(PB[s][0:R, j, 0:D], HT[s][:, j, 0:R], w.w2[:, :], start=False, stop=j == TG - 1)
                last.then_inc(mm_done, 1)

            run_slots(pe, None, units, [(turn, 1), (mm, 1)])

        @block.vector
        def _(dve):
            chain = Chain(dve, dve_step)

            def stats(u, s, r):
                dve.wait_ge(loaded[s], 16 * (r + 1))
                layer_stats(chain, X[s], ST[s], MV[s], TG).then_inc(stats_ready, 1)

            def carry(u, s, r):
                past(dve, turned, u + 1 - NS)
                add_carried(dve, chain, T[s], run, carried, e.lead, LEAD[s], u).then_inc(carried_in, 1)

            def shift(u, s, r):
                dve.wait_ge(rstd_ready, u + 1)
                layer_shift(dve, NM[s], MV[s], RS[s]).then_inc(shift_ready, 1)

            def mean(u, s, r):
                dve.wait_ge(h_ready, u + 1)
                dve.wait_ge(carried_in, u + 1)
                dve.tensor_tensor(T[s][:, :, :], HN[s][:, :, :], T[s][:, :, :], ALU.add).then_inc(sum_ready, 1)
                dve.wait_ge(sum_ready, u + 1)
                alone(dve)
                dve.tensor_tensor(T[s][:, :, :], T[s][:, :, :],
                                  tiles(e.rcount, u)[:, :, None].to_broadcast([R, TG, D]), ALU.mult)\
                    .then_inc(t_ready, 1)

            def leaky(u, s, r):
                dve.wait_ge(z2_ready, u + 1)
                leaky_relu(dve, X3[s][:, :, :], X3[s][:, :, :]).then_inc(l_ready, 1)

            def x3(u, s, r):
                dve.wait_ge(l_ready, u + 1)
                dve.tensor_tensor(X3[s][:, :, :], X[s][:, :, :], X3[s][:, :, :], ALU.add).then_inc(x3_ready, 1)

            run_slots(dve, chain, units, [(stats, 0), (mean, 1), (leaky, 2), (x3, 2), (carry, 0), (shift, 0)])
    ph.end()


def layer3_first(nc, w, e, name, run, own, sm, carried, table):
    R, units, H, C3 = e.R, e.units, w.H3, w.C3
    W3 = C3 * P
    ph = Phase(nc, name)
    X, HN = (ph.sbs(n, [R, TG, D]) for n in ("x", "h"))
    V, SELF = (ph.sbs(n, [R, TG, W3]) for n in ("v", "self"))
    G = ph.sbs("g", [R, TG, D + 2])
    VT = ph.sbs("vt", [P, C3, TG, P])
    HT = [vt[:, 0] for vt in VT]
    IDX, LEAD = ph.sbs("idx", [R, TG], I32), ph.sbs("lead", [R, TG])
    ST, MV, VE, RS, NM = (ph.sbs(n, [R, TG] + d) for n, d in (
        ("st", [6]), ("mv", [2]), ("ve", []), ("rs", []), ("nm", [])))
    PA = ph.pbs("pa", [P, TG, W3])
    scattered, loaded, kept = ph.stream_sems("scattered"), ph.stream_sems("loaded"), ph.stream_sems("kept")
    (pool_step, dve_step, xh_ready, stats_ready, rstd_ready, shift_ready, h_ready, turned, ht_ready, mm_done,
     self_ready, v_carried, v_ready, v_turned, vt_ready, c_ready, mm4_done, g_ready, g_kept) = (ph.sem(n) for n in (
         "pool_step", "dve_step", "xh_ready", "stats_ready", "rstd_ready", "shift_ready", "h_ready", "turned",
         "ht_ready", "mm_done", "self_ready", "v_carried", "v_ready", "v_turned", "vt_ready", "c_ready",
         "mm4_done", "g_ready", "g_kept"))

    def halves(pa):
        return pa[:, :, :].rearrange("p t n -> p (t n)").rearrange("p (c t n) -> p c t n", c=C3, t=TG)

    with nc.Block() as block:
        @block.sync
        def _(sp):
            destination_moves(sp, units, e.x, X, loaded, None, X, xh_ready, kept, lag=1)

        @block.gpsimd
        def _(pool):
            chain = Chain(pool, pool_step)

            def rstd(u, s, r):
                pool.wait_ge(stats_ready, u + 1)
                layer_rstd(chain, MV[s], VE[s][:, :], RS[s][:, :], w.half[0:R, :]).then_inc(rstd_ready, 1)

            def xh(u, s, r):
                pool.wait_ge(h_ready, u + 1)
                pool.tensor_tensor(X[s][:, :, :], HN[s][:, :, :], X[s][:, :, :], ALU.add).then_inc(xh_ready, 1)

            def scatter(u, s, r):
                past(pool, scattered[s], 16 * TG * r)
                n = place_indices(pool, chain, e.row, IDX[s], u)
                pool.wait_ge(g_ready, u + 1)
                chain.upto(n)
                scatter_rows(pool, table, IDX[s], G[s], scattered[s])

            run_slots(pool, chain, units, [(rstd, 0), (xh, 1), (scatter, 4)])
            wait_streams(pool, scattered, units, 16 * TG)

        @block.scalar
        def _(act):
            def norm(u, s, r):
                act.wait_ge(shift_ready, u + 1)
                past(act, turned, u + 1 - NS)
                past(act, xh_ready, u + 1 - NS)
                norm_rows(act, HN[s], X[s], RS[s], NM[s]).then_inc(h_ready, 1)

            def turn(u, s, r):
                act.wait_ge(turned, u + 1)
                act.activation(HT[s][:, :, 0:R], halves(PA[s])[:, 0, :, 0:R], ACT.Copy).then_inc(ht_ready, 1)

            def turn_v(u, s, r):
                act.wait_ge(v_turned, u + 1)
                for c in range(C3):
                    last = act.activation(VT[s][:, c, :, 0:R], halves(PA[s])[:, c, :, 0:R], ACT.Identity,
                                          bias=w.b3[:, c:c + 1])
                last.then_inc(vt_ready, 1)

            def g(u, s, r):
                act.wait_ge(mm4_done, u + 1)
                past(act, scattered[s], 16 * TG * r)
                act.activation(G[s][:, :, :], PA[s][0:R, :, 0:D + 2], ACT.Copy).then_inc(g_ready, 1)
                act.wait_ge(g_ready, u + 1)
                alone(act)
                act.activation(tiles(own, u), G[s][:, :, :], ACT.Copy).then_inc(g_kept, 1)

            run_slots(act, None, units, [(turn, 1), (turn_v, 3), (g, 4), (norm, 0)])

        @block.tensor
        def _(pe):
            def turn(u, s, r):
                pe.wait_ge(h_ready, u + 1)
                past(pe, g_ready, u + 1 - NS)
                for j in range(TG):
                    last = pe.transpose(halves(PA[s])[:, 0, j, 0:R], HN[s][:, j, :], w.ident[0:R, 0:R])
                last.then_inc(turned, 1)

            def mm3(u, s, r):
                pe.wait_ge(ht_ready, u + 1)
                for j in range(TG):
                    last = pe.matmul(PA[s][0:R, j, :], HT[s][:, j, 0:R], w.w3[:, 0:W3], start=True, stop=True)
                last.then_inc(mm_done, 1)

            def turn_v(u, s, r):
                pe.wait_ge(v_ready, u + 1)
                pe.wait_ge(self_ready, u + 1)
                for c in range(C3):
                    for j in range(TG):
                        cols = slice(c * P, (c + 1) * P)
                        pe.matmul(halves(PA[s])[:, c, j, 0:R], V[s][:, j, cols], w.ident[0:R, 0:R],
                                  start=True, stop=False)
                        last = pe.matmul(halves(PA[s])[:, c, j, 0:R], SELF[s][:, j, cols], w.ident[0:R, 0:R],
                                         start=False, stop=True)
                last.then_inc(v_turned, 1)

            def mm4(u, s, r):
                pe.wait_ge(c_ready, u + 1)
                for j in range(TG):
                    for c in range(C3):
                        last = pe.matmul(PA[s][0:R, j, 0:D + 2], VT[s][:, c, j, 0:R], w.w4[:, c, :],
                                         start=(c == 0), stop=(c == C3 - 1))
                last.then_inc(mm4_done, 1)

            run_slots(pe, None, units, [(turn, 1), (mm4, 4), (mm3, 1), (turn_v, 2)])

        @block.vector
        def _(dve):
            chain = Chain(dve, dve_step)

            def stats(u, s, r):
                dve.wait_ge(loaded[s], 16 * (r + 1))
                layer_stats(chain, X[s], ST[s], MV[s], TG).then_inc(stats_ready, 1)

            def shift(u, s, r):
                dve.wait_ge(rstd_ready, u + 1)
                layer_shift(dve, NM[s], MV[s], RS[s]).then_inc(shift_ready, 1)

            def edge_part(u, s, r):
                past(dve, v_turned, u + 1 - NS)
                add_carried(dve, chain, V[s], run, carried, e.lead, LEAD[s], u).then_inc(v_carried, 1)
                dve.wait_ge(v_carried, u + 1)
                alone(dve)
                dve.tensor_tensor(heads(V[s][:, :, :], H), heads(V[s][:, :, :], H),
                                  per_head(sm.rd, u, W3 // H), ALU.mult).then_inc(v_ready, 1)

            def own_part(u, s, r):
                dve.wait_ge(mm_done, u + 1)
                alone(dve)
                dve.tensor_tensor(heads(SELF[s][:, :, :], H), heads(PA[s][0:R, :, :], H),
                                  per_head(sm.ws, u, W3 // H), ALU.mult).then_inc(self_ready, 1)

            def leaky(u, s, r):
                dve.wait_ge(vt_ready, u + 1)
                leaky_relu(dve, VT[s][:, :, :, 0:R].rearrange("p c t n -> p (c t) n"),
                           VT[s][:, :, :, 0:R].rearrange("p c t n -> p (c t) n")).then_inc(c_ready, 1)

            run_slots(dve, chain, units, [(stats, 0), (edge_part, 0), (shift, 0), (own_part, 1), (leaky, 3)])
    ph.end()


def gather_last(nc, w, e, name, table, out):
    R, units = e.R, e.units
    ph = Phase(nc, name)
    XG = ph.sbs("xg", [R, TG, D + 2])
    IDX = ph.sbs("idx", [R, TG], I32)
    gathered = ph.stream_sems("gathered")
    pool_step, stored = ph.sem("pool_step"), ph.sem("stored")
    with nc.Block() as block:
        @block.gpsimd
        def _(pool):
            chain = Chain(pool, pool_step)

            def gather(u, s, r):
                past(pool, stored, u + 1 - NS)
                n = place_indices(pool, chain, e.src, IDX[s], u)
                chain.upto(n)
                gather_rows(pool, table, IDX[s], XG[s], gathered[s])

            run_slots(pool, chain, units, [(gather, 0)])

        @block.scalar
        def _(act):
            def store(u, s, r):
                act.wait_ge(gathered[s], 16 * TG * (r + 1))
                alone(act)
                act.activation(tiles(out, u), XG[s][:, :, :], ACT.Copy).then_inc(stored, 1)

            run_slots(act, None, units, [(store, 0)])
    ph.end()


def layer3_second(nc, w, e, name, run, own, sm, carried, out_dram):
    R, units = e.R, e.units
    ph = Phase(nc, name)
    X, V, SELF, Y, OUT = (ph.sbs(n, [R, TG, D]) for n in ("x", "v", "self", "y", "out"))
    RD = ph.sbs("rd", [R, TG])
    IDX, LEAD = ph.sbs("idx", [R, TG], I32), ph.sbs("lead", [R, TG])
    scattered, loaded = ph.stream_sems("scattered"), ph.stream_sems("loaded")
    pool_step, dve_step, rd_ready, carried_in, v_ready, self_ready, y_ready, l_ready, out_ready = (
        ph.sem(n) for n in ("pool_step", "dve_step", "rd_ready", "carried_in", "v_ready", "self_ready", "y_ready", "l_ready",
                            "out_ready"))
    with nc.Block() as block:
        @block.sync
        def _(sp):
            destination_moves(sp, units, e.x, X, loaded, out_ready)

        @block.gpsimd
        def _(pool):
            chain = Chain(pool, pool_step)

            def scatter(u, s, r):
                past(pool, scattered[s], 16 * TG * r)
                n = place_indices(pool, chain, e.row, IDX[s], u)
                pool.wait_ge(out_ready, u + 1)
                chain.upto(n)
                scatter_rows(pool, out_dram, IDX[s], OUT[s], scattered[s])

            run_slots(pool, chain, units, [(scatter, 3)])
            wait_streams(pool, scattered, units, 16 * TG)

        @block.scalar
        def _(act):
            def edge_part(u, s, r):
                alone(act)
                act.activation(RD[s][:, :], sm.rd[:, 0, bass.ds(u * TG, TG)], ACT.Copy).then_inc(rd_ready, 1)
                act.wait_ge(rd_ready, u + 1)
                act.wait_ge(carried_in, u + 1)
                for j in range(TG):
                    last = act.activation(V[s][:, j, :], V[s][:, j, :], ACT.Copy, scale=RD[s][:, j:j + 1])
                last.then_inc(v_ready, 1)

            run_slots(act, None, units, [(edge_part, 0)])

        @block.vector
        def _(dve):
            chain = Chain(dve, dve_step)

            def edge_part(u, s, r):
                add_carried(dve, chain, V[s], run, carried, e.lead, LEAD[s], u).then_inc(carried_in, 1)

            def own_part(u, s, r):
                alone(dve)
                dve.tensor_tensor(SELF[s][:, :, :], tiles(own, u)[:, :, 0:D],
                                  per_head(sm.ws, u, D)[:, :, 0, :], ALU.mult).then_inc(self_ready, 1)

            def both(u, s, r):
                dve.wait_ge(v_ready, u + 1)
                dve.wait_ge(self_ready, u + 1)
                n = chain.add(dve.tensor_tensor(Y[s][:, :, :], V[s][:, :, :], SELF[s][:, :, :], ALU.add))
                chain.upto(n)
                dve.tensor_tensor(Y[s][:, :, :], Y[s][:, :, :], w.b4[0:R, None, :].to_broadcast([R, TG, D]),
                                  ALU.add).then_inc(y_ready, 1)

            def leaky(u, s, r):
                dve.wait_ge(y_ready, u + 1)
                leaky_relu(dve, V[s][:, :, :], Y[s][:, :, :]).then_inc(l_ready, 1)

            def final(u, s, r):
                dve.wait_ge(l_ready, u + 1)
                dve.wait_ge(loaded[s], 16 * (r + 1))
                past(dve, scattered[s], 16 * TG * r)
                dve.tensor_tensor(OUT[s][:, :, :], X[s][:, :, :], V[s][:, :, :], ALU.add).then_inc(out_ready, 1)

            run_slots(dve, chain, units, [(edge_part, 0), (leaky, 2), (own_part, 0), (final, 2), (both, 1)])
    ph.end()


class FirstHeads:

    def __init__(self, sm, heads):
        self.w, self.ws, self.rd, self.lrd = (t[:, 0:heads, :] for t in (sm.w, sm.ws, sm.rd, sm.lrd))


class Weights:

    def __init__(self, nc, ctx, name, e, H):
        self.w, self.ws, self.rd, self.lrd = (
            ctx.enter_context(nc.sbuf_tensor(f"{name}_{n}", [e.R, H, e.T], F32)) for n in ("w", "ws", "rd", "lrd"))


def sparse_pass(nc, ctx, w, a, tables, out_dram):
    t2, t3, t4 = tables
    e = load_edges(nc, ctx, w, a)
    R, T = e.R, e.T
    e.x = nc.dram_tensor("dst_rows", (R, T, D), F32).ap()
    H0, H3, W3 = w.H0, w.H3, w.C3 * P
    ns = D + H0
    big = ctx.enter_context(nc.sbuf_tensor("big", [R, T, max(ns + D + 2 * H0, W3 + H3, 2 * (D + 2))], F32))
    al = ctx.enter_context(nc.sbuf_tensor("al", [R, T, 2 * H3], F32))
    c0 = ctx.enter_context(nc.sbuf_tensor("c0", [R, D], F32))
    c1 = ctx.enter_context(nc.sbuf_tensor("c1", [R, D], F32))
    c3 = ctx.enter_context(nc.sbuf_tensor("c3", [R, W3], F32))
    sm = Weights(nc, ctx, "sm", e, max(H0, H3))
    sm1 = FirstHeads(sm, 1)

    src0, dst0 = big[:, :, 0:ns], big[:, :, ns:ns + D + 2 * H0]
    project_ends(nc, w, e, "p0", a["x"], True, (w.w0[:, 0:ns], w.w0[:, :]), (src0, dst0), 2)
    edge_softmax(nc, w, e, "q0", H0, src0[:, :, D:D + H0], dst0[:, :, D:D + H0], dst0[:, :, D + H0:D + 2 * H0],
                 1e-16, sm, False)
    sum_layer0(nc, w, e, "s0", src0[:, :, 0:D], dst0[:, :, 0:D], a["edge_attr_128"], sm, c0, c1)
    layers01(nc, w, e, "l01", src0[:, :, 0:D], dst0[:, :, 0:D], sm, c0, c1, t2)
    gather_norm(nc, w, e, "g2", t2, big[:, :, 0:D], c0)
    layer2(nc, w, e, "l2", big[:, :, 0:D], c0, t3)
    src3 = big[:, :, 0:W3 + H3]
    project_ends(nc, w, e, "p3", t3, False, (w.w3[:, 0:W3 + H3], w.w3[:, W3:W3 + 2 * H3]),
                 (src3, al[:, :, :]), 3)
    edge_softmax(nc, w, e, "q3", H3, src3[:, :, W3:W3 + H3], al[:, :, 0:H3], al[:, :, H3:2 * H3], 0.0, sm, True)
    sum_runs(nc, w, e, "s3", src3[:, :, 0:W3], H3, sm, c3)
    own = big[:, :, 0:D + 2]
    layer3_first(nc, w, e, "l3", src3[:, :, 0:W3], own, sm, c3, t4)
    src4 = big[:, :, D + 2:2 * (D + 2)]
    gather_last(nc, w, e, "g4", t4, src4)
    edge_softmax(nc, w, e, "q4", 1, src4[:, :, D:D + 1], own[:, :, D:D + 1], own[:, :, D + 1:D + 2], 0.0, sm1, True)
    sum_runs(nc, w, e, "s4", src4[:, :, 0:D], 1, sm1, c0)
    layer3_second(nc, w, e, "l4", src4[:, :, 0:D], own, sm1, c0, out_dram)


def gnn_kernel(nc, a, out):
    N = a["x"].shape[0]
    with ExitStack() as ctx:
        t2 = nc.dram_tensor("t2", (N, D), F32).ap()
        t3 = nc.dram_tensor("t3", (N, D), F32).ap()
        t4 = nc.dram_tensor("t4", (N, D + 2), F32).ap()
        w = load_weights(nc, ctx, a)
        dense_pass(nc, w, a["x"], (t2, t3, t4), out)
        sparse_pass(nc, ctx, w, a, (t2, t3, t4), out)


_INS = ['x', 'src', 'dst', 'edge_attr_128', 'L0_gnn_W', 'L0_gnn_att_src', 'L0_gnn_att_dst', 'L0_gnn_bias',
        'L1_gnn_W1', 'L1_gnn_b1', 'L1_gnn_W2', 'L1_gnn_b2', 'L2_gnn_W', 'L2_gnn_b', 'L3_gnn_W1',
        'L3_gnn_att_src1', 'L3_gnn_att_dst1', 'L3_gnn_bias1', 'L3_gnn_W2', 'L3_gnn_att_src2',
        'L3_gnn_att_dst2', 'L3_gnn_bias2']


def kernel(**inputs):
    import numpy as _np
    import concourse.bacc as _bacc
    from concourse import mybir as _mybir
    from concourse.bass_utils import run_bass_kernel_spmd as _run

    nc = _bacc.Bacc("TRN2", target_bir_lowering=False, num_devices=1)
    arrays, args = {}, {}
    for name in _INS:
        a = _np.ascontiguousarray(inputs[name])
        arrays[f"in_{name}_dram"] = a
        args[name] = nc.dram_tensor(f"in_{name}_dram", a.shape, _mybir.dt.from_np(a.dtype), kind="ExternalInput").ap()
    out = nc.dram_tensor("out_0_dram", inputs["x"].shape, _mybir.dt.float32, kind="ExternalOutput").ap()
    gnn_kernel(nc, args, out)
    r = _run(nc, [arrays], core_ids=[0])
    return r.results[0]["out_0_dram"]
```
